# Optimizing a Trainium2 kernel written in Bass

```python
import numpy as np
import jax
import jax.numpy as jnp

def _softmax(x, axis=-1):
    return jax.nn.softmax(x, axis=axis)

def _gelu(x):
    return jax.nn.gelu(x, approximate=True)

def _silu(x):
    return jax.nn.silu(x)

def _sigmoid(x):
    return jax.nn.sigmoid(x)

def _layernorm(x, axis=-1, eps=1e-05):
    m = jnp.mean(x, axis=axis, keepdims=True)
    v = jnp.var(x, axis=axis, keepdims=True)
    return (x - m) / jnp.sqrt(v + eps)

def _scatter_add(tgt, idx, src, axis=0):
    return tgt.at[idx].add(src)

def _segment_sum(src, seg, n):
    return jax.ops.segment_sum(src, seg, n)
kernel_name = 'mk_prb_d1_jaxref_r8_bf357b'

def setup_inputs(seed: int=0):
    np.random.seed(seed)
    _w = jnp.asarray

    def _L0_attn_setup():
        import jax, jax.numpy as jnp
        import numpy as np
        D_MODEL = 128
        N_HEAD = 16
        D_HEAD = D_MODEL // N_HEAD
        N_CTX = 256
        ROPE_BASE = 10000.0
        SCALE = 1

        def _rope_cache(seq_len, d_head, dtype=jnp.float32):
            inv_freq = 1.0 / ROPE_BASE ** (jnp.arange(0, d_head, 2, dtype=jnp.float32) / d_head)
            t = jnp.arange(seq_len, dtype=jnp.float32)
            freqs = jnp.outer(t, inv_freq)
            emb = jnp.concatenate([freqs, freqs], -1)
            cos = jnp.cos(emb)[None, :, None, :].astype(dtype)
            sin = jnp.sin(emb)[None, :, None, :].astype(dtype)
            return (cos, sin)

        def _apply_rope(x, cos, sin):
            x_even = x[..., 0::2]
            x_odd = x[..., 1::2]
            x_rot = jnp.stack([-x_odd, x_even], axis=-1).reshape(x.shape)
            return x * cos + x_rot * sin

        def _rmsnorm(x, w):
            eps = jnp.finfo(x.dtype).eps
            var = jnp.mean(jnp.square(x), axis=-1, keepdims=True)
            return x * jax.lax.rsqrt(var + eps) * w
        key = jax.random.key(seed)
        ks = jax.random.split(key, 9)
        B, S = (2, N_CTX)
        x = jax.random.normal(ks[0], (B, S, D_MODEL), jnp.float32)
        s = 0.02
        Wq = jax.random.normal(ks[1], (D_MODEL, D_MODEL), jnp.float32) * s
        bq = jax.random.normal(ks[2], (D_MODEL,), jnp.float32) * s
        Wk = jax.random.normal(ks[3], (D_MODEL, D_MODEL), jnp.float32) * s
        bk = jax.random.normal(ks[4], (D_MODEL,), jnp.float32) * s
        Wv = jax.random.normal(ks[5], (D_MODEL, D_MODEL), jnp.float32) * s
        bv = jax.random.normal(ks[6], (D_MODEL,), jnp.float32) * s
        Wo = jax.random.normal(ks[7], (D_MODEL, D_MODEL), jnp.float32) * s
        norm_w = jnp.ones((D_HEAD,), jnp.float32)
        return {'x': x, 'Wq': Wq, 'bq': bq, 'Wk': Wk, 'bk': bk, 'Wv': Wv, 'bv': bv, 'Wo': Wo, 'norm_w': norm_w}
    _L0_attn_in = _L0_attn_setup()

    def _L0_ffn_setup():
        import jax, jax.numpy as jnp
        import numpy as np
        D = 128
        H = 4
        HD = D // H
        E = 8
        FF = 512
        CAP_FACTOR = 1.0

        def _ln(x, g, b, eps=1e-05):
            mu = jnp.mean(x, -1, keepdims=True)
            v = jnp.mean((x - mu) ** 2, -1, keepdims=True)
            return (x - mu) * jax.lax.rsqrt(v + eps) * g + b

        def _mha(x, w, b, ow, ob):
            L, N, _ = x.shape
            qkv = x @ w.T + b
            q, k, v = jnp.split(qkv, 3, axis=-1)
            rh = lambda t: t.reshape(L, N, H, HD).transpose(1, 2, 0, 3)
            q, k, v = (rh(q), rh(k), rh(v))
            scores = jnp.einsum('nhld,nhmd->nhlm', q, k) / np.float32(np.sqrt(HD))
            attn = jax.nn.softmax(scores, axis=-1)
            o = jnp.einsum('nhlm,nhmd->nhld', attn, v).transpose(2, 0, 1, 3).reshape(L, N, D)
            return o @ ow.T + ob

        def _moe(x, wg, w1, b1, w2, b2):
            L, N, _ = x.shape
            S = L * N
            cap = int(CAP_FACTOR * S) // E
            xf = x.reshape(S, D)
            gates = jax.nn.softmax(xf @ wg, axis=-1)
            idx = jnp.argmax(gates, axis=-1)
            mask1 = jax.nn.one_hot(idx, E, dtype=x.dtype)
            loc = jnp.sum((jnp.cumsum(mask1, 0) - 1.0) * mask1, -1).astype(jnp.int32)
            keep = loc < cap
            gate_val = jnp.take_along_axis(gates, idx[:, None], -1)[:, 0]
            slot = jnp.where(keep, idx.astype(jnp.int32) * cap + loc, E * cap)
            disp = jnp.zeros((E * cap, D), x.dtype).at[slot].set(xf, mode='drop')
            disp = disp.reshape(E, cap, D)
            h = jnp.einsum('ecd,edf->ecf', disp, w1) + b1[:, None, :]
            y = (jnp.einsum('ecf,efd->ecd', h, w2) + b2[:, None, :]).reshape(E * cap, D)
            out = jnp.where(keep[:, None], gate_val[:, None] * y[jnp.minimum(slot, E * cap - 1)], 0.0)
            return out.reshape(L, N, D)
        key = jax.random.key(seed)
        ks = jax.random.split(key, 8)
        L, N = (128, 16)
        s = 0.02
        return {'x': jax.random.normal(ks[0], (L, N, D), jnp.float32), 'in_proj_w': jax.random.normal(ks[1], (3 * D, D), jnp.float32) * s, 'in_proj_b': jnp.zeros((3 * D,), jnp.float32), 'out_proj_w': jax.random.normal(ks[2], (D, D), jnp.float32) * s, 'out_proj_b': jnp.zeros((D,), jnp.float32), 'ln1_g': jnp.ones((D,), jnp.float32), 'ln1_b': jnp.zeros((D,), jnp.float32), 'ln2_g': jnp.ones((D,), jnp.float32), 'ln2_b': jnp.zeros((D,), jnp.float32), 'wg': jax.random.normal(ks[3], (D, E), jnp.float32) * s, 'w1': jax.random.normal(ks[4], (E, D, FF), jnp.float32) * s, 'b1': jnp.zeros((E, FF), jnp.float32), 'w2': jax.random.normal(ks[5], (E, FF, D), jnp.float32) * s, 'b2': jnp.zeros((E, D), jnp.float32)}
    _L0_ffn_in = _L0_ffn_setup()
    _d = {'L0_attn_x': _L0_attn_in['x'], 'L0_attn_Wq': _L0_attn_in['Wq'], 'L0_attn_bq': _L0_attn_in['bq'], 'L0_attn_Wk': _L0_attn_in['Wk'], 'L0_attn_bk': _L0_attn_in['bk'], 'L0_attn_Wv': _L0_attn_in['Wv'], 'L0_attn_bv': _L0_attn_in['bv'], 'L0_attn_Wo': _L0_attn_in['Wo'], 'L0_attn_norm_w': _L0_attn_in['norm_w'], 'L0_ffn_in_proj_w': _L0_ffn_in['in_proj_w'], 'L0_ffn_in_proj_b': _L0_ffn_in['in_proj_b'], 'L0_ffn_out_proj_w': _L0_ffn_in['out_proj_w'], 'L0_ffn_out_proj_b': _L0_ffn_in['out_proj_b'], 'L0_ffn_ln1_g': _L0_ffn_in['ln1_g'], 'L0_ffn_ln1_b': _L0_ffn_in['ln1_b'], 'L0_ffn_ln2_g': _L0_ffn_in['ln2_g'], 'L0_ffn_ln2_b': _L0_ffn_in['ln2_b'], 'L0_ffn_wg': _L0_ffn_in['wg'], 'L0_ffn_w1': _L0_ffn_in['w1'], 'L0_ffn_b1': _L0_ffn_in['b1'], 'L0_ffn_w2': _L0_ffn_in['w2'], 'L0_ffn_b2': _L0_ffn_in['b2']}
    _x0 = _d['L0_attn_x']
    _d['L0_attn_x'] = jax.random.normal(jax.random.fold_in(jax.random.key(seed), 1), (16, 512, 128), dtype=_x0.dtype)
    del _x0
    return _d

def reference(L0_attn_x, L0_attn_Wq, L0_attn_bq, L0_attn_Wk, L0_attn_bk, L0_attn_Wv, L0_attn_bv, L0_attn_Wo, L0_attn_norm_w, L0_ffn_in_proj_w, L0_ffn_in_proj_b, L0_ffn_out_proj_w, L0_ffn_out_proj_b, L0_ffn_ln1_g, L0_ffn_ln1_b, L0_ffn_ln2_g, L0_ffn_ln2_b, L0_ffn_wg, L0_ffn_w1, L0_ffn_b1, L0_ffn_w2, L0_ffn_b2):

    def _L0_attn_ref(x, Wq, bq, Wk, bk, Wv, bv, Wo, norm_w):
        import jax, jax.numpy as jnp
        import numpy as np
        D_MODEL = 128
        N_HEAD = 16
        D_HEAD = D_MODEL // N_HEAD
        N_CTX = 256
        ROPE_BASE = 10000.0
        SCALE = 1

        def _rope_cache(seq_len, d_head, dtype=jnp.float32):
            inv_freq = 1.0 / ROPE_BASE ** (jnp.arange(0, d_head, 2, dtype=jnp.float32) / d_head)
            t = jnp.arange(seq_len, dtype=jnp.float32)
            freqs = jnp.outer(t, inv_freq)
            emb = jnp.concatenate([freqs, freqs], -1)
            cos = jnp.cos(emb)[None, :, None, :].astype(dtype)
            sin = jnp.sin(emb)[None, :, None, :].astype(dtype)
            return (cos, sin)

        def _apply_rope(x, cos, sin):
            x_even = x[..., 0::2]
            x_odd = x[..., 1::2]
            x_rot = jnp.stack([-x_odd, x_even], axis=-1).reshape(x.shape)
            return x * cos + x_rot * sin

        def _rmsnorm(x, w):
            eps = jnp.finfo(x.dtype).eps
            var = jnp.mean(jnp.square(x), axis=-1, keepdims=True)
            return x * jax.lax.rsqrt(var + eps) * w
        B, S, _ = x.shape
        split = lambda t: t.reshape(B, S, N_HEAD, D_HEAD)
        q = split(x @ Wq.T + bq)
        k = split(x @ Wk.T + bk)
        v = split(x @ Wv.T + bv)
        cos, sin = _rope_cache(S, D_HEAD, x.dtype)
        q = _apply_rope(_rmsnorm(q, norm_w), cos, sin)
        k = _apply_rope(_rmsnorm(k, norm_w), cos, sin)
        scores = jnp.einsum('bqhd,bkhd->bhqk', q, k)
        causal = jnp.tril(jnp.ones((S, S), x.dtype))
        pattern = jnp.square(scores / D_HEAD) * causal
        z = jnp.einsum('bhqk,bkhd->bqhd', pattern, v).reshape(B, S, D_MODEL)
        return x + z @ Wo.T * SCALE

    def _L0_ffn_ref(x, in_proj_w, in_proj_b, out_proj_w, out_proj_b, ln1_g, ln1_b, ln2_g, ln2_b, wg, w1, b1, w2, b2):
        import jax, jax.numpy as jnp
        import numpy as np
        D = 128
        H = 4
        HD = D // H
        E = 8
        FF = 512
        CAP_FACTOR = 1.0

        def _ln(x, g, b, eps=1e-05):
            mu = jnp.mean(x, -1, keepdims=True)
            v = jnp.mean((x - mu) ** 2, -1, keepdims=True)
            return (x - mu) * jax.lax.rsqrt(v + eps) * g + b

        def _mha(x, w, b, ow, ob):
            L, N, _ = x.shape
            qkv = x @ w.T + b
            q, k, v = jnp.split(qkv, 3, axis=-1)
            rh = lambda t: t.reshape(L, N, H, HD).transpose(1, 2, 0, 3)
            q, k, v = (rh(q), rh(k), rh(v))
            scores = jnp.einsum('nhld,nhmd->nhlm', q, k) / np.float32(np.sqrt(HD))
            attn = jax.nn.softmax(scores, axis=-1)
            o = jnp.einsum('nhlm,nhmd->nhld', attn, v).transpose(2, 0, 1, 3).reshape(L, N, D)
            return o @ ow.T + ob

        def _moe(x, wg, w1, b1, w2, b2):
            L, N, _ = x.shape
            S = L * N
            cap = int(CAP_FACTOR * S) // E
            xf = x.reshape(S, D)
            gates = jax.nn.softmax(xf @ wg, axis=-1)
            idx = jnp.argmax(gates, axis=-1)
            mask1 = jax.nn.one_hot(idx, E, dtype=x.dtype)
            loc = jnp.sum((jnp.cumsum(mask1, 0) - 1.0) * mask1, -1).astype(jnp.int32)
            keep = loc < cap
            gate_val = jnp.take_along_axis(gates, idx[:, None], -1)[:, 0]
            slot = jnp.where(keep, idx.astype(jnp.int32) * cap + loc, E * cap)
            disp = jnp.zeros((E * cap, D), x.dtype).at[slot].set(xf, mode='drop')
            disp = disp.reshape(E, cap, D)
            h = jnp.einsum('ecd,edf->ecf', disp, w1) + b1[:, None, :]
            y = (jnp.einsum('ecf,efd->ecd', h, w2) + b2[:, None, :]).reshape(E * cap, D)
            out = jnp.where(keep[:, None], gate_val[:, None] * y[jnp.minimum(slot, E * cap - 1)], 0.0)
            return out.reshape(L, N, D)
        y1 = _ln(x + _mha(x, in_proj_w, in_proj_b, out_proj_w, out_proj_b), ln1_g, ln1_b)
        y2 = _ln(y1 + _moe(y1, wg, w1, b1, w2, b2), ln2_g, ln2_b)
        return y2
    x = L0_attn_x
    xn = _layernorm(x, axis=-1)
    x = x + _L0_attn_ref(xn, L0_attn_Wq, L0_attn_bq, L0_attn_Wk, L0_attn_bk, L0_attn_Wv, L0_attn_bv, L0_attn_Wo, L0_attn_norm_w) + _L0_ffn_ref(xn, L0_ffn_in_proj_w, L0_ffn_in_proj_b, L0_ffn_out_proj_w, L0_ffn_out_proj_b, L0_ffn_ln1_g, L0_ffn_ln1_b, L0_ffn_ln2_g, L0_ffn_ln2_b, L0_ffn_wg, L0_ffn_w1, L0_ffn_b1, L0_ffn_w2, L0_ffn_b2)
    return x

_drawn_inputs = setup_inputs


def setup_inputs(seed=0):
    import zlib

    import numpy as np

    out = dict(_drawn_inputs(seed))
    spreads = {'L0_attn_norm_w': (1.0, 0.2),
     'L0_ffn_in_proj_b': (0.0, 0.8),
     'L0_ffn_out_proj_b': (0.0, 0.1),
     'L0_ffn_ln1_g': (1.0, 0.2),
     'L0_ffn_ln1_b': (0.0, 0.1),
     'L0_ffn_ln2_g': (1.0, 0.2),
     'L0_ffn_ln2_b': (0.0, 0.1),
     'L0_ffn_b1': (0.0, 0.8),
     'L0_ffn_b2': (0.0, 0.8)}
    factors = {'L0_attn_bq': 5.955,
     'L0_attn_bk': 5.098,
     'L0_ffn_in_proj_w': 8.0,
     'L0_ffn_out_proj_w': 6.519,
     'L0_ffn_wg': 7.555,
     'L0_ffn_w1': 8.0,
     'L0_ffn_w2': 8.0}
    for name, (base, spread) in spreads.items():
        noise = np.random.default_rng([zlib.crc32(name.encode()), seed]).standard_normal(out[name].shape)
        drawn = base * np.exp(spread * noise) if base else spread * noise
        out[name] = jnp.asarray(drawn.astype(out[name].dtype))
    for name, factor in factors.items():
        out[name] = (out[name] * factor).astype(out[name].dtype)
    return out
```

```python
from contextlib import ExitStack

import numpy as np

import concourse.bass as bass
from concourse import mybir

ALU = mybir.AluOpType
ACT = mybir.ActivationFunctionType
F32 = mybir.dt.float32
BF16 = mybir.dt.bfloat16
AX = mybir.AxisListType.X

P = 128
D = 128
LB, NS = 16, 512
TT = 4
NB = LB * NS // (TT * P)
HA, DA = 16, 8
HB, DB = 4, 32
GA = 4
OFF = 5
FB = HA * OFF * DA // P
E, FF = 8, 512
CAP = LB * NS // E
LN_EPS = 1e-5
RMS_EPS = float(np.finfo(np.float32).eps)
NEG = -1e30


class Batch:

    def __init__(self, i, off):
        self.i, self.off = i, off

    def next(self):
        return Batch(self.i, self.off + 1)

    def prev(self):
        return Batch(self.i, self.off - 1)

    @property
    def number(self):
        return self.i * 2 + self.off

    @property
    def parity(self):
        return self.off % 2


class Signal:

    def __init__(self, sem, per):
        self.sem, self.per = sem, per

    def by(self, b, n=None):
        const = b.off * self.per + (self.per if n is None else n) + 1
        if isinstance(b.i, int):
            return max(b.i * 2 * self.per + const, 1)
        assert const >= 1, "a wait below one"
        return b.i * (2 * self.per) + const


def start(eng, signals):
    for sig in signals:
        eng.sem_inc(sig.sem, 1)


def build(nc, t):
    x, out = t["x"], t["out"]
    ctx = ExitStack()
    with ctx:
        def sb(name, shape, dt=F32):
            return ctx.enter_context(nc.sbuf_tensor(name, shape, dt))

        bank = [ctx.enter_context(nc.psum_tensor(f"bank{i}", [P, 512], F32)) for i in range(8)]
        ident = sb("ident", [P, P])
        wqkvT = sb("wqkvT", [P, 3 * D])
        woT = sb("woT", [P, D])
        ipT = sb("ipT", [P, 3 * D])
        opT = sb("opT", [P, D])
        mexp = sb("mexp", [P, E * D])
        cpad = sb("cpad", [TT * E, TT, D])
        wg = sb("wg", [P, E])
        bqkv = sb("bqkv", [P, 3 * D])
        bcol = sb("bcol", [P, 3])
        pbias = sb("pbias", [P, D])
        ln = sb("ln", [P, 4, D])
        nw = sb("nw", [P, DA])
        rope = sb("rope", [P, 2, TT, DA])
        featw = sb("featw", [P, FB, D])
        jmask = sb("jmask", [P, GA])
        blockmask = sb("blockmask", [P, 32])
        upper = sb("upper", [P, P], BF16)
        ones = sb("ones", [P, P], BF16)
        first = sb("first", [P, E])
        mhalf = sb("mhalf", [P, TT])
        lneps = sb("lneps", [P, TT])
        tmask = sb("tmask", [TT * E, TT])
        eps = sb("eps", [P, 1])
        carry = sb("carry", [P, E])

        y1_dram = t["y1"]
        setup(nc, t, bank, locals())
        softmax_attention(nc, t, bank, locals())
        squared_attention_and_experts(nc, t, bank, locals())


def setup(nc, t, bank, m):
    opT, mexp, cpad, rope, nw, tmask = m["opT"], m["mexp"], m["cpad"], m["rope"], m["nw"], m["tmask"]
    FC = FF // P
    ctx = ExitStack()
    with ctx:
        def sb(name, shape, dt=F32):
            return ctx.enter_context(nc.sbuf_tensor(name, shape, dt))

        def sem(name):
            return ctx.enter_context(nc.semaphore(name))

        w1T = sb("w1T", [P, E, FC, D])
        w2 = sb("w2", [P, E, FC, D])
        b1T = sb("b1T", [P, E, FC])
        b1pad = sb("b1pad", [P, E, FC, TT * E])
        b2r = sb("b2r", [TT * E, D])
        c32 = sb("c32", [TT * E, D])
        bvrep = sb("bvrep", [P, P])
        onesf = sb("onesf", [P, P])
        trig = sb("trig", [P, 2, TT, DA])
        obias = sb("obias", [P, D])

        small_loaded, experts_loaded = sem("small_loaded"), sem("experts_loaded")
        small_loads = []
        fills, zeroed, rope_ready, bvrep_ready, b1pad_ready, pb_full, pb_ready = (
            sem(n) for n in ("fills", "zeroed", "rope_ready", "bvrep_ready", "b1pad_ready", "pb_full", "pb_ready"))
        m_full, m_read, c_full, c_ready, cpad_ready = (
            sem(n) for n in ("m_full", "m_read", "c_full", "c_ready", "cpad_ready"))

        block = ctx.enter_context(nc.Block())

        def wide(v):
            return v.rearrange("(a n) -> a n", a=1).broadcast_to([P, v.shape[0]])

        small = [(m["ident"][:], t["c_ident"]), (m["wqkvT"][:], t["wqkvT"]), (m["woT"][:], t["woT"]),
                 (m["ipT"][:], t["ipT"]), (opT[:], t["opT"]), (m["bcol"][:], t["bcol"]), (m["wg"][:], t["wg"]),
                 (nw[:], wide(t["norm_w"])), (obias[:], wide(t["out_proj_b"])), (trig[:], t["c_trig"]),
                 (m["featw"][:], t["c_featw"]), (m["jmask"][:], t["c_jmask"]), (m["blockmask"][:], t["c_blockmask"]),
                 (m["upper"][:], t["c_upper"]), (m["first"][:], t["c_first"]), (tmask[:], t["c_tmask"])]
        small += [(m["bqkv"][:, i * D:(i + 1) * D], wide(t[n])) for i, n in enumerate(("bq", "bk", "bv"))]
        small += [(m["ln"][:, i, :], wide(t[n])) for i, n in enumerate(("ln1_g", "ln1_b", "ln2_g", "ln2_b"))]
        small += [(b2r[i * E:(i + 1) * E, :], t["b2"]) for i in range(TT)] + [(b1T[:], t["b1T"])]

        @block.sync
        def _(sp):
            for e in range(0, E, 4):
                sp.dma_start(w1T[:, e:e + 4], t["w1T"][:, e:e + 4]).then_inc(experts_loaded, 16)
                sp.dma_start(w2[:, e:e + 4], t["w2"][:, e:e + 4]).then_inc(experts_loaded, 16)

        @block.scalar
        def _(act):
            for d, src in small:
                act.dma_start(d, src).then_inc(small_loaded, 16)

        @block.gpsimd
        def _(pool):
            nc.gpsimd.memset(b1pad[:], 0.0).then_inc(zeroed, 1)
            nc.gpsimd.memset(m["ones"][:], 1.0).then_inc(fills, 1)
            nc.gpsimd.memset(m["mhalf"][:], -0.5).then_inc(fills, 1)
            nc.gpsimd.memset(m["lneps"][:], LN_EPS).then_inc(fills, 1)
            nc.gpsimd.memset(m["eps"][:], RMS_EPS).then_inc(fills, 1)
            nc.gpsimd.memset(m["carry"][:], 0.0).then_inc(fills, 1)

        @block.vector
        def _(dve):
            nc.vector.memset(onesf[:], 1.0).then_inc(fills, 1)
            dve.wait_ge(small_loaded, 16 * len(small))
            dve.wait_ge(fills, 6)
            nc.vector.tensor_scalar(bvrep[:], onesf[:], m["bcol"][:, 2:3], None, ALU.mult).then_inc(bvrep_ready, 1)
            dve.wait_ge(zeroed, 1)
            for e in range(E):
                nc.vector.tensor_copy(b1pad[:, e, :, e::E], b1T[:, e, :].unsqueeze(2).broadcast_to([P, FC, TT])).then_inc(b1pad_ready, 1)
            for c in range(TT):
                nc.vector.tensor_tensor(rope[:, 0, c, :], trig[:, 0, c, :], nw[:], ALU.mult).then_inc(rope_ready, 1)
                for h in range(2):
                    nc.vector.tensor_tensor(rope[:, 1, c, h::2], trig[:, 1, c, h::2], nw[:, 1 - h::2], ALU.mult).then_inc(rope_ready, 1)
            dve.wait_ge(pb_full, 1)
            nc.vector.tensor_tensor(m["pbias"][:], bank[5][:, 0:D], obias[:], ALU.add).then_inc(pb_ready, 1)
            for e in range(E):
                dve.wait_ge(m_full, e + 1)
                nc.vector.tensor_copy(mexp[:, e * D:(e + 1) * D], bank[6 + e % 2][:, 0:D]).then_inc(m_read, 1)
            dve.wait_ge(c_full, 1)
            nc.vector.tensor_tensor(c32[:], bank[4][0:TT * E, 0:D], b2r[:], ALU.add).then_inc(c_ready, 1)
            dve.wait_ge(c_ready, 1)
            for i in range(TT):
                nc.vector.tensor_scalar(cpad[:, i, :], c32[:], tmask[:, i:i + 1], None, ALU.mult).then_inc(cpad_ready, 1)
            dve.wait_ge(cpad_ready, TT)
            dve.wait_ge(rope_ready, 3 * TT)
            dve.wait_ge(pb_ready, 1)
            dve.wait_ge(m_read, E)

        @block.tensor
        def _(pe):
            pe.wait_ge(small_loaded, 16 * len(small))
            pe.wait_ge(bvrep_ready, 1)
            nc.tensor.matmul(bank[5][:, 0:D], bvrep[:], opT[:], start=True, stop=True).then_inc(pb_full, 1)
            pe.wait_ge(experts_loaded, 16 * 4)
            for e in range(E):
                if e >= 2:
                    pe.wait_ge(m_read, e - 1)
                for c in range(FC):
                    last = nc.tensor.matmul(bank[6 + e % 2][:, 0:D], w1T[:, e, c, :], w2[:, e, c, :],
                                            start=(c == 0), stop=(c == FC - 1))
                last.then_inc(m_full, 1)
            pe.wait_ge(b1pad_ready, E)
            for e in range(E):
                for c in range(FC):
                    last = nc.tensor.matmul(bank[4][0:TT * E, 0:D], b1pad[:, e, c, :], w2[:, e, c, :],
                                            start=(e == 0 and c == 0), stop=(e == E - 1 and c == FC - 1))
            last.then_inc(c_full, 1)


def softmax_attention(nc, t, bank, m):
    ident, ipT, opT, bcol, pbias, ln, mhalf, lneps, blockmask = (
        m[k] for k in ("ident", "ipT", "opT", "bcol", "pbias", "ln", "mhalf", "lneps", "blockmask"))
    x, y1_dram = t["x"], t["y1"]
    ctx = ExitStack()
    with ctx:
        def sb(name, shape, dt=F32):
            return ctx.enter_context(nc.sbuf_tensor(name, shape, dt))

        def sig(name, per=1):
            return Signal(ctx.enter_context(nc.semaphore(name)), per)

        two = range(2)
        xs = [sb(f"xs{i}", [P, TT, D]) for i in two]
        stats = sb("stats", [P, TT, 6])
        mv = sb("mv", [P, TT, 2])
        rstd = sb("rstd", [P, TT])
        xn = sb("xn", [P, TT, D])
        xT = [sb(f"xT{i}", [P, TT * P]) for i in two]
        qT = sb("qT", [P, TT * P])
        kTm = sb("kTm", [P, HB, TT * P])
        v = [sb(f"v{i}", [P, TT, D]) for i in two]
        sc = sb("sc", [P, TT * HB, 32])
        mx = sb("mx", [P, TT * HB])
        ex = sb("ex", [P, TT * HB, 32])
        sm = sb("sm", [P, TT * HB])
        rs = sb("rs", [P, TT * HB])
        pr = sb("pr", [P, TT * HB, 32])
        pT = sb("pT", [P, TT * HB, P])
        oT = sb("oT", [P, TT * P])
        y = sb("y", [P, TT, D])
        stats1 = sb("stats1", [P, TT, 6])
        mv1 = sb("mv1", [P, TT, 2])
        rstd1 = sb("rstd1", [P, TT])
        yn = sb("yn", [P, TT, D])
        yg = sb("yg", [P, TT, D])
        y1 = [sb(f"y1_{i}", [P, TT, D]) for i in two]

        x_loaded = [Signal(ctx.enter_context(nc.semaphore(f"a_x_loaded{i}")), 0) for i in two]
        stored = [Signal(ctx.enter_context(nc.semaphore(f"a_y1_stored{i}")), 0) for i in two]
        zeroed = sig("a_zeroed")
        alone = ctx.enter_context(nc.semaphore("a_alone"))
        s = {n: sig("a_" + n, per) for n, per in dict(
            stats=TT, mv=TT, veps=1, rstd=1, xn=TT, xT_full=1, xT=1, q_full=1, q=1, k_full=1, k=HB, v_full=1, v=1,
            sc_full=1, sc=1, mx=1, sub=1, ex=1, sm=1, rs=1, pr=1, pT=TT, o_full=1, o=1, y_full=1, y=1,
            stats1=TT, mv1=TT, veps1=1, rstd1=1, yn=TT, yg=1, y1=1).items()}

        xv = x.rearrange("l (g t n) d -> g n l t d", t=TT, n=8)
        yv = y1_dram.rearrange("l (g t n) d -> g n l t d", t=TT, n=8)
        B_XT, B_Q, B_K, B_V, B_S, B_O, B_Y = bank[0:7]
        block = ctx.enter_context(nc.Block())

        @block.sync
        def _(sp):
            def load(b, wait=True):
                if wait:
                    sp.wait_ge(s["xn"].sem, s["xn"].by(b.prev().prev()))
                for n in range(8):
                    sp.dma_start(xs[b.parity][16 * n:16 * n + 16, :, :], xv[b.number, n]).then_inc(x_loaded[b.parity].sem, 16)

            def store(b):
                sp.wait_ge(s["y1"].sem, s["y1"].by(b))
                for n in range(8):
                    sp.dma_start(yv[b.number, n], y1[b.parity][16 * n:16 * n + 16, :, :]).then_inc(stored[b.parity].sem, 16)

            for o in two:
                load(Batch(0, o), wait=False)
            start(sp, [*s.values(), zeroed, *stored])
            with sp.Fori(0, NB // 2 - 1) as i:
                for o in two:
                    load(Batch(i, o + 2))
                    store(Batch(i, o))
            for o in two:
                store(Batch(NB // 2 - 1, o))
            for o in two:
                sp.wait_ge(stored[o].sem, 128 * (NB // 2) + 1)

        @block.tensor
        def _(pe):
            def project(b):
                pe.wait_ge(s["xn"].sem, s["xn"].by(b))
                pe.wait_ge(s["xT"].sem, s["xT"].by(b.prev()))
                for c in range(TT):
                    last = nc.tensor.transpose(B_XT[:, c * P:(c + 1) * P], xn[:, c, :], ident[:])
                last.then_inc(s["xT_full"].sem, 1)
                pe.wait_ge(s["xT"].sem, s["xT"].by(b))
                pe.wait_ge(s["q"].sem, s["q"].by(b.prev()))
                nc.tensor.matmul(B_Q[:], ipT[:, 0:D], xT[b.parity][:], start=True, stop=True).then_inc(s["q_full"].sem, 1)
                pe.wait_ge(s["k"].sem, s["k"].by(b.prev()))
                nc.tensor.matmul(B_K[:], ipT[:, D:2 * D], xT[b.parity][:], start=True, stop=True).then_inc(s["k_full"].sem, 1)
                pe.wait_ge(s["v"].sem, s["v"].by(b.prev()))
                for c in range(TT):
                    last = nc.tensor.matmul(B_V[:, c * D:(c + 1) * D], xT[b.parity][:, c * P:(c + 1) * P],
                                            ipT[:, 2 * D:3 * D], start=True, stop=True)
                last.then_inc(s["v_full"].sem, 1)

            def scores(b):
                pe.wait_ge(s["q"].sem, s["q"].by(b))
                pe.wait_ge(s["k"].sem, s["k"].by(b))
                pe.wait_ge(s["sc"].sem, s["sc"].by(b.prev()))
                for c in range(TT):
                    for k in range(4):
                        a = c * P + 32 * k
                        last = nc.tensor.matmul(B_S[32 * k:32 * k + 32, c * P:(c + 1) * P], qT[:, a:a + 32],
                                                kTm[:, :, a:a + 32], start=True, stop=True)
                last.then_inc(s["sc_full"].sem, 1)

            def values(b):
                pe.wait_ge(s["v"].sem, s["v"].by(b))
                pe.wait_ge(s["pT"].sem, s["pT"].by(b))
                pe.wait_ge(s["o"].sem, s["o"].by(b.prev()))
                for c in range(TT):
                    for h in range(HB):
                        last = nc.tensor.matmul(B_O[32 * h:32 * h + 32, c * P:(c + 1) * P], v[b.parity][:, c, 32 * h:32 * h + 32],
                                                pT[:, c * HB + h, :], start=True, stop=True)
                last.then_inc(s["o_full"].sem, 1)

            def output(b):
                pe.wait_ge(s["o"].sem, s["o"].by(b))
                pe.wait_ge(s["y"].sem, s["y"].by(b.prev()))
                for c in range(TT):
                    nc.tensor.matmul(B_Y[:, c * D:(c + 1) * D], oT[:, c * P:(c + 1) * P], opT[:], start=True, stop=False)
                    last = nc.tensor.matmul(B_Y[:, c * D:(c + 1) * D], xT[b.parity][:, c * P:(c + 1) * P], ident[:],
                                            start=False, stop=True)
                last.then_inc(s["y_full"].sem, 1)

            def body(b):
                scores(b)
                project(b.next())
                values(b)
                output(b)

            project(Batch(0, 0))
            with pe.Fori(0, NB // 2 - 1) as i:
                for o in two:
                    body(Batch(i, o))
            body(Batch(NB // 2 - 1, 0))
            last_b = Batch(NB // 2 - 1, 1)
            scores(last_b)
            values(last_b)
            output(last_b)

        @block.scalar
        def _(act):
            def project(b):
                act.wait_ge(s["xT_full"].sem, s["xT_full"].by(b))
                act.wait_ge(s["y_full"].sem, s["y_full"].by(b.prev().prev()))
                nc.scalar.activation(xT[b.parity][:], B_XT[:], ACT.Copy).then_inc(s["xT"].sem, 1)
                act.wait_ge(s["q_full"].sem, s["q_full"].by(b))
                act.wait_ge(s["sc_full"].sem, s["sc_full"].by(b.prev()))
                nc.scalar.activation(qT[:], B_Q[:], ACT.Identity, bias=bcol[:, 0:1]).then_inc(s["q"].sem, 1)
                act.wait_ge(s["k_full"].sem, s["k_full"].by(b))
                act.wait_ge(zeroed.sem, zeroed.by(Batch(0, 0), 1))
                for h in range(HB):
                    r = slice(32 * h, 32 * h + 32)
                    nc.scalar.activation(kTm[r, h, :], B_K[r, :], ACT.Identity, bias=bcol[r, 1:2]).then_inc(s["k"].sem, 1)
                act.wait_ge(s["v_full"].sem, s["v_full"].by(b))
                act.wait_ge(s["o_full"].sem, s["o_full"].by(b.prev().prev()))
                nc.scalar.activation(v[b.parity][:].rearrange("p t d -> p (t d)"), B_V[:], ACT.Copy).then_inc(s["v"].sem, 1)

            def exps(b):
                act.wait_ge(s["sub"].sem, s["sub"].by(b))
                act.wait_ge(s["pr"].sem, s["pr"].by(b.prev()))
                nc.scalar.activation(ex[:].rearrange("p a k -> p (a k)"), sc[:].rearrange("p a k -> p (a k)"), ACT.Exp).then_inc(s["ex"].sem, 1)

            def outs(b):
                act.wait_ge(s["o_full"].sem, s["o_full"].by(b))
                act.wait_ge(s["y_full"].sem, s["y_full"].by(b.prev()))
                nc.scalar.activation(oT[:], B_O[:], ACT.Copy).then_inc(s["o"].sem, 1)

            project(Batch(0, 0))
            with act.Fori(0, NB // 2 - 1) as i:
                for o in two:
                    b = Batch(i, o)
                    exps(b)
                    project(b.next())
                    outs(b)
            b = Batch(NB // 2 - 1, 0)
            exps(b)
            project(b.next())
            outs(b)
            exps(b.next())
            outs(b.next())

        @block.gpsimd
        def _(pool):
            def norm_rstd(b):
                pool.wait_ge(s["mv"].sem, s["mv"].by(b))
                pool.wait_ge(s["xn"].sem, s["xn"].by(b.prev()))
                nc.gpsimd.tensor_tensor(rstd[:], mv[:, :, 1], lneps[:], ALU.add).then_inc(s["veps"].sem, 1)
                pool.wait_ge(s["veps"].sem, s["veps"].by(b))
                nc.gpsimd.tensor_tensor(rstd[:], rstd[:], mhalf[:], ALU.pow).then_inc(s["rstd"].sem, 1)

            def norm_rstd1(b):
                pool.wait_ge(s["mv1"].sem, s["mv1"].by(b))
                pool.wait_ge(s["yn"].sem, s["yn"].by(b.prev()))
                nc.gpsimd.tensor_tensor(rstd1[:], mv1[:, :, 1], lneps[:], ALU.add).then_inc(s["veps1"].sem, 1)
                pool.wait_ge(s["veps1"].sem, s["veps1"].by(b))
                nc.gpsimd.tensor_tensor(rstd1[:], rstd1[:], mhalf[:], ALU.pow).then_inc(s["rstd1"].sem, 1)

            def probs(b):
                pool.wait_ge(s["rs"].sem, s["rs"].by(b))
                pool.wait_ge(s["pT"].sem, s["pT"].by(b.prev()))
                nc.gpsimd.tensor_tensor(pr[:], ex[:], rs[:].unsqueeze(2).broadcast_to([P, TT * HB, 32]), ALU.mult).then_inc(s["pr"].sem, 1)

            def gain(b):
                pool.wait_ge(s["yn"].sem, s["yn"].by(b))
                pool.wait_ge(s["y1"].sem, s["y1"].by(b.prev()))
                nc.gpsimd.tensor_tensor(yg[:], yn[:], ln[:, 0, :].unsqueeze(1).broadcast_to([P, TT, D]), ALU.mult).then_inc(s["yg"].sem, 1)

            nc.gpsimd.memset(kTm[:], 0.0)
            nc.gpsimd.memset(pT[:], 0.0).then_inc(zeroed.sem, 1)
            norm_rstd(Batch(0, 0))
            with pool.Fori(0, NB // 2 - 1) as i:
                for o in two:
                    b = Batch(i, o)
                    norm_rstd(b.next())
                    probs(b)
                    norm_rstd1(b)
                    gain(b)
            b = Batch(NB // 2 - 1, 0)
            norm_rstd(b.next())
            for b in (b, b.next()):
                probs(b)
                norm_rstd1(b)
                gain(b)

        @block.vector
        def _(dve):
            def norm_stats(b):
                dve.wait_ge(x_loaded[b.parity].sem, b.i * 128 + 128 * (b.off // 2 + 1))
                dve.wait_ge(s["rstd"].sem, s["rstd"].by(b.prev()))
                for c in range(TT):
                    nc.vector.bn_stats(stats[:, c, :], xs[b.parity][:, c, :]).then_inc(s["stats"].sem, 1)
                dve.wait_ge(s["stats"].sem, s["stats"].by(b))
                dve.sem_inc(alone, 1)
                for c in range(TT):
                    nc.vector.bn_aggr(mv[:, c, :], stats[:, c, :]).then_inc(s["mv"].sem, 1)

            def norm(b):
                dve.wait_ge(s["mv"].sem, s["mv"].by(b))
                dve.wait_ge(s["rstd"].sem, s["rstd"].by(b))
                dve.wait_ge(s["xT_full"].sem, s["xT_full"].by(b.prev()))
                for c in range(TT):
                    nc.vector.tensor_scalar(xn[:, c, :], xs[b.parity][:, c, :], mv[:, c, 0:1], rstd[:, c:c + 1],
                                            ALU.subtract, ALU.mult).then_inc(s["xn"].sem, 1)

            def softmax_top(b):
                dve.wait_ge(s["sc_full"].sem, s["sc_full"].by(b))
                dve.wait_ge(s["ex"].sem, s["ex"].by(b.prev()))
                nc.vector.scalar_tensor_tensor(out=sc[:], in0=B_S[:].rearrange("p (a k) -> p a k", k=32), scalar=float(DB) ** -0.5,
                                               in1=blockmask[:].unsqueeze(1).broadcast_to([P, TT * HB, 32]),
                                               op0=ALU.mult, op1=ALU.add).then_inc(s["sc"].sem, 1)
                dve.wait_ge(s["sc"].sem, s["sc"].by(b))
                nc.vector.tensor_reduce(mx[:], sc[:], AX, ALU.max).then_inc(s["mx"].sem, 1)
                dve.wait_ge(s["mx"].sem, s["mx"].by(b))
                nc.vector.tensor_tensor(sc[:], sc[:], mx[:].unsqueeze(2).broadcast_to([P, TT * HB, 32]), ALU.subtract).then_inc(s["sub"].sem, 1)

            def softmax_sum(b):
                dve.wait_ge(s["ex"].sem, s["ex"].by(b))
                nc.vector.tensor_reduce(sm[:], ex[:], AX, ALU.add).then_inc(s["sm"].sem, 1)
                dve.wait_ge(s["sm"].sem, s["sm"].by(b))
                dve.wait_ge(s["pr"].sem, s["pr"].by(b.prev()))
                nc.vector.reciprocal(rs[:], sm[:]).then_inc(s["rs"].sem, 1)

            def turn(b):
                dve.wait_ge(s["pr"].sem, s["pr"].by(b))
                dve.wait_ge(s["o_full"].sem, s["o_full"].by(b.prev()))
                for k in range(4):
                    r = slice(32 * k, 32 * k + 32)
                    nc.vector.transpose(pT[r, :, r], pr[r, :, :]).then_inc(s["pT"].sem, 1)

            def residual(b):
                dve.wait_ge(s["y_full"].sem, s["y_full"].by(b))
                dve.wait_ge(s["yn"].sem, s["yn"].by(b.prev()))
                nc.vector.tensor_tensor(y[:], B_Y[:].rearrange("p (t d) -> p t d", t=TT),
                                        pbias[:].unsqueeze(1).broadcast_to([P, TT, D]), ALU.add).then_inc(s["y"].sem, 1)
                dve.wait_ge(s["y"].sem, s["y"].by(b))
                dve.wait_ge(s["rstd1"].sem, s["rstd1"].by(b.prev()))
                for c in range(TT):
                    nc.vector.bn_stats(stats1[:, c, :], y[:, c, :]).then_inc(s["stats1"].sem, 1)
                dve.wait_ge(s["stats1"].sem, s["stats1"].by(b))
                dve.sem_inc(alone, 1)
                for c in range(TT):
                    nc.vector.bn_aggr(mv1[:, c, :], stats1[:, c, :]).then_inc(s["mv1"].sem, 1)

            def norm1(b):
                dve.wait_ge(s["rstd1"].sem, s["rstd1"].by(b))
                dve.wait_ge(s["yg"].sem, s["yg"].by(b.prev()))
                for c in range(TT):
                    nc.vector.tensor_scalar(yn[:, c, :], y[:, c, :], mv1[:, c, 0:1], rstd1[:, c:c + 1],
                                            ALU.subtract, ALU.mult).then_inc(s["yn"].sem, 1)

            def shift(b):
                dve.wait_ge(s["yg"].sem, s["yg"].by(b))
                done = b.i * 128 + 128 * (b.off // 2)
                if not isinstance(b.i, int) or done > 0:
                    dve.wait_ge(stored[b.parity].sem, done + 1)
                nc.vector.tensor_tensor(y1[b.parity][:], yg[:], ln[:, 1, :].unsqueeze(1).broadcast_to([P, TT, D]), ALU.add).then_inc(s["y1"].sem, 1)

            dve.wait_ge(zeroed.sem, zeroed.by(Batch(0, 0), 1))
            norm_stats(Batch(0, 0))
            norm(Batch(0, 0))

            def body(b, more=True):
                if more:
                    norm_stats(b.next())
                softmax_top(b)
                if more:
                    norm(b.next())
                softmax_sum(b)
                turn(b)
                residual(b)
                norm1(b)
                shift(b)

            with dve.Fori(0, NB // 2 - 1) as i:
                for o in two:
                    body(Batch(i, o))
            body(Batch(NB // 2 - 1, 0))
            body(Batch(NB // 2 - 1, 1), more=False)


def squared_attention_and_experts(nc, t, bank, m):
    ident, wqkvT, woT, mexp, cpad, wg, bqkv, ln, rope, featw, jmask = (
        m[k] for k in ("ident", "wqkvT", "woT", "mexp", "cpad", "wg", "bqkv", "ln", "rope", "featw", "jmask"))
    upper, ones, first, mhalf, lneps, eps, carry = (m[k] for k in ("upper", "ones", "first", "mhalf", "lneps", "eps", "carry"))
    x, y1_dram, out = t["x"], t["y1"], t["out"]
    H2 = 2 * HA
    W = OFF * DA
    ctx = ExitStack()
    with ctx:
        def sb(name, shape, dt=F32):
            return ctx.enter_context(nc.sbuf_tensor(name, shape, dt))

        def sem(name):
            return ctx.enter_context(nc.semaphore(name))

        two = range(2)
        xs = [sb(f"b_xs{i}", [P, TT, D]) for i in two]
        y1 = [sb(f"b_y1_{i}", [P, TT, D]) for i in two]
        stats, mv, rstd = sb("b_stats", [P, TT, 6]), sb("b_mv", [P, TT, 2]), sb("b_rstd", [P, TT])
        xn = sb("b_xn", [P, TT, D])
        res = [sb(f"res{i}", [P, TT, D]) for i in two]
        xT = sb("b_xT", [P, TT * P])
        qkv = [sb(f"qkv{i}", [P, TT, 3 * D]) for i in two]
        vm = [sb(f"vm{i}", [P, TT, HA, 32]) for i in two]
        sq = sb("sq", [P, TT, H2, DA])
        ms, lnv, r0, va, ra, rb, rc, rr = (sb(n, [P, TT, H2]) for n in ("ms", "lnv", "r0", "va", "ra", "rb", "rc", "rr"))
        qn = sb("qn", [P, TT, H2, DA])
        t1 = sb("t1", [P, TT, H2, DA])
        t2 = sb("t2", [P, TT, H2, DA])
        qr = sb("qr", [P, TT, 2 * D])
        qd = [sb(f"qd{i}", [P, TT, H2, DA + OFF - 1]) for i in two]
        qm = [sb(f"qm{i}", [P, GA, TT * P]) for i in two]
        kg = [sb(f"kg{i}", [P, GA, TT * P]) for i in two]
        fk = [sb(f"fk{i}", [P, HA, OFF, DA]) for i in two]
        fq = [sb(f"fq{i}", [P, HA, OFF, DA]) for i in two]
        fqT = [sb(f"fqT{i}", [P, FB, P]) for i in two]
        state = [sb(f"state{i}", [P, FB, D]) for i in two]
        pat = [sb(f"pat{i}", [P, HA, P]) for i in two]
        zT = sb("zT", [P, P])
        y1T = sb("y1T", [P, TT * P])
        lg = sb("lg", [P, TT, E])
        top = sb("top", [P, TT])
        sh = sb("sh", [P, TT, E])
        ge = sb("ge", [P, TT, E])
        gs = sb("gs", [P, TT])
        gr = sb("gr", [P, TT])
        pick = sb("pick", [P, TT, E])
        best = sb("best", [P, TT])
        oh = sb("oh", [P, TT, E])
        ohb = sb("ohb", [P, TT, E], BF16)
        loc = sb("loc", [P, TT, E])
        keep = sb("keep", [P, TT, E])
        w = sb("w", [P, TT, E])
        wT = sb("wT", [TT * E, P])
        acc = [sb(f"acc{i}", [P, TT, D]) for i in two]
        stats2, mv2, rstd2 = sb("stats2", [P, TT, 6]), sb("mv2", [P, TT, 2]), sb("rstd2", [P, TT])
        z = sb("z", [P, TT, D])
        zg = sb("zg", [P, TT, D])
        zr = sb("zr", [P, TT, D])
        outs = [sb(f"outs{i}", [P, TT, D]) for i in two]

        S_BANKS, G_BANKS, ST_A, ST_B, B_Z, B_OUT = bank[0:2], bank[2:4], bank[4], bank[5], bank[6], bank[7]

        x_loaded = [sem(f"b_x_loaded{i}") for i in two]
        y_loaded = [sem(f"b_y_loaded{i}") for i in two]
        stored = [Signal(sem(f"b_stored{i}"), 0) for i in two]
        passed = sem("passed")
        zeroed = Signal(sem("b_zeroed"), 1)
        alone = sem("b_alone")
        s = {n: Signal(sem("b_" + n), per) for n, per in dict(
            stats=TT, mv=TT, veps=1, rstd=1, xn=TT, xxn=1, res=1, xT=1, qkv=TT, qkv_used=1, vm=TT, sq=1, ms=1, lnv=1, r0=1,
            va=1, ra=1, rb=1, rc=1, rr=1, qn=1, t1=TT, t2=2, qr=1, qd=2, qm=GA, kg=GA, q_used=1,
            fk=TT - 1, fq=TT - 1, fqT=2 * (TT - 1), st_full=TT - 1, state=2 * (TT - 1),
            s_full=HA, pat=HA, masked=HA, z_full=TT, z=TT, o_full=TT, y1T=1, lg=1, top=1, sh=1, ge=1, gs=1, gr=1,
            pick=1, best=1, oh=1, ohb=1, loc=1, keep=1, w=1, carry=1, wT=1, acc=TT * E, ym=1,
            stats2=TT, mv2=TT, veps2=1, rstd2=1, z2=TT, zg=1, zr=1, outs=1).items()}

        NEXT = ["xT'", "qkv'0", "qkv'1", "qkv'2", "qkv'3", "q'", "k'"]
        TURNS = ["fq1a", "fq1b", "xT'", "fq2a", "fq2b", "qkv'0", "qkv'1", "qkv'2", "qkv'3", "fq3a", "fq3b",
                 "y1T", "lg", "rank", "wT", "q'", "k'"] + [f"y{c}{h}" for c in range(TT) for h in "ab"] + ["bias"]
        LAST = [n for n in TURNS if n not in NEXT]

        MOVED = {"xT'": ("xT", 1, 1), "q'": ("qm", GA, 1), "k'": ("kg", GA, 1), "y1T": ("y1T", 1, 0), "lg": ("lg", 1, 0),
                 "rank": ("carry", 1, 0), "wT": ("wT", 1, 0), "bias": ("ym", 1, 0)}
        MOVED.update({f"qkv'{c}": ("qkv", c + 1, 1) for c in range(TT)})
        MOVED.update({f"fq{c}{h}": ("fqT", 2 * c - 1 + (h == "b"), 0) for c in range(1, TT) for h in "ab"})
        MOVED.update({f"y{c}{h}": ("acc", E * c + E // 2 * (1 + (h == "b")), 0) for c in range(TT) for h in "ab"})
        assert len(TURNS) % 2 == 0

        class Turn:

            def __init__(self, b, names, name):
                k = names.index(name)
                self.to = G_BANKS[k % 2]
                if names is NEXT:
                    self.full = k + 1
                else:
                    self.full = b.i * (2 * len(TURNS)) + b.off * len(TURNS) + len(NEXT) + k + 1
                before, of = (names[k - 2], b if names is not NEXT else b.prev()) if k >= 2 else (TURNS[k - 2], b.prev())
                signal, n, ahead = MOVED[before]
                self.prior = s[signal]
                self.moved = self.prior.by(of.next() if ahead else of, n)

        xv = x.rearrange("b (c p) d -> b p c d", p=P)
        yv = y1_dram.rearrange("b (c p) d -> b p c d", p=P)
        ov = out.rearrange("b (c p) d -> b p c d", p=P)
        LASTB = NB // 2 - 1
        block = ctx.enter_context(nc.Block())

        @block.sync
        def _(sp):
            def load(b, wait=True):
                if wait:
                    sp.wait_ge(s["res"].sem, s["res"].by(b.prev().prev()))
                sp.dma_start(xs[b.parity][:], xv[b.number]).then_inc(x_loaded[b.parity], 16)
                if wait:
                    sp.wait_ge(s["ym"].sem, s["ym"].by(b.prev().prev()))
                sp.dma_start(y1[b.parity][:], yv[b.number]).then_inc(y_loaded[b.parity], 16)

            def store(b):
                sp.wait_ge(s["outs"].sem, s["outs"].by(b))
                sp.dma_start(ov[b.number], outs[b.parity][:]).then_inc(stored[b.parity].sem, 16)

            for o in two:
                load(Batch(0, o), wait=False)
            start(sp, [*s.values(), zeroed, *stored])
            with sp.Fori(0, LASTB) as i:
                for o in two:
                    load(Batch(i, o + 2))
                    store(Batch(i, o))
            for o in two:
                store(Batch(LASTB, o))
            for o in two:
                sp.wait_ge(stored[o].sem, 16 * (NB // 2) + 1)

        @block.tensor
        def _(pe):
            def pe_xT(b, turn):
                pe.wait_ge(s["xn"].sem, s["xn"].by(b))
                pe.wait_ge(turn.prior.sem, turn.moved)
                to = turn.to
                for c in range(TT):
                    last = nc.tensor.transpose(to[:, c * P:(c + 1) * P], xn[:, c, :], ident[:])
                last.then_inc(passed, 1)

            def pe_qkv(b, c, turn):
                pe.wait_ge(s["xT"].sem, s["xT"].by(b))
                pe.wait_ge(turn.prior.sem, turn.moved)
                to = turn.to
                nc.tensor.matmul(to[:, 0:3 * D], xT[:, c * P:(c + 1) * P], wqkvT[:], start=True, stop=True).then_inc(passed, 1)

            def pe_turn_qk(b, which, turn):
                pe.wait_ge(s["qr"].sem, s["qr"].by(b))
                pe.wait_ge(turn.prior.sem, turn.moved)
                to = turn.to
                for c in range(TT):
                    last = nc.tensor.transpose(to[:, c * P:(c + 1) * P], qr[:, c, which * D:(which + 1) * D], ident[:])
                last.then_inc(passed, 1)

            def pe_scores(b, c):
                pe.wait_ge(s["qm"].sem, s["qm"].by(b))
                pe.wait_ge(s["kg"].sem, s["kg"].by(b))
                for g in range(GA):
                    n = c * GA + g
                    if n >= 2:
                        pe.wait_ge(s["pat"].sem, s["pat"].by(b, n - 1))
                    else:
                        pe.wait_ge(s["pat"].sem, s["pat"].by(b.prev()))
                    last = nc.tensor.matmul(S_BANKS[n % 2][:].rearrange("p (j q) -> p j q", j=GA), kg[b.parity][:, g, c * P:(c + 1) * P],
                                            qm[b.parity][:, :, c * P:(c + 1) * P], start=True, stop=True)
                    last.then_inc(s["s_full"].sem, 1)

            def pe_fq(b, c, turns):
                pe.wait_ge(s["fq"].sem, s["fq"].by(b, c))
                for k in range(FB):
                    turn = turns[k // 4]
                    if k % 4 == 0:
                        pe.wait_ge(turn.prior.sem, turn.moved)
                        to = turn.to
                    last = nc.tensor.transpose(to[:, k % 4 * P:(k % 4 + 1) * P], fq[(c + 1) % 2][:].rearrange("p h o i -> p (h o i)")[:, k * P:(k + 1) * P], ident[:])
                    if k in (3, FB - 1):
                        last.then_inc(passed, 1)

            def pe_state(b, c):
                pe.wait_ge(s["fk"].sem, s["fk"].by(b, c + 1))
                if c == 0:
                    pe.wait_ge(s["state"].sem, s["state"].by(b.prev()))
                else:
                    pe.wait_ge(s["state"].sem, s["state"].by(b, 2 * c))
                for k in range(FB):
                    to = ST_A[:, k * P:(k + 1) * P] if k < 4 else ST_B[:, 0:P]
                    last = nc.tensor.matmul(to, fk[c % 2][:].rearrange("p h o i -> p (h o i)")[:, k * P:(k + 1) * P],
                                            qkv[b.parity][:, c, 2 * D:3 * D], start=(c == 0 and k in (0, 4)), stop=(c == TT - 2),
                                            skip_group_check=True)
                last.then_inc(s["st_full"].sem, 1)

            def pe_values(b, c):
                if c == 0:
                    pe.wait_ge(s["z"].sem, s["z"].by(b.prev()))
                else:
                    pe.wait_ge(s["z"].sem, s["z"].by(b, c))
                    pe.wait_ge(s["fqT"].sem, s["fqT"].by(b, 2 * c))
                    pe.wait_ge(s["state"].sem, s["state"].by(b, 2 * c))
                    for k in range(FB):
                        nc.tensor.matmul(B_Z[:, 0:P], state[(c - 1) % 2][:, k, :], fqT[(c + 1) % 2][:, k, :], start=(k == 0), stop=False,
                                         skip_group_check=True)
                pe.wait_ge(s["vm"].sem, s["vm"].by(b))
                pe.wait_ge(s["masked"].sem, s["masked"].by(b, GA * (c + 1)))
                for j in range(GA):
                    for g in range(GA):
                        last = nc.tensor.matmul(B_Z[32 * g:32 * g + 32, 0:P], vm[b.parity][:, c, g * GA + j, :],
                                                pat[c % 2][:, g * GA + j, :], start=(c == 0 and j == 0), stop=(j == GA - 1),
                                                skip_group_check=True)
                last.then_inc(s["z_full"].sem, 1)

            def pe_out(b, c):
                pe.wait_ge(s["z"].sem, s["z"].by(b, c + 1))
                if c == 0:
                    pe.wait_ge(s["outs"].sem, s["outs"].by(b.prev()))
                nc.tensor.matmul(B_OUT[:, c * D:(c + 1) * D], zT[:], woT[:], start=True, stop=True).then_inc(s["o_full"].sem, 1)

            def pe_y1T(b, turn):
                pe.wait_ge(y_loaded[b.parity], b.i * 16 + 16 * (b.off // 2 + 1))
                pe.wait_ge(turn.prior.sem, turn.moved)
                to = turn.to
                for c in range(TT):
                    last = nc.tensor.transpose(to[:, c * P:(c + 1) * P], y1[b.parity][:, c, :], ident[:])
                last.then_inc(passed, 1)

            def pe_logits(b, turn):
                pe.wait_ge(s["y1T"].sem, s["y1T"].by(b))
                pe.wait_ge(turn.prior.sem, turn.moved)
                to = turn.to
                for c in range(TT):
                    last = nc.tensor.matmul(to[:, c * E:(c + 1) * E], y1T[:, c * P:(c + 1) * P], wg[:], start=True, stop=True)
                last.then_inc(passed, 1)

            def pe_rank(b, turn):
                pe.wait_ge(s["ohb"].sem, s["ohb"].by(b))
                pe.wait_ge(turn.prior.sem, turn.moved)
                to = turn.to
                o2 = ohb[:].rearrange("p c e -> p (c e)")
                nc.tensor.matmul(to[:, 0:TT * E], upper[:], o2, start=True, stop=False, skip_group_check=True)
                for d in range(1, TT):
                    nc.tensor.matmul(to[:, d * E:TT * E], ones[:], o2[:, 0:(TT - d) * E], start=False, stop=False, skip_group_check=True)
                for c in range(TT):
                    last = nc.tensor.matmul(to[:, TT * E:(TT + 1) * E], ones[:], o2[:, c * E:(c + 1) * E], start=False, stop=(c == TT - 1),
                                            skip_group_check=True)
                last.then_inc(passed, 1)

            def pe_wT(b, turn):
                pe.wait_ge(s["w"].sem, s["w"].by(b))
                pe.wait_ge(turn.prior.sem, turn.moved)
                to = turn.to
                nc.tensor.transpose(to[0:TT * E, 0:P], w[:].rearrange("p c e -> p (c e)"), ident[:]).then_inc(passed, 1)

            def pe_expert(b, c, half, turn):
                pe.wait_ge(turn.prior.sem, turn.moved)
                to = turn.to
                nc.tensor.matmul(to[:], y1T[:, c * P:(c + 1) * P], mexp[:, half * 512:(half + 1) * 512], start=True, stop=True)\
                    .then_inc(passed, 1)

            def pe_bias(b, turn):
                pe.wait_ge(s["wT"].sem, s["wT"].by(b))
                pe.wait_ge(turn.prior.sem, turn.moved)
                to = turn.to
                for c in range(TT):
                    last = nc.tensor.matmul(to[:, c * D:(c + 1) * D], wT[:], cpad[:, c, :], start=True, stop=True)
                last.then_inc(passed, 1)

            def body(b, names):
                def T(name):
                    return Turn(b, names, name)

                n, more = b.next(), names is TURNS
                pe_scores(b, 0)
                pe_fq(b, 1, (T("fq1a"), T("fq1b")))
                pe_state(b, 0)
                pe_scores(b, 1)
                if more:
                    pe_xT(n, T("xT'"))
                pe_values(b, 0)
                pe_fq(b, 2, (T("fq2a"), T("fq2b")))
                pe_state(b, 1)
                pe_out(b, 0)
                if more:
                    pe_qkv(n, 0, T("qkv'0"))
                    pe_qkv(n, 1, T("qkv'1"))
                pe_scores(b, 2)
                pe_values(b, 1)
                if more:
                    pe_qkv(n, 2, T("qkv'2"))
                    pe_qkv(n, 3, T("qkv'3"))
                pe_fq(b, 3, (T("fq3a"), T("fq3b")))
                pe_state(b, 2)
                pe_out(b, 1)
                pe_y1T(b, T("y1T"))
                pe_logits(b, T("lg"))
                pe_scores(b, 3)
                pe_values(b, 2)
                pe_rank(b, T("rank"))
                pe_out(b, 2)
                pe_wT(b, T("wT"))
                if more:
                    pe_turn_qk(n, 0, T("q'"))
                    pe_turn_qk(n, 1, T("k'"))
                pe_values(b, 3)
                for c in range(TT):
                    pe_expert(b, c, 0, T(f"y{c}a"))
                    pe_expert(b, c, 1, T(f"y{c}b"))
                    if c == 0:
                        pe_out(b, 3)
                pe_bias(b, T("bias"))

            b0 = Batch(0, 0)
            T = lambda name: Turn(b0, NEXT, name)
            pe_xT(b0, T("xT'"))
            for c in range(TT):
                pe_qkv(b0, c, T(f"qkv'{c}"))
            pe_turn_qk(b0, 0, T("q'"))
            pe_turn_qk(b0, 1, T("k'"))
            with pe.Fori(0, LASTB) as i:
                for o in two:
                    body(Batch(i, o), TURNS)
            body(Batch(LASTB, 0), TURNS)
            body(Batch(LASTB, 1), LAST)

        @block.scalar
        def _(act):
            def act_xT(b, turn):
                act.wait_ge(passed, turn.full)
                src = turn.to
                act.wait_ge(s["qkv"].sem, s["qkv"].by(b.prev()))
                nc.scalar.activation(xT[:], src[:], ACT.Copy).then_inc(s["xT"].sem, 1)

            def act_vm(b):
                act.wait_ge(s["qkv"].sem, s["qkv"].by(b))
                for c in range(TT):
                    to = bass.AP(vm[b.parity], c * HA * 32, [[TT * HA * 32, P], [GA * 32, GA], [32 + DA, GA], [1, DA]])
                    nc.scalar.activation(to, qkv[b.parity][:, c, 2 * D:3 * D].rearrange("p (g j d) -> p g j d", g=GA, j=GA), ACT.Copy).then_inc(s["vm"].sem, 1)

            def act_square_qk(b):
                act.wait_ge(s["qkv"].sem, s["qkv"].by(b))
                act.wait_ge(s["ms"].sem, s["ms"].by(b.prev()))
                nc.scalar.activation(sq[:].rearrange("p c h d -> p c (h d)"), qkv[b.parity][:, :, 0:2 * D], ACT.Square).then_inc(s["sq"].sem, 1)

            def act_rsqrt(b):
                act.wait_ge(s["ms"].sem, s["ms"].by(b))
                act.wait_ge(s["rr"].sem, s["rr"].by(b.prev()))
                nc.scalar.activation(lnv[:], ms[:], ACT.Ln, bias=eps[:], scale=1.0 / DA).then_inc(s["lnv"].sem, 1)
                act.wait_ge(s["lnv"].sem, s["lnv"].by(b))
                nc.scalar.activation(r0[:], lnv[:], ACT.Exp, scale=-0.5).then_inc(s["r0"].sem, 1)

            def act_double(b):
                act.wait_ge(s["qr"].sem, s["qr"].by(b))
                src = qr[:].rearrange("p c (h d) -> p (c h) d", d=DA)
                to = qd[b.parity][:].rearrange("p c h d -> p (c h) d")
                nc.scalar.activation(to[:, :, 0:DA], src, ACT.Copy).then_inc(s["qd"].sem, 1)
                nc.scalar.activation(to[:, :, DA:DA + OFF - 1], src[:, :, 0:OFF - 1], ACT.Copy).then_inc(s["qd"].sem, 1)

            def act_kg(b, turn):
                act.wait_ge(passed, turn.full)
                src = turn.to
                for g in range(GA):
                    r = slice(32 * g, 32 * g + 32)
                    nc.scalar.activation(kg[b.parity][r, g, :], src[r, :], ACT.Copy).then_inc(s["kg"].sem, 1)

            def act_square(b, c):
                for g in range(GA):
                    n = GA * c + g
                    act.wait_ge(s["s_full"].sem, s["s_full"].by(b, n + 1))
                    if g == 0 and c >= 2:
                        act.wait_ge(s["z_full"].sem, s["z_full"].by(b, c - 1))
                    elif g == 0:
                        act.wait_ge(s["z_full"].sem, s["z_full"].by(b.prev()))
                    nc.scalar.activation(pat[c % 2][:, g * GA:(g + 1) * GA, :].rearrange("p j q -> p (j q)"), S_BANKS[n % 2][:],
                                         ACT.Square, scale=1.0 / DA).then_inc(s["pat"].sem, 1)

            def act_fqT(b, c, turns):
                for k, turn in enumerate(turns):
                    act.wait_ge(passed, turn.full)
                    src = turn.to
                    if c == 3:
                        act.wait_ge(s["z_full"].sem, s["z_full"].by(b, c - 1))
                    else:
                        act.wait_ge(s["z_full"].sem, s["z_full"].by(b.prev()))
                    wide = 4 if k == 0 else FB - 4
                    nc.scalar.activation(fqT[(c + 1) % 2][:, 4 * k:4 * k + wide, :].rearrange("p k q -> p (k q)"), src[:, 0:wide * P],
                                         ACT.Copy).then_inc(s["fqT"].sem, 1)

            def act_zT(b, c):
                act.wait_ge(s["z_full"].sem, s["z_full"].by(b, c + 1))
                if c:
                    act.wait_ge(s["o_full"].sem, s["o_full"].by(b, c))
                else:
                    act.wait_ge(s["o_full"].sem, s["o_full"].by(b.prev()))
                nc.scalar.activation(zT[:], B_Z[:, 0:P], ACT.Copy).then_inc(s["z"].sem, 1)

            def act_y1T(b, turn):
                act.wait_ge(passed, turn.full)
                src = turn.to
                act.wait_ge(s["acc"].sem, s["acc"].by(b.prev()))
                nc.scalar.activation(y1T[:], src[:], ACT.Copy).then_inc(s["y1T"].sem, 1)

            def act_gate(b):
                act.wait_ge(s["sh"].sem, s["sh"].by(b))
                act.wait_ge(s["gs"].sem, s["gs"].by(b.prev()))
                nc.scalar.activation(ge[:], sh[:], ACT.Exp).then_inc(s["ge"].sem, 1)

            def act_wT(b, turn):
                act.wait_ge(passed, turn.full)
                src = turn.to
                act.wait_ge(s["ym"].sem, s["ym"].by(b.prev()))
                nc.scalar.activation(wT[:], src[0:TT * E, 0:P], ACT.Copy).then_inc(s["wT"].sem, 1)

            def body(b, names):
                def T(name):
                    return Turn(b, names, name)

                n, more = b.next(), names is TURNS
                act_square(b, 0)
                act_fqT(b, 1, (T("fq1a"), T("fq1b")))
                act_square(b, 1)
                if more:
                    act_xT(n, T("xT'"))
                act_zT(b, 0)
                act_fqT(b, 2, (T("fq2a"), T("fq2b")))
                act_square(b, 2)
                act_zT(b, 1)
                act_fqT(b, 3, (T("fq3a"), T("fq3b")))
                if more:
                    act_square_qk(n)
                act_y1T(b, T("y1T"))
                if more:
                    act_vm(n)
                act_gate(b)
                if more:
                    act_rsqrt(n)
                act_square(b, 3)
                act_zT(b, 2)
                act_wT(b, T("wT"))
                if more:
                    act_double(n)
                    act_kg(n, T("k'"))
                act_zT(b, 3)

            act.preload_act_table_set("natural_log_exp_and_others")
            act.wait_ge(zeroed.sem, zeroed.by(Batch(0, 0), 1))
            b0 = Batch(0, 0)
            act_xT(b0, Turn(b0, NEXT, "xT'"))
            act_square_qk(b0)
            act_vm(b0)
            act_rsqrt(b0)
            act_double(b0)
            act_kg(b0, Turn(b0, NEXT, "k'"))
            with act.Fori(0, LASTB) as i:
                for o in two:
                    body(Batch(i, o), TURNS)
            body(Batch(LASTB, 0), TURNS)
            body(Batch(LASTB, 1), LAST)

        @block.gpsimd
        def _(pool):
            def pool_mask(b, c):
                for g in range(GA):
                    pool.wait_ge(s["pat"].sem, s["pat"].by(b, GA * c + g + 1))
                    pool.sem_inc(alone, 1)
                    part = pat[c % 2][:, g * GA:(g + 1) * GA, :]
                    nc.gpsimd.affine_select(out=part, in_=part, compare_op=ALU.is_ge, fill=zero, base=0,
                                            pattern=[[0, GA], [1, P]], channel_multiplier=-1).then_inc(s["masked"].sem, 1)

            def pool_rstd(b):
                pool.wait_ge(s["mv"].sem, s["mv"].by(b))
                pool.wait_ge(s["xn"].sem, s["xn"].by(b.prev()))
                nc.gpsimd.tensor_tensor(rstd[:], mv[:, :, 1], lneps[:], ALU.add).then_inc(s["veps"].sem, 1)
                pool.wait_ge(s["veps"].sem, s["veps"].by(b))
                nc.gpsimd.tensor_tensor(rstd[:], rstd[:], mhalf[:], ALU.pow).then_inc(s["rstd"].sem, 1)

            def pool_newton(b):
                pool.wait_ge(s["ms"].sem, s["ms"].by(b))
                pool.sem_inc(alone, 1)
                nc.gpsimd.tensor_scalar(va[:], ms[:], 1.0 / DA, RMS_EPS, ALU.mult, ALU.add).then_inc(s["va"].sem, 1)
                pool.wait_ge(s["r0"].sem, s["r0"].by(b))
                nc.gpsimd.tensor_tensor(ra[:], r0[:], r0[:], ALU.mult).then_inc(s["ra"].sem, 1)
                pool.wait_ge(s["va"].sem, s["va"].by(b))
                pool.wait_ge(s["ra"].sem, s["ra"].by(b))
                nc.gpsimd.tensor_tensor(rb[:], ra[:], va[:], ALU.mult).then_inc(s["rb"].sem, 1)
                pool.wait_ge(s["rb"].sem, s["rb"].by(b))
                pool.sem_inc(alone, 1)
                nc.gpsimd.tensor_scalar(rc[:], rb[:], -0.5, 1.5, ALU.mult, ALU.add).then_inc(s["rc"].sem, 1)
                pool.wait_ge(s["rc"].sem, s["rc"].by(b))
                pool.wait_ge(s["qn"].sem, s["qn"].by(b.prev()))
                nc.gpsimd.tensor_tensor(rr[:], rc[:], r0[:], ALU.mult).then_inc(s["rr"].sem, 1)

            def pool_cos(b):
                pool.wait_ge(s["qn"].sem, s["qn"].by(b))
                pool.wait_ge(s["qr"].sem, s["qr"].by(b.prev()))
                for c in range(TT):
                    nc.gpsimd.tensor_tensor(t1[:, c], qn[:, c], rope[:, 0, c, :].unsqueeze(1).broadcast_to([P, H2, DA]), ALU.mult).then_inc(s["t1"].sem, 1)

            def pool_rstd2(b):
                pool.wait_ge(s["mv2"].sem, s["mv2"].by(b))
                pool.wait_ge(s["z2"].sem, s["z2"].by(b.prev()))
                nc.gpsimd.tensor_tensor(rstd2[:], mv2[:, :, 1], lneps[:], ALU.add).then_inc(s["veps2"].sem, 1)
                pool.wait_ge(s["veps2"].sem, s["veps2"].by(b))
                nc.gpsimd.tensor_tensor(rstd2[:], rstd2[:], mhalf[:], ALU.pow).then_inc(s["rstd2"].sem, 1)

            def pool_gain(b):
                pool.wait_ge(s["z2"].sem, s["z2"].by(b))
                pool.wait_ge(s["zr"].sem, s["zr"].by(b.prev()))
                nc.gpsimd.tensor_tensor(zg[:], z[:], ln[:, 2, :].unsqueeze(1).broadcast_to([P, TT, D]), ALU.mult).then_inc(s["zg"].sem, 1)

            def body(b, more):
                n = b.next()
                pool_mask(b, 0)
                if more:
                    pool_rstd(n)
                pool_mask(b, 1)
                pool_mask(b, 2)
                if more:
                    pool_newton(n)
                pool_mask(b, 3)
                if more:
                    pool_cos(n)
                pool_rstd2(b)
                pool_gain(b)

            for i in two:
                nc.gpsimd.memset(vm[i][:], 0.0)
                last = nc.gpsimd.memset(kg[i][:], 0.0)
            last.then_inc(zeroed.sem, 1)
            pool.wait_ge(zeroed.sem, zeroed.by(Batch(0, 0), 1))
            zero = pool.to_reg(0.0)
            b0 = Batch(0, 0)
            pool_rstd(b0)
            pool_newton(b0)
            pool_cos(b0)
            with pool.Fori(0, LASTB) as i:
                for o in two:
                    body(Batch(i, o), True)
            body(Batch(LASTB, 0), True)
            body(Batch(LASTB, 1), False)

        @block.vector
        def _(dve):
            def dve_stats(b):
                dve.wait_ge(x_loaded[b.parity], b.i * 16 + 16 * (b.off // 2 + 1))
                dve.wait_ge(s["veps"].sem, s["veps"].by(b.prev()))
                for c in range(TT):
                    nc.vector.bn_stats(stats[:, c, :], xs[b.parity][:, c, :]).then_inc(s["stats"].sem, 1)
                dve.wait_ge(s["stats"].sem, s["stats"].by(b))
                dve.sem_inc(alone, 1)
                for c in range(TT):
                    nc.vector.bn_aggr(mv[:, c, :], stats[:, c, :]).then_inc(s["mv"].sem, 1)

            def dve_xn(b):
                dve.wait_ge(s["rstd"].sem, s["rstd"].by(b))
                dve.wait_ge(s["xT"].sem, s["xT"].by(b.prev()))
                dve.wait_ge(s["xxn"].sem, s["xxn"].by(b.prev()))
                for c in range(TT):
                    nc.vector.tensor_scalar(xn[:, c, :], xs[b.parity][:, c, :], mv[:, c, 0:1], rstd[:, c:c + 1],
                                            ALU.subtract, ALU.mult).then_inc(s["xn"].sem, 1)

            def dve_res(b):
                dve.wait_ge(s["xn"].sem, s["xn"].by(b))
                dve.wait_ge(s["zr"].sem, s["zr"].by(b.prev().prev()))
                nc.vector.tensor_tensor(res[b.parity][:], xs[b.parity][:], xn[:], ALU.add).then_inc(s["xxn"].sem, 1)
                dve.wait_ge(s["xxn"].sem, s["xxn"].by(b))
                nc.vector.tensor_tensor(res[b.parity][:], res[b.parity][:], ln[:, 3, :].unsqueeze(1).broadcast_to([P, TT, D]),
                                        ALU.add).then_inc(s["res"].sem, 1)

            def dve_qkv(b, c, turn):
                dve.wait_ge(passed, turn.full)
                src = turn.to
                if c == 0:
                    dve.wait_ge(s["z_full"].sem, s["z_full"].by(b.prev().prev()))
                    dve.wait_ge(s["qr"].sem, s["qr"].by(b.prev().prev()))
                nc.vector.tensor_tensor(qkv[b.parity][:, c, :], src[:, 0:3 * D], bqkv[:], ALU.add).then_inc(s["qkv"].sem, 1)

            def dve_ms(b):
                dve.wait_ge(s["sq"].sem, s["sq"].by(b))
                dve.wait_ge(s["rr"].sem, s["rr"].by(b.prev()))
                nc.vector.tensor_reduce(ms[:], sq[:], AX, ALU.add).then_inc(s["ms"].sem, 1)

            def dve_qn(b):
                dve.wait_ge(s["rr"].sem, s["rr"].by(b))
                dve.wait_ge(s["qr"].sem, s["qr"].by(b.prev()))
                nc.vector.tensor_tensor(qn[:], qkv[b.parity][:, :, 0:2 * D].rearrange("p c (h d) -> p c h d", d=DA),
                                        rr[:].unsqueeze(3).broadcast_to([P, TT, H2, DA]), ALU.mult).then_inc(s["qn"].sem, 1)

            def dve_rope(b):
                dve.wait_ge(s["qn"].sem, s["qn"].by(b))
                for e in two:
                    nc.vector.tensor_tensor(t2[:, :, :, e::2], qn[:, :, :, 1 - e::2],
                                            rope[:, 1, :, e::2].unsqueeze(2).broadcast_to([P, TT, H2, DA // 2]), ALU.mult).then_inc(s["t2"].sem, 1)
                dve.wait_ge(s["t2"].sem, s["t2"].by(b))
                dve.wait_ge(s["t1"].sem, s["t1"].by(b))
                dve.wait_ge(s["qd"].sem, s["qd"].by(b.prev()))
                dve.wait_ge(s["kg"].sem, s["kg"].by(b.prev()))
                dve.wait_ge(s["qm"].sem, s["qm"].by(b.prev()))
                nc.vector.tensor_tensor(qr[:].rearrange("p c (h d) -> p c h d", d=DA), t1[:], t2[:], ALU.add).then_inc(s["qr"].sem, 1)

            def dve_qm(b, turn):
                dve.wait_ge(passed, turn.full)
                src = turn.to
                for j in range(GA):
                    nc.vector.tensor_scalar(qm[b.parity][:, j, :], src[:], jmask[:, j:j + 1], None, ALU.mult).then_inc(s["qm"].sem, 1)

            def features(to, b, c, which):
                wide = H2 * (DA + OFF - 1)
                base = (c * H2 + which * HA) * (DA + OFF - 1)
                dims = [[TT * wide, P], [DA + OFF - 1, HA]]
                a0 = bass.AP(qd[b.parity], base, dims + [[0, OFF], [1, DA]])
                a1 = bass.AP(qd[b.parity], base, dims + [[1, OFF], [1, DA]])
                return nc.vector.tensor_tensor(to[:], a0, a1, ALU.mult)

            def dve_fk(b, c):
                dve.wait_ge(s["qd"].sem, s["qd"].by(b))
                if c == 2:
                    dve.wait_ge(s["st_full"].sem, s["st_full"].by(b, 1))
                else:
                    dve.wait_ge(s["st_full"].sem, s["st_full"].by(b.prev()))
                features(fk[c % 2], b, c, 1).then_inc(s["fk"].sem, 1)

            def dve_fq(b, c):
                if c == 3:
                    dve.wait_ge(s["fqT"].sem, s["fqT"].by(b, 2))
                else:
                    dve.wait_ge(s["fqT"].sem, s["fqT"].by(b.prev()))
                features(fq[(c + 1) % 2], b, c, 0).then_inc(s["fq"].sem, 1)

            def dve_state(b, c):
                dve.wait_ge(s["st_full"].sem, s["st_full"].by(b, c + 1))
                if c == 2:
                    dve.wait_ge(s["z_full"].sem, s["z_full"].by(b, 2))
                else:
                    dve.wait_ge(s["z_full"].sem, s["z_full"].by(b.prev()))
                nc.vector.tensor_tensor(state[c % 2][:, 0:4, :], ST_A[:].rearrange("p (k d) -> p k d", k=4), featw[:, 0:4, :], ALU.mult)\
                    .then_inc(s["state"].sem, 1)
                nc.vector.tensor_tensor(state[c % 2][:, 4, :], ST_B[:, 0:P], featw[:, 4, :], ALU.mult).then_inc(s["state"].sem, 1)

            def dve_gate(b, turn):
                dve.wait_ge(passed, turn.full)
                src = turn.to
                dve.wait_ge(s["sh"].sem, s["sh"].by(b.prev()))
                nc.vector.tensor_copy(lg[:].rearrange("p c e -> p (c e)"), src[:, 0:TT * E]).then_inc(s["lg"].sem, 1)
                dve.wait_ge(s["lg"].sem, s["lg"].by(b))
                nc.vector.tensor_reduce(top[:], lg[:], AX, ALU.max).then_inc(s["top"].sem, 1)
                dve.wait_ge(s["top"].sem, s["top"].by(b))
                dve.wait_ge(s["ge"].sem, s["ge"].by(b.prev()))
                nc.vector.tensor_tensor(sh[:], lg[:], top[:].unsqueeze(2).broadcast_to([P, TT, E]), ALU.subtract).then_inc(s["sh"].sem, 1)
                dve.wait_ge(s["sh"].sem, s["sh"].by(b))
                nc.vector.scalar_tensor_tensor(out=pick[:], in0=sh[:], scalar=0.0, in1=first[:].unsqueeze(1).broadcast_to([P, TT, E]),
                                               op0=ALU.is_equal, op1=ALU.mult).then_inc(s["pick"].sem, 1)
                dve.wait_ge(s["pick"].sem, s["pick"].by(b))
                nc.vector.tensor_reduce(best[:], pick[:], AX, ALU.max).then_inc(s["best"].sem, 1)
                dve.wait_ge(s["best"].sem, s["best"].by(b))
                nc.vector.tensor_tensor(oh[:], pick[:], best[:].unsqueeze(2).broadcast_to([P, TT, E]), ALU.is_equal).then_inc(s["oh"].sem, 1)
                dve.wait_ge(s["oh"].sem, s["oh"].by(b))
                nc.vector.tensor_copy(ohb[:], oh[:]).then_inc(s["ohb"].sem, 1)
                dve.wait_ge(s["ge"].sem, s["ge"].by(b))
                nc.vector.tensor_reduce(gs[:], ge[:], AX, ALU.add).then_inc(s["gs"].sem, 1)
                dve.wait_ge(s["gs"].sem, s["gs"].by(b))
                nc.vector.reciprocal(gr[:], gs[:]).then_inc(s["gr"].sem, 1)

            def dve_rank(b, turn):
                dve.wait_ge(passed, turn.full)
                src = turn.to
                nc.vector.tensor_tensor(loc[:], src[:, 0:TT * E].rearrange("p (c e) -> p c e", c=TT),
                                        carry[:].unsqueeze(1).broadcast_to([P, TT, E]), ALU.add).then_inc(s["loc"].sem, 1)
                dve.wait_ge(s["loc"].sem, s["loc"].by(b))
                nc.vector.tensor_tensor(carry[:], src[:, TT * E:(TT + 1) * E], carry[:], ALU.add).then_inc(s["carry"].sem, 1)
                nc.vector.scalar_tensor_tensor(out=keep[:], in0=loc[:], scalar=float(CAP), in1=oh[:], op0=ALU.is_lt, op1=ALU.mult).then_inc(s["keep"].sem, 1)
                dve.wait_ge(s["keep"].sem, s["keep"].by(b))
                dve.wait_ge(s["gr"].sem, s["gr"].by(b))
                dve.wait_ge(s["acc"].sem, s["acc"].by(b.prev()))
                nc.vector.tensor_tensor(w[:], keep[:], gr[:].unsqueeze(2).broadcast_to([P, TT, E]), ALU.mult).then_inc(s["w"].sem, 1)

            def dve_expert(b, c, half, turn):
                dve.wait_ge(passed, turn.full)
                src = turn.to
                dve.wait_ge(s["w"].sem, s["w"].by(b))
                for k in range(E // 2):
                    e = half * (E // 2) + k
                    if e:
                        dve.wait_ge(s["acc"].sem, s["acc"].by(b, c * E + e))
                    else:
                        dve.wait_ge(s["z2"].sem, s["z2"].by(b.prev()))
                    prior = y1[b.parity][:, c, :] if e == 0 else acc[(e + 1) % 2][:, c, :]
                    nc.vector.scalar_tensor_tensor(out=acc[e % 2][:, c, :], in0=src[:, k * D:(k + 1) * D], scalar=w[:, c, e:e + 1], in1=prior,
                                                   op0=ALU.mult, op1=ALU.add).then_inc(s["acc"].sem, 1)

            def dve_ln2(b, turn):
                dve.wait_ge(passed, turn.full)
                src = turn.to
                dve.wait_ge(s["acc"].sem, s["acc"].by(b))
                nc.vector.tensor_tensor(acc[0][:], acc[1][:], src[:].rearrange("p (c d) -> p c d", c=TT), ALU.add).then_inc(s["ym"].sem, 1)
                dve.wait_ge(s["ym"].sem, s["ym"].by(b))
                for c in range(TT):
                    nc.vector.bn_stats(stats2[:, c, :], acc[0][:, c, :]).then_inc(s["stats2"].sem, 1)
                dve.wait_ge(s["stats2"].sem, s["stats2"].by(b))
                dve.sem_inc(alone, 1)
                for c in range(TT):
                    nc.vector.bn_aggr(mv2[:, c, :], stats2[:, c, :]).then_inc(s["mv2"].sem, 1)

            def dve_out(b):
                dve.wait_ge(s["rstd2"].sem, s["rstd2"].by(b))
                dve.wait_ge(s["zg"].sem, s["zg"].by(b.prev()))
                for c in range(TT):
                    nc.vector.tensor_scalar(z[:, c, :], acc[0][:, c, :], mv2[:, c, 0:1], rstd2[:, c:c + 1], ALU.subtract, ALU.mult).then_inc(s["z2"].sem, 1)
                dve.wait_ge(s["zg"].sem, s["zg"].by(b))
                nc.vector.tensor_tensor(zr[:], zg[:], res[b.parity][:], ALU.add).then_inc(s["zr"].sem, 1)
                dve.wait_ge(s["zr"].sem, s["zr"].by(b))
                dve.wait_ge(s["o_full"].sem, s["o_full"].by(b))
                done = b.i * 16 + 16 * (b.off // 2)
                if not isinstance(b.i, int) or done > 0:
                    dve.wait_ge(stored[b.parity].sem, done + 1)
                nc.vector.tensor_tensor(outs[b.parity][:], zr[:], B_OUT[:].rearrange("p (c d) -> p c d", c=TT), ALU.add).then_inc(s["outs"].sem, 1)

            def body(b, names):
                def T(name):
                    return Turn(b, names, name)

                n, more = b.next(), names is TURNS
                dve_fk(b, 0)
                dve_fq(b, 1)
                dve_fk(b, 1)
                dve_fq(b, 2)
                if more:
                    dve_stats(n)
                dve_state(b, 0)
                if more:
                    dve_xn(n)
                    dve_res(n)
                dve_state(b, 1)
                dve_fk(b, 2)
                dve_fq(b, 3)
                if more:
                    dve_qkv(n, 0, T("qkv'0"))
                    dve_qkv(n, 1, T("qkv'1"))
                    dve_qkv(n, 2, T("qkv'2"))
                    dve_qkv(n, 3, T("qkv'3"))
                dve_state(b, 2)
                if more:
                    dve_ms(n)
                dve_gate(b, T("lg"))
                if more:
                    dve_qn(n)
                dve_rank(b, T("rank"))
                if more:
                    dve_rope(n)
                    dve_qm(n, T("q'"))
                for c in range(TT):
                    dve_expert(b, c, 0, T(f"y{c}a"))
                    dve_expert(b, c, 1, T(f"y{c}b"))
                dve_ln2(b, T("bias"))
                dve_out(b)

            dve.wait_ge(zeroed.sem, zeroed.by(Batch(0, 0), 1))
            b0 = Batch(0, 0)
            dve_stats(b0)
            dve_xn(b0)
            dve_res(b0)
            for c in range(TT):
                dve_qkv(b0, c, Turn(b0, NEXT, f"qkv'{c}"))
            dve_ms(b0)
            dve_qn(b0)
            dve_rope(b0)
            dve_qm(b0, Turn(b0, NEXT, "q'"))
            with dve.Fori(0, LASTB) as i:
                for o in two:
                    body(Batch(i, o), TURNS)
            body(Batch(LASTB, 0), TURNS)
            body(Batch(LASTB, 1), LAST)


def constants():
    pos = np.arange(NS, dtype=np.float32)
    inv = np.float32(1.0) / np.float32(10000.0) ** (np.arange(0, DA, 2, dtype=np.float32) / np.float32(DA))
    ang = np.outer(pos, inv.astype(np.float32)).astype(np.float32)
    ang = np.concatenate([ang, ang], -1)
    cos, sin = np.cos(ang), np.sin(ang)
    sin[:, 0::2] *= -1
    trig = np.stack([cos, sin]).reshape(2, TT, P, DA).transpose(2, 0, 1, 3)
    row, col = np.arange(P)[:, None], np.arange(P)[None, :]
    f = np.arange(FB * P)
    weight = np.array([1, 2, 2, 2, 1], np.float32)[(f // DA) % OFF] / DA ** 2
    featw = (f[:, None] // (OFF * DA) == col // DA) * weight[:, None]
    return {
        "c_ident": np.eye(P, dtype=np.float32),
        "c_trig": np.ascontiguousarray(trig, dtype=np.float32),
        "c_featw": np.ascontiguousarray(featw.reshape(FB, P, P).transpose(1, 0, 2), dtype=np.float32),
        "c_jmask": (row // DA % GA == np.arange(GA)[None, :]).astype(np.float32),
        "c_blockmask": np.where(row // LB % 2 == np.arange(32)[None, :] // LB, 0.0, NEG).astype(np.float32),
        "c_upper": (row < col).astype(mybir.dt.np(BF16)),
        "c_first": np.broadcast_to(E - np.arange(E), (P, E)).astype(np.float32).copy(),
        "c_tmask": (np.arange(TT * E)[:, None] // E == np.arange(TT)[None, :]).astype(np.float32),
    }


_INS = ["attn_x", "attn_Wq", "attn_bq", "attn_Wk", "attn_bk", "attn_Wv", "attn_bv", "attn_Wo", "attn_norm_w",
        "ffn_in_proj_w", "ffn_in_proj_b", "ffn_out_proj_w", "ffn_out_proj_b", "ffn_ln1_g", "ffn_ln1_b",
        "ffn_ln2_g", "ffn_ln2_b", "ffn_wg", "ffn_w1", "ffn_b1", "ffn_w2", "ffn_b2"]


def laid_out(inputs):
    g = {n.split("_", 1)[1]: np.asarray(inputs["L0_" + n]) for n in _INS}
    fc = FF // P
    arrays = {
        "x": g["x"], "wg": g["wg"], "b2": g["b2"],
        "wqkvT": np.concatenate([g["Wq"].T, g["Wk"].T, g["Wv"].T], 1), "woT": g["Wo"].T,
        "ipT": g["in_proj_w"].T, "opT": g["out_proj_w"].T, "bcol": g["in_proj_b"].reshape(3, P).T,
        "w1T": g["w1"].reshape(E, D, fc, P).transpose(3, 0, 2, 1), "w2": g["w2"].reshape(E, fc, P, D).transpose(2, 0, 1, 3),
        "b1T": g["b1"].reshape(E, fc, P).transpose(2, 0, 1),
    }
    for n in ("bq", "bk", "bv", "norm_w", "out_proj_b", "ln1_g", "ln1_b", "ln2_g", "ln2_b"):
        arrays[n] = g[n]
    arrays = {n: np.ascontiguousarray(a) for n, a in arrays.items()}
    arrays.update(constants())
    return arrays


SCRATCH = (("y1", (LB, NS, D)),)


def kernel(**inputs):
    import concourse.bacc as _bacc
    from concourse.bass_utils import run_bass_kernel_spmd as _run

    nc = _bacc.Bacc("TRN2", target_bir_lowering=False, num_devices=1)
    arrays = {n + "_dram": a for n, a in laid_out(inputs).items()}
    t = {n.removesuffix("_dram"): nc.dram_tensor(n, a.shape, mybir.dt.from_np(a.dtype), kind="ExternalInput").ap() for n, a in arrays.items()}
    t["out"] = nc.dram_tensor("out_dram", (LB, NS, D), F32, kind="ExternalOutput").ap()
    for n, shape in SCRATCH:
        t[n] = nc.dram_tensor(n + "_scratch", shape, F32, kind="Internal").ap()
    build(nc, t)
    r = _run(nc, [arrays], core_ids=[0])
    return r.results[0]["out_dram"]
```

```python
from contextlib import ExitStack

import numpy as np

import concourse.bass as bass
from concourse import mybir

ALU = mybir.AluOpType
ACT = mybir.ActivationFunctionType
F32 = mybir.dt.float32
BF16 = mybir.dt.bfloat16
AX = mybir.AxisListType.X

P = 128
D = 128
LB, NS = 16, 512
TT = 4
NB = LB * NS // (TT * P)
HA, DA = 16, 8
HB, DB = 4, 32
GA = 4
OFF = 5
FB = HA * OFF * DA // P
E, FF = 8, 512
CAP = LB * NS // E
LN_EPS = 1e-5
RMS_EPS = float(np.finfo(np.float32).eps)
NEG = -1e30


class Batch:

    def __init__(self, i, off):
        self.i, self.off = i, off

    def next(self, n=1):
        return Batch(self.i, self.off + n)

    def prev(self):
        return Batch(self.i, self.off - 1)

    @property
    def number(self):
        return self.i * 2 + self.off

    @property
    def parity(self):
        return self.off % 2


class Signal:

    def __init__(self, sem, per):
        self.sem, self.per = sem, per

    def by(self, b, n=None):
        const = b.off * self.per + (self.per if n is None else n) + 1
        if isinstance(b.i, int):
            return max(b.i * 2 * self.per + const, 1)
        assert const >= 1, "a wait below one"
        return b.i * (2 * self.per) + const


def start(eng, signals):
    for sig in signals:
        eng.sem_inc(sig.sem, 1)


def build(nc, t):
    x, out = t["x"], t["out"]
    ctx = ExitStack()
    with ctx:
        def sb(name, shape, dt=F32):
            return ctx.enter_context(nc.sbuf_tensor(name, shape, dt))

        bank = [ctx.enter_context(nc.psum_tensor(f"bank{i}", [P, 512], F32)) for i in range(8)]
        ident = sb("ident", [P, P])
        wqkvT = sb("wqkvT", [P, 3 * D])
        woT = sb("woT", [P, D])
        ipT = sb("ipT", [P, 3 * D])
        opT = sb("opT", [P, D])
        mexp = sb("mexp", [P, E * D])
        cpad = sb("cpad", [TT * E, TT, D])
        wg = sb("wg", [P, E])
        bqkv = sb("bqkv", [P, 3 * D])
        bcol = sb("bcol", [P, 4])
        pbcol = sb("pbcol", [P, 1])
        ln = sb("ln", [P, 4, D])
        nw = sb("nw", [P, DA])
        rope = sb("rope", [P, 2, TT, DA])
        featw = sb("featw", [P, FB, D])
        jmask = sb("jmask", [P, GA])
        blockmask = sb("blockmask", [P, 32])
        upper = sb("upper", [P, P], BF16)
        ones = sb("ones", [P, P], BF16)
        first = sb("first", [P, E])
        mhalf = sb("mhalf", [P, TT])
        lneps = sb("lneps", [P, TT])
        tmask = sb("tmask", [TT * E, TT])
        eps = sb("eps", [P, 1])
        carry = sb("carry", [P, E])

        y1_dram = t["y1"]
        setup(nc, t, bank, locals())
        softmax_attention(nc, t, bank, locals())
        squared_attention_and_experts(nc, t, bank, locals())


def setup(nc, t, bank, m):
    opT, mexp, cpad, rope, nw, tmask = m["opT"], m["mexp"], m["cpad"], m["rope"], m["nw"], m["tmask"]
    FC = FF // P
    ctx = ExitStack()
    with ctx:
        def sb(name, shape, dt=F32):
            return ctx.enter_context(nc.sbuf_tensor(name, shape, dt))

        def sem(name):
            return ctx.enter_context(nc.semaphore(name))

        w1T = sb("w1T", [P, E, FC, D])
        w2 = sb("w2", [P, E, FC, D])
        b1T = sb("b1T", [P, E, FC])
        b1pad = sb("b1pad", [P, E, FC, TT * E])
        b2r = sb("b2r", [TT * E, D])
        c32 = sb("c32", [TT * E, D])
        trig = sb("trig", [P, 2, TT, DA])

        small_loaded, experts_loaded = sem("small_loaded"), sem("experts_loaded")
        small_loads = []
        zeroed, rope_ready, b1pad_ready, pb_full, pb_ready = (
            sem(n) for n in ("zeroed", "rope_ready", "b1pad_ready", "pb_full", "pb_ready"))
        m_full, m_read, c_full, c_ready, cpad_ready = (
            sem(n) for n in ("m_full", "m_read", "c_full", "c_ready", "cpad_ready"))

        block = ctx.enter_context(nc.Block())

        def wide(v):
            return v.rearrange("(a n) -> a n", a=1).broadcast_to([P, v.shape[0]])

        small = [(m["ident"][:], t["c_ident"]), (m["wqkvT"][:], t["wqkvT"]), (m["woT"][:], t["woT"]),
                 (m["ipT"][:], t["ipT"]), (opT[:], t["opT"]), (m["bcol"][:], t["bcol"]), (m["wg"][:], t["wg"]),
                 (nw[:], wide(t["norm_w"])), (trig[:], t["c_trig"]),
                 (m["featw"][:], t["c_featw"]), (m["jmask"][:], t["c_jmask"]), (m["blockmask"][:], t["c_blockmask"]),
                 (m["upper"][:], t["c_upper"]), (m["first"][:], t["c_first"]), (tmask[:], t["c_tmask"])]
        small += [(m["bqkv"][:, i * D:(i + 1) * D], wide(t[n])) for i, n in enumerate(("bq", "bk", "bv"))]
        small += [(m["ln"][:, i, :], wide(t[n])) for i, n in enumerate(("ln1_g", "ln1_b", "ln2_g", "ln2_b"))]
        small += [(b2r[i * E:(i + 1) * E, :], t["b2"]) for i in range(TT)] + [(b1T[:], t["b1T"])]

        @block.sync
        def _(sp):
            for e in range(0, E, 4):
                sp.dma_start(w1T[:, e:e + 4], t["w1T"][:, e:e + 4]).then_inc(experts_loaded, 16)
                sp.dma_start(w2[:, e:e + 4], t["w2"][:, e:e + 4]).then_inc(experts_loaded, 16)

        @block.scalar
        def _(act):
            for d, src in small:
                act.dma_start(d, src).then_inc(small_loaded, 16)

        @block.gpsimd
        def _(pool):
            nc.gpsimd.memset(b1pad[:], 0.0).then_inc(zeroed, 1)
            nc.gpsimd.memset(m["ones"][:], 1.0)
            nc.gpsimd.memset(m["mhalf"][:], -0.5)
            nc.gpsimd.memset(m["lneps"][:], LN_EPS)
            nc.gpsimd.memset(m["eps"][:], RMS_EPS)
            nc.gpsimd.memset(m["carry"][:], 0.0)

        @block.vector
        def _(dve):
            dve.wait_ge(small_loaded, 16 * len(small))
            dve.wait_ge(zeroed, 1)
            for e in range(E):
                nc.vector.tensor_copy(b1pad[:, e, :, e::E], b1T[:, e, :].unsqueeze(2).broadcast_to([P, FC, TT])).then_inc(b1pad_ready, 1)
            for c in range(TT):
                nc.vector.tensor_tensor(rope[:, 0, c, :], trig[:, 0, c, :], nw[:], ALU.mult).then_inc(rope_ready, 1)
                for h in range(2):
                    nc.vector.tensor_tensor(rope[:, 1, c, h::2], trig[:, 1, c, h::2], nw[:, 1 - h::2], ALU.mult).then_inc(rope_ready, 1)
            dve.wait_ge(pb_full, 1)
            nc.vector.tensor_tensor(m["pbcol"][:], bank[5][:, 0:1], m["bcol"][:, 3:4], ALU.add).then_inc(pb_ready, 1)
            for e in range(E):
                dve.wait_ge(m_full, e + 1)
                nc.vector.tensor_copy(mexp[:, e * D:(e + 1) * D], bank[6 + e % 2][:, 0:D]).then_inc(m_read, 1)
            dve.wait_ge(c_full, 1)
            nc.vector.tensor_tensor(c32[:], bank[4][0:TT * E, 0:D], b2r[:], ALU.add).then_inc(c_ready, 1)
            dve.wait_ge(c_ready, 1)
            for i in range(TT):
                nc.vector.tensor_scalar(cpad[:, i, :], c32[:], tmask[:, i:i + 1], None, ALU.mult).then_inc(cpad_ready, 1)
            dve.wait_ge(cpad_ready, TT)
            dve.wait_ge(rope_ready, 3 * TT)
            dve.wait_ge(pb_ready, 1)
            dve.wait_ge(m_read, E)

        @block.tensor
        def _(pe):
            pe.wait_ge(small_loaded, 16 * len(small))
            nc.tensor.matmul(bank[5][:, 0:1], opT[:], m["bcol"][:, 2:3], start=True, stop=True).then_inc(pb_full, 1)
            pe.wait_ge(experts_loaded, 16 * 4)
            for e in range(E):
                if e >= 2:
                    pe.wait_ge(m_read, e - 1)
                for c in range(FC):
                    last = nc.tensor.matmul(bank[6 + e % 2][:, 0:D], w1T[:, e, c, :], w2[:, e, c, :],
                                            start=(c == 0), stop=(c == FC - 1))
                last.then_inc(m_full, 1)
            pe.wait_ge(b1pad_ready, E)
            for e in range(E):
                for c in range(FC):
                    last = nc.tensor.matmul(bank[4][0:TT * E, 0:D], b1pad[:, e, c, :], w2[:, e, c, :],
                                            start=(e == 0 and c == 0), stop=(e == E - 1 and c == FC - 1))
            last.then_inc(c_full, 1)


def softmax_attention(nc, t, bank, m):
    ident, ipT, opT, bcol, pbcol, ln, mhalf, lneps, blockmask = (
        m[k] for k in ("ident", "ipT", "opT", "bcol", "pbcol", "ln", "mhalf", "lneps", "blockmask"))
    x, y1_dram = t["x"], t["y1"]
    ctx = ExitStack()
    with ctx:
        def sb(name, shape, dt=F32):
            return ctx.enter_context(nc.sbuf_tensor(name, shape, dt))

        def sig(name, per=1):
            return Signal(ctx.enter_context(nc.semaphore(name)), per)

        two = range(2)
        xs = [sb(f"xs{i}", [P, TT, D]) for i in two]
        stats = sb("stats", [P, TT, 6])
        mv = sb("mv", [P, TT, 2])
        rstd = sb("rstd", [P, TT])
        mr = sb("mr", [P, TT])
        nb = sb("nb", [P, TT])
        xn = sb("xn", [P, TT, D])
        xT = [sb(f"xT{i}", [P, TT * P]) for i in two]
        xb = [sb(f"xb{i}", [P, TT * P]) for i in two]
        qT = sb("qT", [P, TT * P])
        kTm = sb("kTm", [P, HB, TT * P])
        v = [sb(f"v{i}", [P, TT, D]) for i in two]
        sc = sb("sc", [P, TT * HB, 32])
        mx = sb("mx", [P, TT * HB])
        ex = sb("ex", [P, TT * HB, 32])
        sm = sb("sm", [P, TT * HB])
        rs = sb("rs", [P, TT * HB])
        pr = sb("pr", [P, TT * HB, 32])
        pT = sb("pT", [P, TT * HB, P])
        oT = sb("oT", [P, TT * P])
        stats1 = sb("stats1", [P, TT, 6])
        mv1 = sb("mv1", [P, TT, 2])
        rstd1 = sb("rstd1", [P, TT])
        mr1 = sb("mr1", [P, TT])
        nb1 = sb("nb1", [P, TT])
        none = sb("none", [P, TT])
        yn = sb("yn", [P, TT, D])
        yg = sb("yg", [P, TT, D])
        y1 = [sb(f"y1_{i}", [P, TT, D]) for i in two]

        x_loaded = [Signal(ctx.enter_context(nc.semaphore(f"a_x_loaded{i}")), 0) for i in two]
        stored = [Signal(ctx.enter_context(nc.semaphore(f"a_y1_stored{i}")), 0) for i in two]
        zeroed = sig("a_zeroed")
        alone = ctx.enter_context(nc.semaphore("a_alone"))
        s = {n: sig("a_" + n, per) for n, per in dict(
            stats=TT, mv=TT, veps=1, rstd=1, mr=1, nb=1, xn=TT, xT_full=1, xT=1, xb=1, q_full=1, q=1, k_full=1, k=HB, v_full=1, v=1,
            sc_full=1, sc=1, mx=1, sub=1, ex=1, sm=1, rs=1, pr=1, pT=TT, o_full=1, o=1, y_full=1,
            stats1=TT, mv1=TT, veps1=1, rstd1=1, mr1=1, nb1=1, yn=TT, yg=1, y1=1).items()}

        xv = x.rearrange("l (g t n) d -> g n l t d", t=TT, n=8)
        yv = y1_dram.rearrange("l (g t n) d -> g n l t d", t=TT, n=8)
        B_XT, B_Q, B_K, B_V, B_S, B_O, B_Y = *bank[0:6], bank[6:8]
        block = ctx.enter_context(nc.Block())

        AHEAD = 3
        IN_LOOP = (NB - AHEAD - 1) // 2

        def there(b):
            return not isinstance(b.i, int) or 0 <= b.number < NB

        def before_loop():
            return [Batch(0, o) for o in range(-AHEAD, 1)]

        def after_loop():
            return [Batch(0, o) for o in range(2 * IN_LOOP + 1, NB + 1)]

        @block.sync
        def _(sp):
            def load(b):
                if b.number is not None and not (isinstance(b.i, int) and b.number < 2):
                    sp.wait_ge(s["xn"].sem, s["xn"].by(b.next(-2)))
                for n in range(8):
                    sp.dma_start(xs[b.parity][16 * n:16 * n + 16, :, :], xv[b.number, n]).then_inc(x_loaded[b.parity].sem, 16)

            def store(b):
                sp.wait_ge(s["y1"].sem, s["y1"].by(b))
                for n in range(8):
                    sp.dma_start(yv[b.number, n], y1[b.parity][16 * n:16 * n + 16, :, :]).then_inc(stored[b.parity].sem, 16)

            load(Batch(0, 0))
            load(Batch(0, 1))
            start(sp, [*s.values(), zeroed, *stored])
            for o in range(2, 6):
                load(Batch(0, o))
            with sp.Fori(0, NB // 2 - 3) as i:
                for o in two:
                    load(Batch(i, o + 6))
                    store(Batch(i, o))
            for o in range(NB - 6, NB):
                store(Batch(0, o))
            for o in two:
                sp.wait_ge(stored[o].sem, 128 * (NB // 2) + 1)

        @block.tensor
        def _(pe):
            def turn_x(b):
                pe.wait_ge(s["xn"].sem, s["xn"].by(b))
                pe.wait_ge(s["xT"].sem, s["xT"].by(b.prev()))
                for c in range(TT):
                    last = nc.tensor.transpose(B_XT[:, c * P:(c + 1) * P], xn[:, c, :], ident[:])
                last.then_inc(s["xT_full"].sem, 1)

            def project_qk(b):
                pe.wait_ge(s["xT"].sem, s["xT"].by(b))
                pe.wait_ge(s["q"].sem, s["q"].by(b.prev()))
                nc.tensor.matmul(B_Q[:], ipT[:, 0:D], xT[b.parity][:], start=True, stop=True).then_inc(s["q_full"].sem, 1)
                pe.wait_ge(s["k"].sem, s["k"].by(b.prev()))
                nc.tensor.matmul(B_K[:], ipT[:, D:2 * D], xT[b.parity][:], start=True, stop=True).then_inc(s["k_full"].sem, 1)

            def project_v(b):
                pe.wait_ge(s["v"].sem, s["v"].by(b.prev()))
                for c in range(TT):
                    last = nc.tensor.matmul(B_V[:, c * D:(c + 1) * D], xT[b.parity][:, c * P:(c + 1) * P],
                                            ipT[:, 2 * D:3 * D], start=True, stop=True)
                last.then_inc(s["v_full"].sem, 1)

            def scores(b):
                pe.wait_ge(s["q"].sem, s["q"].by(b))
                pe.wait_ge(s["k"].sem, s["k"].by(b))
                pe.wait_ge(s["sc"].sem, s["sc"].by(b.prev()))
                for c in range(TT):
                    for k in range(4):
                        a = c * P + 32 * k
                        last = nc.tensor.matmul(B_S[32 * k:32 * k + 32, c * P:(c + 1) * P], qT[:, a:a + 32],
                                                kTm[:, :, a:a + 32], start=True, stop=True)
                last.then_inc(s["sc_full"].sem, 1)

            def values(b):
                pe.wait_ge(s["v"].sem, s["v"].by(b))
                pe.wait_ge(s["pT"].sem, s["pT"].by(b))
                pe.wait_ge(s["o"].sem, s["o"].by(b.prev()))
                for c in range(TT):
                    for h in range(HB):
                        last = nc.tensor.matmul(B_O[32 * h:32 * h + 32, c * P:(c + 1) * P], v[b.parity][:, c, 32 * h:32 * h + 32],
                                                pT[:, c * HB + h, :], start=True, stop=True)
                last.then_inc(s["o_full"].sem, 1)

            def output(b):
                pe.wait_ge(s["o"].sem, s["o"].by(b))
                pe.wait_ge(s["xb"].sem, s["xb"].by(b))
                pe.wait_ge(s["yn"].sem, s["yn"].by(b.next(-2)))
                for c in range(TT):
                    nc.tensor.matmul(B_Y[b.parity][:, c * D:(c + 1) * D], oT[:, c * P:(c + 1) * P], opT[:], start=True, stop=False)
                    last = nc.tensor.matmul(B_Y[b.parity][:, c * D:(c + 1) * D], xb[b.parity][:, c * P:(c + 1) * P], ident[:],
                                            start=False, stop=True)
                last.then_inc(s["y_full"].sem, 1)

            def step(b):
                if there(b.next(2)):
                    turn_x(b.next(2))
                if there(b.next(1)):
                    scores(b.next(1))
                if there(b.next(2)):
                    project_qk(b.next(2))
                if there(b):
                    values(b)
                if there(b.next(2)):
                    project_v(b.next(2))
                if there(b):
                    output(b)

            for b in before_loop():
                step(b)
            with pe.Fori(0, IN_LOOP) as i:
                for o in (1, 2):
                    step(Batch(i, o))
            for b in after_loop():
                step(b)

        @block.scalar
        def _(act):
            def copy_xT(b):
                act.wait_ge(s["xT_full"].sem, s["xT_full"].by(b))
                act.wait_ge(s["v_full"].sem, s["v_full"].by(b.next(-2)))
                act.wait_ge(s["xb"].sem, s["xb"].by(b.next(-2)))
                nc.scalar.activation(xT[b.parity][:], B_XT[:], ACT.Copy).then_inc(s["xT"].sem, 1)

            def copy_qk(b):
                act.wait_ge(s["q_full"].sem, s["q_full"].by(b))
                act.wait_ge(s["sc_full"].sem, s["sc_full"].by(b.prev()))
                nc.scalar.activation(qT[:], B_Q[:], ACT.Identity, bias=bcol[:, 0:1]).then_inc(s["q"].sem, 1)
                act.wait_ge(s["k_full"].sem, s["k_full"].by(b))
                for h in range(HB):
                    r = slice(32 * h, 32 * h + 32)
                    nc.scalar.activation(kTm[r, h, :], B_K[r, :], ACT.Identity, bias=bcol[r, 1:2]).then_inc(s["k"].sem, 1)

            def copy_v(b):
                act.wait_ge(s["v_full"].sem, s["v_full"].by(b))
                act.wait_ge(s["o_full"].sem, s["o_full"].by(b.next(-2)))
                nc.scalar.activation(v[b.parity][:].rearrange("p t d -> p (t d)"), B_V[:], ACT.Copy).then_inc(s["v"].sem, 1)

            def exps(b):
                act.wait_ge(s["sub"].sem, s["sub"].by(b))
                act.wait_ge(s["pr"].sem, s["pr"].by(b.prev()))
                nc.scalar.activation(ex[:].rearrange("p a k -> p (a k)"), sc[:].rearrange("p a k -> p (a k)"), ACT.Exp).then_inc(s["ex"].sem, 1)

            def copy_o(b):
                act.wait_ge(s["o_full"].sem, s["o_full"].by(b))
                act.wait_ge(s["y_full"].sem, s["y_full"].by(b.prev()))
                nc.scalar.activation(oT[:], B_O[:], ACT.Copy).then_inc(s["o"].sem, 1)

            def norm(b):
                act.wait_ge(s["nb"].sem, s["nb"].by(b))
                act.wait_ge(s["xT_full"].sem, s["xT_full"].by(b.prev()))
                for c in range(TT):
                    nc.scalar.activation(xn[:, c, :], xs[b.parity][:, c, :], ACT.Identity, bias=nb[:, c:c + 1],
                                         scale=rstd[:, c:c + 1]).then_inc(s["xn"].sem, 1)

            def norm1(b):
                act.wait_ge(s["nb1"].sem, s["nb1"].by(b))
                act.wait_ge(s["yg"].sem, s["yg"].by(b.prev()))
                for c in range(TT):
                    nc.scalar.activation(yn[:, c, :], B_Y[b.parity][:, c * D:(c + 1) * D], ACT.Identity, bias=nb1[:, c:c + 1],
                                         scale=rstd1[:, c:c + 1]).then_inc(s["yn"].sem, 1)

            def step(b):
                if there(b.next(2)):
                    copy_xT(b.next(2))
                if there(b.next()):
                    copy_v(b.next())
                if there(b.next(2)):
                    copy_qk(b.next(2))
                if there(b):
                    copy_o(b)
                if there(b.next()):
                    exps(b.next())
                if there(b.next(3)):
                    norm(b.next(3))
                if there(b.prev()):
                    norm1(b.prev())

            act.preload_act_table_set("natural_log_exp_and_others")
            act.wait_ge(zeroed.sem, zeroed.by(Batch(0, 0)))
            for b in before_loop():
                step(b)
            with act.Fori(0, IN_LOOP) as i:
                for o in (1, 2):
                    step(Batch(i, o))
            for b in after_loop():
                step(b)

        @block.gpsimd
        def _(pool):
            def norm_scale(b):
                pool.wait_ge(s["mv"].sem, s["mv"].by(b))
                pool.wait_ge(s["xn"].sem, s["xn"].by(b.prev()))
                nc.gpsimd.tensor_tensor(rstd[:], mv[:, :, 1], lneps[:], ALU.add).then_inc(s["veps"].sem, 1)
                pool.wait_ge(s["veps"].sem, s["veps"].by(b))
                nc.gpsimd.tensor_tensor(rstd[:], rstd[:], mhalf[:], ALU.pow).then_inc(s["rstd"].sem, 1)
                pool.wait_ge(s["rstd"].sem, s["rstd"].by(b))
                nc.gpsimd.tensor_tensor(mr[:], mv[:, :, 0], rstd[:], ALU.mult).then_inc(s["mr"].sem, 1)
                pool.wait_ge(s["mr"].sem, s["mr"].by(b))
                nc.gpsimd.tensor_tensor(nb[:], none[:], mr[:], ALU.subtract).then_inc(s["nb"].sem, 1)

            def norm_scale1(b):
                pool.wait_ge(s["mv1"].sem, s["mv1"].by(b))
                pool.wait_ge(s["yn"].sem, s["yn"].by(b.prev()))
                nc.gpsimd.tensor_tensor(rstd1[:], mv1[:, :, 1], lneps[:], ALU.add).then_inc(s["veps1"].sem, 1)
                pool.wait_ge(s["veps1"].sem, s["veps1"].by(b))
                nc.gpsimd.tensor_tensor(rstd1[:], rstd1[:], mhalf[:], ALU.pow).then_inc(s["rstd1"].sem, 1)
                pool.wait_ge(s["rstd1"].sem, s["rstd1"].by(b))
                nc.gpsimd.tensor_tensor(mr1[:], mv1[:, :, 0], rstd1[:], ALU.mult).then_inc(s["mr1"].sem, 1)
                pool.wait_ge(s["mr1"].sem, s["mr1"].by(b))
                nc.gpsimd.tensor_tensor(nb1[:], none[:], mr1[:], ALU.subtract).then_inc(s["nb1"].sem, 1)

            def probs(b):
                pool.wait_ge(s["rs"].sem, s["rs"].by(b))
                pool.wait_ge(s["pT"].sem, s["pT"].by(b.prev()))
                nc.gpsimd.tensor_tensor(pr[:], ex[:], rs[:].unsqueeze(2).broadcast_to([P, TT * HB, 32]), ALU.mult).then_inc(s["pr"].sem, 1)

            def gain(b):
                pool.wait_ge(s["yn"].sem, s["yn"].by(b))
                pool.wait_ge(s["y1"].sem, s["y1"].by(b.prev()))
                nc.gpsimd.tensor_tensor(yg[:], yn[:], ln[:, 0, :].unsqueeze(1).broadcast_to([P, TT, D]), ALU.mult).then_inc(s["yg"].sem, 1)

            def shift(b):
                pool.wait_ge(s["yg"].sem, s["yg"].by(b))
                done = b.i * 128 + 128 * (b.off // 2)
                if not isinstance(b.i, int) or done > 0:
                    pool.wait_ge(stored[b.parity].sem, done + 1)
                nc.gpsimd.tensor_tensor(y1[b.parity][:], yg[:], ln[:, 1, :].unsqueeze(1).broadcast_to([P, TT, D]), ALU.add).then_inc(s["y1"].sem, 1)

            def step(b):
                if there(b.next(3)):
                    norm_scale(b.next(3))
                if there(b.prev()):
                    norm_scale1(b.prev())
                if there(b.next()):
                    probs(b.next())
                if there(b.prev()):
                    gain(b.prev())
                    shift(b.prev())

            nc.gpsimd.memset(none[:], 0.0)
            nc.gpsimd.memset(kTm[:], 0.0)
            nc.gpsimd.memset(pT[:], 0.0).then_inc(zeroed.sem, 1)
            pool.wait_ge(zeroed.sem, zeroed.by(Batch(0, 0)))
            for b in before_loop():
                step(b)
            with pool.Fori(0, IN_LOOP) as i:
                for o in (1, 2):
                    step(Batch(i, o))
            for b in after_loop():
                step(b)

        @block.vector
        def _(dve):
            def norm_stats(b):
                dve.wait_ge(x_loaded[b.parity].sem, b.i * 128 + 128 * (b.off // 2 + 1))
                dve.wait_ge(s["mr"].sem, s["mr"].by(b.prev()))
                for c in range(TT):
                    nc.vector.bn_stats(stats[:, c, :], xs[b.parity][:, c, :]).then_inc(s["stats"].sem, 1)
                dve.wait_ge(s["stats"].sem, s["stats"].by(b))
                dve.sem_inc(alone, 1)
                for c in range(TT):
                    nc.vector.bn_aggr(mv[:, c, :], stats[:, c, :]).then_inc(s["mv"].sem, 1)

            def copy_xb(b):
                dve.wait_ge(s["xT"].sem, s["xT"].by(b))
                dve.wait_ge(s["y_full"].sem, s["y_full"].by(b.next(-2)))
                nc.vector.tensor_scalar(xb[b.parity][:], xT[b.parity][:], pbcol[:], None, ALU.add).then_inc(s["xb"].sem, 1)

            def norm_stats1(b):
                dve.wait_ge(s["y_full"].sem, s["y_full"].by(b))
                dve.wait_ge(s["mr1"].sem, s["mr1"].by(b.prev()))
                for c in range(TT):
                    nc.vector.bn_stats(stats1[:, c, :], B_Y[b.parity][:, c * D:(c + 1) * D]).then_inc(s["stats1"].sem, 1)
                dve.wait_ge(s["stats1"].sem, s["stats1"].by(b))
                dve.sem_inc(alone, 1)
                for c in range(TT):
                    nc.vector.bn_aggr(mv1[:, c, :], stats1[:, c, :]).then_inc(s["mv1"].sem, 1)

            def softmax_top(b):
                dve.wait_ge(s["sc_full"].sem, s["sc_full"].by(b))
                dve.wait_ge(s["ex"].sem, s["ex"].by(b.prev()))
                nc.vector.scalar_tensor_tensor(out=sc[:], in0=B_S[:].rearrange("p (a k) -> p a k", k=32), scalar=float(DB) ** -0.5,
                                               in1=blockmask[:].unsqueeze(1).broadcast_to([P, TT * HB, 32]),
                                               op0=ALU.mult, op1=ALU.add).then_inc(s["sc"].sem, 1)
                dve.wait_ge(s["sc"].sem, s["sc"].by(b))
                nc.vector.tensor_reduce(mx[:], sc[:], AX, ALU.max).then_inc(s["mx"].sem, 1)
                dve.wait_ge(s["mx"].sem, s["mx"].by(b))
                nc.vector.tensor_tensor(sc[:], sc[:], mx[:].unsqueeze(2).broadcast_to([P, TT * HB, 32]), ALU.subtract).then_inc(s["sub"].sem, 1)

            def softmax_sum(b):
                dve.wait_ge(s["ex"].sem, s["ex"].by(b))
                nc.vector.tensor_reduce(sm[:], ex[:], AX, ALU.add).then_inc(s["sm"].sem, 1)
                dve.wait_ge(s["sm"].sem, s["sm"].by(b))
                dve.wait_ge(s["pr"].sem, s["pr"].by(b.prev()))
                nc.vector.reciprocal(rs[:], sm[:]).then_inc(s["rs"].sem, 1)

            def turn_probs(b):
                dve.wait_ge(s["pr"].sem, s["pr"].by(b))
                dve.wait_ge(s["o_full"].sem, s["o_full"].by(b.prev()))
                for k in range(4):
                    r = slice(32 * k, 32 * k + 32)
                    nc.vector.transpose(pT[r, :, r], pr[r, :, :]).then_inc(s["pT"].sem, 1)

            def step(b):
                if there(b.next(3)):
                    norm_stats(b.next(3))
                if there(b.next()):
                    copy_xb(b.next())
                if there(b):
                    turn_probs(b)
                if there(b.next()):
                    softmax_top(b.next())
                if there(b.prev()):
                    norm_stats1(b.prev())
                if there(b.next()):
                    softmax_sum(b.next())

            dve.wait_ge(zeroed.sem, zeroed.by(Batch(0, 0)))
            for b in before_loop():
                step(b)
            with dve.Fori(0, IN_LOOP) as i:
                for o in (1, 2):
                    step(Batch(i, o))
            for b in after_loop():
                step(b)


def squared_attention_and_experts(nc, t, bank, m):
    ident, wqkvT, woT, mexp, cpad, wg, bqkv, ln, rope, featw, jmask = (
        m[k] for k in ("ident", "wqkvT", "woT", "mexp", "cpad", "wg", "bqkv", "ln", "rope", "featw", "jmask"))
    upper, ones, first, mhalf, lneps, eps, carry = (m[k] for k in ("upper", "ones", "first", "mhalf", "lneps", "eps", "carry"))
    x, y1_dram, out = t["x"], t["y1"], t["out"]
    H2 = 2 * HA
    W = OFF * DA
    ctx = ExitStack()
    with ctx:
        def sb(name, shape, dt=F32):
            return ctx.enter_context(nc.sbuf_tensor(name, shape, dt))

        def sem(name):
            return ctx.enter_context(nc.semaphore(name))

        two = range(2)
        xs = [sb(f"b_xs{i}", [P, TT, D]) for i in two]
        y1 = [sb(f"b_y1_{i}", [P, TT, D]) for i in two]
        stats, mv, rstd = sb("b_stats", [P, TT, 6]), sb("b_mv", [P, TT, 2]), sb("b_rstd", [P, TT])
        xn = sb("b_xn", [P, TT, D])
        res = [sb(f"res{i}", [P, TT, D]) for i in two]
        xT = sb("b_xT", [P, TT * P])
        qkv = [sb(f"qkv{i}", [P, TT, 3 * D]) for i in two]
        vm = [sb(f"vm{i}", [P, TT, HA, 32]) for i in two]
        sq = sb("sq", [P, TT, H2, DA])
        ms, lnv, r0, va, ra, rb, rc, rr = (sb(n, [P, TT, H2]) for n in ("ms", "lnv", "r0", "va", "ra", "rb", "rc", "rr"))
        qn = sb("qn", [P, TT, H2, DA])
        t1 = sb("t1", [P, TT, H2, DA])
        t2 = sb("t2", [P, TT, H2, DA])
        qr = sb("qr", [P, TT, 2 * D])
        qd = [sb(f"qd{i}", [P, TT, H2, DA + OFF - 1]) for i in two]
        qT = sb("b_qT", [P, TT * P])
        qm = [sb(f"qm{i}", [P, GA, TT * P]) for i in two]
        kg = [sb(f"kg{i}", [P, GA, TT * P]) for i in two]
        fk = [sb(f"fk{i}", [P, HA, OFF, DA]) for i in two]
        fq = [sb(f"fq{i}", [P, HA, OFF, DA]) for i in two]
        fqT = [sb(f"fqT{i}", [P, FB, P]) for i in two]
        state = [sb(f"state{i}", [P, FB, D]) for i in two]
        pat = [sb(f"pat{i}", [P, HA, P]) for i in two]
        zT = sb("zT", [P, TT * P])
        y1T = [sb(f"y1T{i}", [P, TT * P]) for i in two]
        lg = sb("lg", [P, TT, E])
        top = sb("top", [P, TT])
        sh = sb("sh", [P, TT, E])
        ge = sb("ge", [P, TT, E])
        gs = sb("gs", [P, TT])
        gr = sb("gr", [P, TT])
        pick = sb("pick", [P, TT, E])
        best = sb("best", [P, TT])
        oh = sb("oh", [P, TT, E])
        ohb = sb("ohb", [P, TT, E], BF16)
        loc = sb("loc", [P, TT, E])
        keep = sb("keep", [P, TT, E])
        w = [sb(f"w{i}", [P, TT, E]) for i in two]
        wT = sb("wT", [TT * E, P])
        acc = [sb(f"acc{i}", [P, TT, D]) for i in two]
        stats2, mv2, rstd2 = sb("stats2", [P, TT, 6]), sb("mv2", [P, TT, 2]), sb("rstd2", [P, TT])
        z = sb("z", [P, TT, D])
        zg = sb("zg", [P, TT, D])
        zo = sb("zo", [P, TT, D])
        outs = [sb(f"outs{i}", [P, TT, D]) for i in two]

        S_BANKS, G_BANKS, ST_A, ST_B, B_Z = bank[0:2], bank[2:5], bank[5], bank[6], bank[7]

        x_loaded = [sem(f"b_x_loaded{i}") for i in two]
        y_loaded = [sem(f"b_y_loaded{i}") for i in two]
        stored = [Signal(sem(f"b_stored{i}"), 0) for i in two]
        passed = sem("passed")
        zeroed = Signal(sem("b_zeroed"), 1)
        alone = sem("b_alone")
        s = {n: Signal(sem("b_" + n), per) for n, per in dict(
            stats=TT, mv=TT, veps=1, rstd=1, xn=TT, xxn=1, res=1, xT=1, qkv=TT, qkv_used=1, vm=TT, sq=1, ms=1, lnv=1, r0=1,
            va=1, ra=1, rb=1, rc=1, rr=1, qn=1, t1=TT, t2=2, qr=1, qd=2, qT=1, qm=GA, kg=GA, q_used=1,
            fk=TT - 1, fq=TT - 1, fqT=2 * (TT - 1), st_full=TT - 1, state=2 * (TT - 1),
            s_full=HA, pat=HA, masked=HA, z_full=TT, z=TT, y1T=1, lg=1, top=1, sh=1, ge=1, gs=1, gr=1,
            pick=1, best=1, oh=1, ohb=1, loc=1, keep=1, w=1, carry=1, wT=1, acc=TT * E, ym=1,
            stats2=TT, mv2=TT, veps2=1, rstd2=1, z2=TT, zg=1, zo=1, outs=1).items()}

        TURNS = ["wT", "y0a", "fq1a", "fq1b", "xT'", "y0b", "qkv'0", "qkv'1", "y1T'", "fq2a", "fq2b", "y1a", "qkv'2", "qkv'3", "y1b",
                 "lg'", "y2a", "fq3a", "fq3b", "y2b", "rank'", "y3a", "q'", "k'", "y3b", "bias", "out"]
        NEXT = [n for n in TURNS if "'" in n]
        LAST = [n for n in TURNS if "'" not in n]

        MOVED = {"xT'": ("xT", 1, 1), "q'": ("qT", 1, 1), "k'": ("kg", GA, 1), "y1T'": ("y1T", 1, 1), "lg'": ("lg", 1, 1),
                 "rank'": ("carry", 1, 1), "wT": ("wT", 1, 0), "bias": ("ym", 1, 0), "out": ("zo", 1, 0)}
        MOVED.update({f"qkv'{c}": ("qkv", c + 1, 1) for c in range(TT)})
        MOVED.update({f"fq{c}{h}": ("fqT", 2 * c - 1 + (h == "b"), 0) for c in range(1, TT) for h in "ab"})
        MOVED.update({f"y{c}{h}": ("acc", E * c + E // 2 * (1 + (h == "b")), 0) for c in range(TT) for h in "ab"})
        assert len(TURNS) % len(G_BANKS) == 0

        class Turn:

            def __init__(self, b, names, name):
                k = names.index(name)
                self.to = G_BANKS[k % len(G_BANKS)]
                if names is NEXT:
                    self.full = k + 1
                else:
                    self.full = b.i * (2 * len(TURNS)) + b.off * len(TURNS) + len(NEXT) + k + 1
                k -= len(G_BANKS)
                before, of = (names[k], b if names is not NEXT else b.prev()) if k >= 0 else (TURNS[k], b.prev())
                signal, n, ahead = MOVED[before]
                self.prior = s[signal]
                self.moved = self.prior.by(of.next() if ahead else of, n)

        xv = x.rearrange("b (c p) d -> b p c d", p=P)
        yv = y1_dram.rearrange("b (c p) d -> b p c d", p=P)
        ov = out.rearrange("b (c p) d -> b p c d", p=P)
        LASTB = NB // 2 - 1
        block = ctx.enter_context(nc.Block())

        @block.sync
        def _(sp):
            def load(b, wait=True):
                if wait:
                    sp.wait_ge(s["res"].sem, s["res"].by(b.prev().prev()))
                sp.dma_start(xs[b.parity][:], xv[b.number]).then_inc(x_loaded[b.parity], 16)
                if wait:
                    sp.wait_ge(s["acc"].sem, s["acc"].by(b.prev().prev(), TT * E - E + 1))
                sp.dma_start(y1[b.parity][:], yv[b.number]).then_inc(y_loaded[b.parity], 16)

            def store(b):
                sp.wait_ge(s["outs"].sem, s["outs"].by(b))
                sp.dma_start(ov[b.number], outs[b.parity][:]).then_inc(stored[b.parity].sem, 16)

            for o in two:
                load(Batch(0, o), wait=False)
            start(sp, [*s.values(), zeroed, *stored])
            with sp.Fori(0, LASTB) as i:
                for o in two:
                    load(Batch(i, o + 2))
                    store(Batch(i, o))
            for o in two:
                store(Batch(LASTB, o))
            for o in two:
                sp.wait_ge(stored[o].sem, 16 * (NB // 2) + 1)

        @block.tensor
        def _(pe):
            def pe_xT(b, turn):
                pe.wait_ge(s["xn"].sem, s["xn"].by(b))
                pe.wait_ge(turn.prior.sem, turn.moved)
                to = turn.to
                for c in range(TT):
                    last = nc.tensor.transpose(to[:, c * P:(c + 1) * P], xn[:, c, :], ident[:])
                last.then_inc(passed, 1)

            def pe_qkv(b, c, turn):
                pe.wait_ge(s["xT"].sem, s["xT"].by(b))
                pe.wait_ge(turn.prior.sem, turn.moved)
                to = turn.to
                nc.tensor.matmul(to[:, 0:3 * D], xT[:, c * P:(c + 1) * P], wqkvT[:], start=True, stop=True).then_inc(passed, 1)

            def pe_turn_qk(b, which, turn):
                pe.wait_ge(s["qr"].sem, s["qr"].by(b))
                pe.wait_ge(turn.prior.sem, turn.moved)
                to = turn.to
                for c in range(TT):
                    last = nc.tensor.transpose(to[:, c * P:(c + 1) * P], qr[:, c, which * D:(which + 1) * D], ident[:])
                last.then_inc(passed, 1)

            def pe_scores(b, c):
                pe.wait_ge(s["qm"].sem, s["qm"].by(b))
                pe.wait_ge(s["kg"].sem, s["kg"].by(b))
                for g in range(GA):
                    n = c * GA + g
                    if n >= 2:
                        pe.wait_ge(s["pat"].sem, s["pat"].by(b, n - 1))
                    else:
                        pe.wait_ge(s["pat"].sem, s["pat"].by(b.prev()))
                    last = nc.tensor.matmul(S_BANKS[n % 2][:].rearrange("p (j q) -> p j q", j=GA), kg[b.parity][:, g, c * P:(c + 1) * P],
                                            qm[b.parity][:, :, c * P:(c + 1) * P], start=True, stop=True)
                    last.then_inc(s["s_full"].sem, 1)

            def pe_fq(b, c, turns):
                pe.wait_ge(s["fq"].sem, s["fq"].by(b, c))
                for k in range(FB):
                    turn = turns[k // 4]
                    if k % 4 == 0:
                        pe.wait_ge(turn.prior.sem, turn.moved)
                        to = turn.to
                    last = nc.tensor.transpose(to[:, k % 4 * P:(k % 4 + 1) * P], fq[(c + 1) % 2][:].rearrange("p h o i -> p (h o i)")[:, k * P:(k + 1) * P], ident[:])
                    if k in (3, FB - 1):
                        last.then_inc(passed, 1)

            def pe_state(b, c):
                pe.wait_ge(s["fk"].sem, s["fk"].by(b, c + 1))
                if c == 0:
                    pe.wait_ge(s["state"].sem, s["state"].by(b.prev()))
                else:
                    pe.wait_ge(s["state"].sem, s["state"].by(b, 2 * c))
                for k in range(FB):
                    to = ST_A[:, k * P:(k + 1) * P] if k < 4 else ST_B[:, 0:P]
                    last = nc.tensor.matmul(to, fk[c % 2][:].rearrange("p h o i -> p (h o i)")[:, k * P:(k + 1) * P],
                                            qkv[b.parity][:, c, 2 * D:3 * D], start=(c == 0 and k in (0, 4)), stop=(c == TT - 2),
                                            skip_group_check=True)
                last.then_inc(s["st_full"].sem, 1)

            def pe_values(b, c):
                if c == 0:
                    pe.wait_ge(s["z"].sem, s["z"].by(b.prev()))
                else:
                    pe.wait_ge(s["z"].sem, s["z"].by(b, c))
                    pe.wait_ge(s["fqT"].sem, s["fqT"].by(b, 2 * c))
                    pe.wait_ge(s["state"].sem, s["state"].by(b, 2 * c))
                    for k in range(FB):
                        nc.tensor.matmul(B_Z[:, 0:P], state[(c - 1) % 2][:, k, :], fqT[(c + 1) % 2][:, k, :], start=(k == 0), stop=False,
                                         skip_group_check=True)
                pe.wait_ge(s["vm"].sem, s["vm"].by(b))
                pe.wait_ge(s["masked"].sem, s["masked"].by(b, GA * (c + 1)))
                for j in range(GA):
                    for g in range(GA):
                        last = nc.tensor.matmul(B_Z[32 * g:32 * g + 32, 0:P], vm[b.parity][:, c, g * GA + j, :],
                                                pat[c % 2][:, g * GA + j, :], start=(c == 0 and j == 0), stop=(j == GA - 1),
                                                skip_group_check=True)
                last.then_inc(s["z_full"].sem, 1)

            def pe_out(b, turn):
                pe.wait_ge(s["z"].sem, s["z"].by(b))
                pe.wait_ge(turn.prior.sem, turn.moved)
                to = turn.to
                for c in range(TT):
                    last = nc.tensor.matmul(to[:, c * D:(c + 1) * D], zT[:, c * P:(c + 1) * P], woT[:], start=True, stop=True)
                last.then_inc(passed, 1)

            def pe_y1T(b, turn):
                pe.wait_ge(y_loaded[b.parity], b.i * 16 + 16 * (b.off // 2 + 1))
                pe.wait_ge(turn.prior.sem, turn.moved)
                to = turn.to
                for c in range(TT):
                    last = nc.tensor.transpose(to[:, c * P:(c + 1) * P], y1[b.parity][:, c, :], ident[:])
                last.then_inc(passed, 1)

            def pe_logits(b, turn):
                pe.wait_ge(s["y1T"].sem, s["y1T"].by(b))
                pe.wait_ge(turn.prior.sem, turn.moved)
                to = turn.to
                for c in range(TT):
                    last = nc.tensor.matmul(to[:, c * E:(c + 1) * E], y1T[b.parity][:, c * P:(c + 1) * P], wg[:], start=True, stop=True)
                last.then_inc(passed, 1)

            def pe_rank(b, turn):
                pe.wait_ge(s["ohb"].sem, s["ohb"].by(b))
                pe.wait_ge(turn.prior.sem, turn.moved)
                to = turn.to
                o2 = ohb[:].rearrange("p c e -> p (c e)")
                nc.tensor.matmul(to[:, 0:TT * E], upper[:], o2, start=True, stop=False, skip_group_check=True)
                for d in range(1, TT):
                    nc.tensor.matmul(to[:, d * E:TT * E], ones[:], o2[:, 0:(TT - d) * E], start=False, stop=False, skip_group_check=True)
                for c in range(TT):
                    last = nc.tensor.matmul(to[:, TT * E:(TT + 1) * E], ones[:], o2[:, c * E:(c + 1) * E], start=False, stop=(c == TT - 1),
                                            skip_group_check=True)
                last.then_inc(passed, 1)

            def pe_wT(b, turn):
                pe.wait_ge(s["w"].sem, s["w"].by(b))
                pe.wait_ge(turn.prior.sem, turn.moved)
                to = turn.to
                nc.tensor.transpose(to[0:TT * E, 0:P], w[b.parity][:].rearrange("p c e -> p (c e)"), ident[:]).then_inc(passed, 1)

            def pe_expert(b, c, half, turn):
                pe.wait_ge(turn.prior.sem, turn.moved)
                to = turn.to
                nc.tensor.matmul(to[:], y1T[b.parity][:, c * P:(c + 1) * P], mexp[:, half * 512:(half + 1) * 512], start=True, stop=True)\
                    .then_inc(passed, 1)

            def pe_bias(b, turn):
                pe.wait_ge(s["wT"].sem, s["wT"].by(b))
                pe.wait_ge(turn.prior.sem, turn.moved)
                to = turn.to
                for c in range(TT):
                    last = nc.tensor.matmul(to[:, c * D:(c + 1) * D], wT[:], cpad[:, c, :], start=True, stop=True)
                last.then_inc(passed, 1)

            def body(b, names):
                def T(name):
                    return Turn(b, names, name)

                n, more = b.next(), names is TURNS
                pe_scores(b, 0)
                pe_wT(b, T("wT"))
                pe_expert(b, 0, 0, T("y0a"))
                pe_fq(b, 1, (T("fq1a"), T("fq1b")))
                pe_state(b, 0)
                if more:
                    pe_xT(n, T("xT'"))
                pe_values(b, 0)
                pe_expert(b, 0, 1, T("y0b"))
                pe_scores(b, 1)
                if more:
                    pe_qkv(n, 0, T("qkv'0"))
                    pe_qkv(n, 1, T("qkv'1"))
                    pe_y1T(n, T("y1T'"))
                pe_fq(b, 2, (T("fq2a"), T("fq2b")))
                pe_state(b, 1)
                pe_expert(b, 1, 0, T("y1a"))
                if more:
                    pe_qkv(n, 2, T("qkv'2"))
                    pe_qkv(n, 3, T("qkv'3"))
                pe_values(b, 1)
                pe_expert(b, 1, 1, T("y1b"))
                pe_scores(b, 2)
                if more:
                    pe_logits(n, T("lg'"))
                pe_expert(b, 2, 0, T("y2a"))
                pe_fq(b, 3, (T("fq3a"), T("fq3b")))
                pe_state(b, 2)
                pe_values(b, 2)
                pe_expert(b, 2, 1, T("y2b"))
                if more:
                    pe_rank(n, T("rank'"))
                pe_scores(b, 3)
                pe_expert(b, 3, 0, T("y3a"))
                if more:
                    pe_turn_qk(n, 0, T("q'"))
                    pe_turn_qk(n, 1, T("k'"))
                pe_expert(b, 3, 1, T("y3b"))
                pe_values(b, 3)
                pe_bias(b, T("bias"))
                pe_out(b, T("out"))

            b0 = Batch(0, 0)
            T = lambda name: Turn(b0, NEXT, name)
            pe_xT(b0, T("xT'"))
            pe_qkv(b0, 0, T("qkv'0"))
            pe_qkv(b0, 1, T("qkv'1"))
            pe_y1T(b0, T("y1T'"))
            pe_qkv(b0, 2, T("qkv'2"))
            pe_qkv(b0, 3, T("qkv'3"))
            pe_logits(b0, T("lg'"))
            pe_rank(b0, T("rank'"))
            pe_turn_qk(b0, 0, T("q'"))
            pe_turn_qk(b0, 1, T("k'"))
            body(Batch(0, 0), TURNS)
            with pe.Fori(0, LASTB) as i:
                for o in (1, 2):
                    body(Batch(i, o), TURNS)
            body(Batch(LASTB, 1), LAST)

        @block.scalar
        def _(act):
            def act_xT(b, turn):
                act.wait_ge(passed, turn.full)
                src = turn.to
                act.wait_ge(s["qkv"].sem, s["qkv"].by(b.prev()))
                nc.scalar.activation(xT[:], src[:], ACT.Copy).then_inc(s["xT"].sem, 1)

            def act_vm(b):
                act.wait_ge(s["qkv"].sem, s["qkv"].by(b))
                for c in range(TT):
                    to = bass.AP(vm[b.parity], c * HA * 32, [[TT * HA * 32, P], [GA * 32, GA], [32 + DA, GA], [1, DA]])
                    nc.scalar.activation(to, qkv[b.parity][:, c, 2 * D:3 * D].rearrange("p (g j d) -> p g j d", g=GA, j=GA), ACT.Copy).then_inc(s["vm"].sem, 1)

            def act_square_qk(b):
                act.wait_ge(s["qkv"].sem, s["qkv"].by(b))
                act.wait_ge(s["ms"].sem, s["ms"].by(b.prev()))
                nc.scalar.activation(sq[:].rearrange("p c h d -> p c (h d)"), qkv[b.parity][:, :, 0:2 * D], ACT.Square).then_inc(s["sq"].sem, 1)

            def act_rsqrt(b):
                act.wait_ge(s["ms"].sem, s["ms"].by(b))
                act.wait_ge(s["rr"].sem, s["rr"].by(b.prev()))
                nc.scalar.activation(lnv[:], ms[:], ACT.Ln, bias=eps[:], scale=1.0 / DA).then_inc(s["lnv"].sem, 1)
                act.wait_ge(s["lnv"].sem, s["lnv"].by(b))
                nc.scalar.activation(r0[:], lnv[:], ACT.Exp, scale=-0.5).then_inc(s["r0"].sem, 1)

            def act_double(b):
                act.wait_ge(s["qr"].sem, s["qr"].by(b))
                src = qr[:].rearrange("p c (h d) -> p (c h) d", d=DA)
                to = qd[b.parity][:].rearrange("p c h d -> p (c h) d")
                nc.scalar.activation(to[:, :, 0:DA], src, ACT.Copy).then_inc(s["qd"].sem, 1)
                nc.scalar.activation(to[:, :, DA:DA + OFF - 1], src[:, :, 0:OFF - 1], ACT.Copy).then_inc(s["qd"].sem, 1)

            def act_qT(b, turn):
                act.wait_ge(passed, turn.full)
                act.wait_ge(s["qm"].sem, s["qm"].by(b.prev()))
                nc.scalar.activation(qT[:], turn.to[:], ACT.Copy).then_inc(s["qT"].sem, 1)

            def act_kg(b, turn):
                act.wait_ge(passed, turn.full)
                src = turn.to
                for g in range(GA):
                    r = slice(32 * g, 32 * g + 32)
                    nc.scalar.activation(kg[b.parity][r, g, :], src[r, :], ACT.Copy).then_inc(s["kg"].sem, 1)

            def act_square(b, c):
                for g in range(GA):
                    n = GA * c + g
                    act.wait_ge(s["s_full"].sem, s["s_full"].by(b, n + 1))
                    if g == 0 and c >= 2:
                        act.wait_ge(s["z_full"].sem, s["z_full"].by(b, c - 1))
                    elif g == 0:
                        act.wait_ge(s["z_full"].sem, s["z_full"].by(b.prev(), TT - 1 + c))
                    nc.scalar.activation(pat[c % 2][:, g * GA:(g + 1) * GA, :].rearrange("p j q -> p (j q)"), S_BANKS[n % 2][:],
                                         ACT.Square, scale=1.0 / DA).then_inc(s["pat"].sem, 1)

            def act_fqT(b, c, turns):
                for k, turn in enumerate(turns):
                    act.wait_ge(passed, turn.full)
                    src = turn.to
                    if c == 3:
                        act.wait_ge(s["z_full"].sem, s["z_full"].by(b, c - 1))
                    else:
                        act.wait_ge(s["z_full"].sem, s["z_full"].by(b.prev()))
                    wide = 4 if k == 0 else FB - 4
                    nc.scalar.activation(fqT[(c + 1) % 2][:, 4 * k:4 * k + wide, :].rearrange("p k q -> p (k q)"), src[:, 0:wide * P],
                                         ACT.Copy).then_inc(s["fqT"].sem, 1)

            def act_zT(b, c):
                act.wait_ge(s["z_full"].sem, s["z_full"].by(b, c + 1))
                act.wait_ge(s["zo"].sem, s["zo"].by(b.prev()))
                nc.scalar.activation(zT[:, c * P:(c + 1) * P], B_Z[:, 0:P], ACT.Copy).then_inc(s["z"].sem, 1)

            def act_y1T(b, turn):
                act.wait_ge(passed, turn.full)
                src = turn.to
                act.wait_ge(s["acc"].sem, s["acc"].by(b.prev().prev()))
                nc.scalar.activation(y1T[b.parity][:], src[:], ACT.Copy).then_inc(s["y1T"].sem, 1)

            def act_gate(b):
                act.wait_ge(s["sh"].sem, s["sh"].by(b))
                act.wait_ge(s["gs"].sem, s["gs"].by(b.prev()))
                nc.scalar.activation(ge[:], sh[:], ACT.Exp).then_inc(s["ge"].sem, 1)

            def act_wT(b, turn):
                act.wait_ge(passed, turn.full)
                src = turn.to
                act.wait_ge(s["ym"].sem, s["ym"].by(b.prev()))
                nc.scalar.activation(wT[:], src[0:TT * E, 0:P], ACT.Copy).then_inc(s["wT"].sem, 1)

            def body(b, names):
                def T(name):
                    return Turn(b, names, name)

                n, more = b.next(), names is TURNS
                act_square(b, 0)
                act_wT(b, T("wT"))
                act_fqT(b, 1, (T("fq1a"), T("fq1b")))
                if more:
                    act_xT(n, T("xT'"))
                act_zT(b, 0)
                act_square(b, 1)
                if more:
                    act_y1T(n, T("y1T'"))
                act_fqT(b, 2, (T("fq2a"), T("fq2b")))
                if more:
                    act_square_qk(n)
                act_zT(b, 1)
                act_square(b, 2)
                if more:
                    act_rsqrt(n)
                    act_gate(n)
                act_fqT(b, 3, (T("fq3a"), T("fq3b")))
                if more:
                    act_vm(n)
                act_zT(b, 2)
                act_square(b, 3)
                if more:
                    act_double(n)
                    act_qT(n, T("q'"))
                    act_kg(n, T("k'"))
                act_zT(b, 3)

            act.preload_act_table_set("natural_log_exp_and_others")
            act.wait_ge(zeroed.sem, zeroed.by(Batch(0, 0), 1))
            b0 = Batch(0, 0)
            act_xT(b0, Turn(b0, NEXT, "xT'"))
            act_y1T(b0, Turn(b0, NEXT, "y1T'"))
            act_square_qk(b0)
            act_vm(b0)
            act_rsqrt(b0)
            act_gate(b0)
            act_double(b0)
            act_qT(b0, Turn(b0, NEXT, "q'"))
            act_kg(b0, Turn(b0, NEXT, "k'"))
            body(Batch(0, 0), TURNS)
            with act.Fori(0, LASTB) as i:
                for o in (1, 2):
                    body(Batch(i, o), TURNS)
            body(Batch(LASTB, 1), LAST)

        @block.gpsimd
        def _(pool):
            def pool_mask(b, c):
                for g in range(GA):
                    pool.wait_ge(s["pat"].sem, s["pat"].by(b, GA * c + g + 1))
                    pool.sem_inc(alone, 1)
                    part = pat[c % 2][:, g * GA:(g + 1) * GA, :]
                    nc.gpsimd.affine_select(out=part, in_=part, compare_op=ALU.is_ge, fill=zero, base=0,
                                            pattern=[[0, GA], [1, P]], channel_multiplier=-1).then_inc(s["masked"].sem, 1)

            def pool_rstd(b):
                pool.wait_ge(s["mv"].sem, s["mv"].by(b))
                pool.wait_ge(s["xn"].sem, s["xn"].by(b.prev()))
                nc.gpsimd.tensor_tensor(rstd[:], mv[:, :, 1], lneps[:], ALU.add).then_inc(s["veps"].sem, 1)
                pool.wait_ge(s["veps"].sem, s["veps"].by(b))
                nc.gpsimd.tensor_tensor(rstd[:], rstd[:], mhalf[:], ALU.pow).then_inc(s["rstd"].sem, 1)

            def pool_newton(b):
                pool.wait_ge(s["ms"].sem, s["ms"].by(b))
                pool.sem_inc(alone, 1)
                nc.gpsimd.tensor_scalar(va[:], ms[:], 1.0 / DA, RMS_EPS, ALU.mult, ALU.add).then_inc(s["va"].sem, 1)
                pool.wait_ge(s["r0"].sem, s["r0"].by(b))
                nc.gpsimd.tensor_tensor(ra[:], r0[:], r0[:], ALU.mult).then_inc(s["ra"].sem, 1)
                pool.wait_ge(s["va"].sem, s["va"].by(b))
                pool.wait_ge(s["ra"].sem, s["ra"].by(b))
                nc.gpsimd.tensor_tensor(rb[:], ra[:], va[:], ALU.mult).then_inc(s["rb"].sem, 1)
                pool.wait_ge(s["rb"].sem, s["rb"].by(b))
                pool.sem_inc(alone, 1)
                nc.gpsimd.tensor_scalar(rc[:], rb[:], -0.5, 1.5, ALU.mult, ALU.add).then_inc(s["rc"].sem, 1)
                pool.wait_ge(s["rc"].sem, s["rc"].by(b))
                pool.wait_ge(s["qn"].sem, s["qn"].by(b.prev()))
                nc.gpsimd.tensor_tensor(rr[:], rc[:], r0[:], ALU.mult).then_inc(s["rr"].sem, 1)

            def pool_cos(b):
                pool.wait_ge(s["qn"].sem, s["qn"].by(b))
                pool.wait_ge(s["qr"].sem, s["qr"].by(b.prev()))
                for c in range(TT):
                    nc.gpsimd.tensor_tensor(t1[:, c], qn[:, c], rope[:, 0, c, :].unsqueeze(1).broadcast_to([P, H2, DA]), ALU.mult).then_inc(s["t1"].sem, 1)

            def pool_rstd2(b):
                pool.wait_ge(s["mv2"].sem, s["mv2"].by(b))
                pool.wait_ge(s["z2"].sem, s["z2"].by(b.prev()))
                nc.gpsimd.tensor_tensor(rstd2[:], mv2[:, :, 1], lneps[:], ALU.add).then_inc(s["veps2"].sem, 1)
                pool.wait_ge(s["veps2"].sem, s["veps2"].by(b))
                nc.gpsimd.tensor_tensor(rstd2[:], rstd2[:], mhalf[:], ALU.pow).then_inc(s["rstd2"].sem, 1)

            def pool_gain(b):
                pool.wait_ge(s["z2"].sem, s["z2"].by(b))
                pool.wait_ge(s["outs"].sem, s["outs"].by(b.prev()))
                nc.gpsimd.tensor_tensor(zg[:], z[:], ln[:, 2, :].unsqueeze(1).broadcast_to([P, TT, D]), ALU.mult).then_inc(s["zg"].sem, 1)

            def body(b, more=True, before=True):
                n, p = b.next(), b.prev()
                if more:
                    pool_rstd(n)
                if before:
                    pool_rstd2(p)
                pool_mask(b, 0)
                if before:
                    pool_gain(p)
                pool_mask(b, 1)
                pool_mask(b, 2)
                if more:
                    pool_newton(n)
                    pool_cos(n)
                pool_mask(b, 3)

            for i in two:
                nc.gpsimd.memset(vm[i][:], 0.0)
                last = nc.gpsimd.memset(kg[i][:], 0.0)
            last.then_inc(zeroed.sem, 1)
            pool.wait_ge(zeroed.sem, zeroed.by(Batch(0, 0), 1))
            zero = pool.to_reg(0.0)
            b0 = Batch(0, 0)
            pool_rstd(b0)
            pool_newton(b0)
            pool_cos(b0)
            body(Batch(0, 0), before=False)
            with pool.Fori(0, LASTB) as i:
                for o in (1, 2):
                    body(Batch(i, o))
            body(Batch(LASTB, 1), more=False)
            pool_rstd2(Batch(LASTB, 1))
            pool_gain(Batch(LASTB, 1))

        @block.vector
        def _(dve):
            def dve_stats(b):
                dve.wait_ge(x_loaded[b.parity], b.i * 16 + 16 * (b.off // 2 + 1))
                dve.wait_ge(s["veps"].sem, s["veps"].by(b.prev()))
                for c in range(TT):
                    nc.vector.bn_stats(stats[:, c, :], xs[b.parity][:, c, :]).then_inc(s["stats"].sem, 1)
                dve.wait_ge(s["stats"].sem, s["stats"].by(b))
                dve.sem_inc(alone, 1)
                for c in range(TT):
                    nc.vector.bn_aggr(mv[:, c, :], stats[:, c, :]).then_inc(s["mv"].sem, 1)

            def dve_xn(b):
                dve.wait_ge(s["rstd"].sem, s["rstd"].by(b))
                dve.wait_ge(s["xT"].sem, s["xT"].by(b.prev()))
                dve.wait_ge(s["xxn"].sem, s["xxn"].by(b.prev()))
                for c in range(TT):
                    nc.vector.tensor_scalar(xn[:, c, :], xs[b.parity][:, c, :], mv[:, c, 0:1], rstd[:, c:c + 1],
                                            ALU.subtract, ALU.mult).then_inc(s["xn"].sem, 1)

            def dve_res(b):
                dve.wait_ge(s["xn"].sem, s["xn"].by(b))
                dve.wait_ge(s["zo"].sem, s["zo"].by(b.prev().prev()))
                nc.vector.tensor_tensor(res[b.parity][:], xs[b.parity][:], xn[:], ALU.add).then_inc(s["xxn"].sem, 1)
                dve.wait_ge(s["xxn"].sem, s["xxn"].by(b))
                nc.vector.tensor_tensor(res[b.parity][:], res[b.parity][:], ln[:, 3, :].unsqueeze(1).broadcast_to([P, TT, D]),
                                        ALU.add).then_inc(s["res"].sem, 1)

            def dve_qkv(b, c, turn):
                dve.wait_ge(passed, turn.full)
                src = turn.to
                if c == 0:
                    dve.wait_ge(s["z_full"].sem, s["z_full"].by(b.prev().prev()))
                    dve.wait_ge(s["qr"].sem, s["qr"].by(b.prev().prev()))
                nc.vector.tensor_tensor(qkv[b.parity][:, c, :], src[:, 0:3 * D], bqkv[:], ALU.add).then_inc(s["qkv"].sem, 1)

            def dve_ms(b):
                dve.wait_ge(s["sq"].sem, s["sq"].by(b))
                dve.wait_ge(s["rr"].sem, s["rr"].by(b.prev()))
                nc.vector.tensor_reduce(ms[:], sq[:], AX, ALU.add).then_inc(s["ms"].sem, 1)

            def dve_qn(b):
                dve.wait_ge(s["rr"].sem, s["rr"].by(b))
                dve.wait_ge(s["qr"].sem, s["qr"].by(b.prev()))
                nc.vector.tensor_tensor(qn[:], qkv[b.parity][:, :, 0:2 * D].rearrange("p c (h d) -> p c h d", d=DA),
                                        rr[:].unsqueeze(3).broadcast_to([P, TT, H2, DA]), ALU.mult).then_inc(s["qn"].sem, 1)

            def dve_swap(b):
                dve.wait_ge(s["qn"].sem, s["qn"].by(b))
                for e in two:
                    nc.vector.tensor_tensor(t2[:, :, :, e::2], qn[:, :, :, 1 - e::2],
                                            rope[:, 1, :, e::2].unsqueeze(2).broadcast_to([P, TT, H2, DA // 2]), ALU.mult).then_inc(s["t2"].sem, 1)

            def dve_rope(b):
                dve.wait_ge(s["t2"].sem, s["t2"].by(b))
                dve.wait_ge(s["t1"].sem, s["t1"].by(b))
                dve.wait_ge(s["qd"].sem, s["qd"].by(b.prev()))
                dve.wait_ge(s["kg"].sem, s["kg"].by(b.prev()))
                dve.wait_ge(s["qT"].sem, s["qT"].by(b.prev()))
                nc.vector.tensor_tensor(qr[:].rearrange("p c (h d) -> p c h d", d=DA), t1[:], t2[:], ALU.add).then_inc(s["qr"].sem, 1)

            def dve_qm(b):
                dve.wait_ge(s["qT"].sem, s["qT"].by(b))
                dve.wait_ge(s["pat"].sem, s["pat"].by(b.prev().prev()))
                for j in range(GA):
                    nc.vector.tensor_scalar(qm[b.parity][:, j, :], qT[:], jmask[:, j:j + 1], None, ALU.mult).then_inc(s["qm"].sem, 1)

            def features(to, b, c, which):
                wide = H2 * (DA + OFF - 1)
                base = (c * H2 + which * HA) * (DA + OFF - 1)
                dims = [[TT * wide, P], [DA + OFF - 1, HA]]
                a0 = bass.AP(qd[b.parity], base, dims + [[0, OFF], [1, DA]])
                a1 = bass.AP(qd[b.parity], base, dims + [[1, OFF], [1, DA]])
                return nc.vector.tensor_tensor(to[:], a0, a1, ALU.mult)

            def dve_fk(b, c):
                dve.wait_ge(s["qd"].sem, s["qd"].by(b))
                if c == 2:
                    dve.wait_ge(s["st_full"].sem, s["st_full"].by(b, 1))
                else:
                    dve.wait_ge(s["st_full"].sem, s["st_full"].by(b.prev()))
                features(fk[c % 2], b, c, 1).then_inc(s["fk"].sem, 1)

            def dve_fq(b, c):
                dve.wait_ge(s["qd"].sem, s["qd"].by(b))
                if c == 3:
                    dve.wait_ge(s["fqT"].sem, s["fqT"].by(b, 2))
                else:
                    dve.wait_ge(s["fqT"].sem, s["fqT"].by(b.prev()))
                features(fq[(c + 1) % 2], b, c, 0).then_inc(s["fq"].sem, 1)

            def dve_state(b, c):
                dve.wait_ge(s["st_full"].sem, s["st_full"].by(b, c + 1))
                if c == 2:
                    dve.wait_ge(s["z_full"].sem, s["z_full"].by(b, 2))
                else:
                    dve.wait_ge(s["z_full"].sem, s["z_full"].by(b.prev()))
                nc.vector.tensor_tensor(state[c % 2][:, 0:4, :], ST_A[:].rearrange("p (k d) -> p k d", k=4), featw[:, 0:4, :], ALU.mult)\
                    .then_inc(s["state"].sem, 1)
                nc.vector.tensor_tensor(state[c % 2][:, 4, :], ST_B[:, 0:P], featw[:, 4, :], ALU.mult).then_inc(s["state"].sem, 1)

            def dve_gate(b, turn):
                dve.wait_ge(passed, turn.full)
                src = turn.to
                dve.wait_ge(s["sh"].sem, s["sh"].by(b.prev()))
                nc.vector.tensor_copy(lg[:].rearrange("p c e -> p (c e)"), src[:, 0:TT * E]).then_inc(s["lg"].sem, 1)
                dve.wait_ge(s["lg"].sem, s["lg"].by(b))
                nc.vector.tensor_reduce(top[:], lg[:], AX, ALU.max).then_inc(s["top"].sem, 1)
                dve.wait_ge(s["top"].sem, s["top"].by(b))
                dve.wait_ge(s["ge"].sem, s["ge"].by(b.prev()))
                nc.vector.tensor_tensor(sh[:], lg[:], top[:].unsqueeze(2).broadcast_to([P, TT, E]), ALU.subtract).then_inc(s["sh"].sem, 1)
                dve.wait_ge(s["sh"].sem, s["sh"].by(b))
                nc.vector.scalar_tensor_tensor(out=pick[:], in0=sh[:], scalar=0.0, in1=first[:].unsqueeze(1).broadcast_to([P, TT, E]),
                                               op0=ALU.is_equal, op1=ALU.mult).then_inc(s["pick"].sem, 1)
                dve.wait_ge(s["pick"].sem, s["pick"].by(b))
                nc.vector.tensor_reduce(best[:], pick[:], AX, ALU.max).then_inc(s["best"].sem, 1)
                dve.wait_ge(s["best"].sem, s["best"].by(b))
                nc.vector.tensor_tensor(oh[:], pick[:], best[:].unsqueeze(2).broadcast_to([P, TT, E]), ALU.is_equal).then_inc(s["oh"].sem, 1)
                dve.wait_ge(s["oh"].sem, s["oh"].by(b))
                nc.vector.tensor_copy(ohb[:], oh[:]).then_inc(s["ohb"].sem, 1)

            def dve_gate_sum(b):
                dve.wait_ge(s["ge"].sem, s["ge"].by(b))
                nc.vector.tensor_reduce(gs[:], ge[:], AX, ALU.add).then_inc(s["gs"].sem, 1)
                dve.wait_ge(s["gs"].sem, s["gs"].by(b))
                nc.vector.reciprocal(gr[:], gs[:]).then_inc(s["gr"].sem, 1)

            def dve_rank(b, turn):
                dve.wait_ge(passed, turn.full)
                src = turn.to
                nc.vector.tensor_tensor(loc[:], src[:, 0:TT * E].rearrange("p (c e) -> p c e", c=TT),
                                        carry[:].unsqueeze(1).broadcast_to([P, TT, E]), ALU.add).then_inc(s["loc"].sem, 1)
                dve.wait_ge(s["loc"].sem, s["loc"].by(b))
                nc.vector.tensor_tensor(carry[:], src[:, TT * E:(TT + 1) * E], carry[:], ALU.add).then_inc(s["carry"].sem, 1)
                nc.vector.scalar_tensor_tensor(out=keep[:], in0=loc[:], scalar=float(CAP), in1=oh[:], op0=ALU.is_lt, op1=ALU.mult).then_inc(s["keep"].sem, 1)
                dve.wait_ge(s["keep"].sem, s["keep"].by(b))
                dve.wait_ge(s["gr"].sem, s["gr"].by(b))
                dve.wait_ge(s["acc"].sem, s["acc"].by(b.prev().prev()))
                nc.vector.tensor_tensor(w[b.parity][:], keep[:], gr[:].unsqueeze(2).broadcast_to([P, TT, E]), ALU.mult).then_inc(s["w"].sem, 1)

            def dve_expert(b, c, half, turn):
                dve.wait_ge(passed, turn.full)
                src = turn.to
                dve.wait_ge(s["w"].sem, s["w"].by(b))
                for k in range(E // 2):
                    e = half * (E // 2) + k
                    if e:
                        dve.wait_ge(s["acc"].sem, s["acc"].by(b, c * E + e))
                    else:
                        dve.wait_ge(s["z2"].sem, s["z2"].by(b.prev()))
                    prior = y1[b.parity][:, c, :] if e == 0 else acc[(e + 1) % 2][:, c, :]
                    nc.vector.scalar_tensor_tensor(out=acc[e % 2][:, c, :], in0=src[:, k * D:(k + 1) * D], scalar=w[b.parity][:, c, e:e + 1], in1=prior,
                                                   op0=ALU.mult, op1=ALU.add).then_inc(s["acc"].sem, 1)

            def dve_ln2(b, turn):
                dve.wait_ge(passed, turn.full)
                src = turn.to
                dve.wait_ge(s["acc"].sem, s["acc"].by(b))
                nc.vector.tensor_tensor(acc[0][:], acc[1][:], src[:].rearrange("p (c d) -> p c d", c=TT), ALU.add).then_inc(s["ym"].sem, 1)
                dve.wait_ge(s["ym"].sem, s["ym"].by(b))
                for c in range(TT):
                    nc.vector.bn_stats(stats2[:, c, :], acc[0][:, c, :]).then_inc(s["stats2"].sem, 1)
                dve.wait_ge(s["stats2"].sem, s["stats2"].by(b))
                dve.sem_inc(alone, 1)
                for c in range(TT):
                    nc.vector.bn_aggr(mv2[:, c, :], stats2[:, c, :]).then_inc(s["mv2"].sem, 1)

            def dve_norm2(b):
                dve.wait_ge(s["rstd2"].sem, s["rstd2"].by(b))
                dve.wait_ge(s["zg"].sem, s["zg"].by(b.prev()))
                for c in range(TT):
                    nc.vector.tensor_scalar(z[:, c, :], acc[0][:, c, :], mv2[:, c, 0:1], rstd2[:, c:c + 1], ALU.subtract, ALU.mult).then_inc(s["z2"].sem, 1)

            def dve_residual(b, turn):
                dve.wait_ge(passed, turn.full)
                dve.wait_ge(s["outs"].sem, s["outs"].by(b.prev()))
                nc.vector.tensor_tensor(zo[:], turn.to[:].rearrange("p (c d) -> p c d", c=TT), res[b.parity][:], ALU.add).then_inc(s["zo"].sem, 1)

            def dve_out(b):
                dve.wait_ge(s["zg"].sem, s["zg"].by(b))
                dve.wait_ge(s["zo"].sem, s["zo"].by(b))
                done = b.i * 16 + 16 * (b.off // 2)
                if not isinstance(b.i, int) or done > 0:
                    dve.wait_ge(stored[b.parity].sem, done + 1)
                nc.vector.tensor_tensor(outs[b.parity][:], zg[:], zo[:], ALU.add).then_inc(s["outs"].sem, 1)

            def body(b, names, before=True):
                def T(name):
                    return Turn(b, names, name)

                n, p, more = b.next(), b.prev(), names is TURNS
                if more:
                    dve_stats(n)
                if before:
                    dve_ln2(p, Turn(p, TURNS, "bias"))
                    dve_residual(p, Turn(p, TURNS, "out"))
                dve_fq(b, 1)
                dve_fk(b, 0)
                if more:
                    dve_xn(n)
                if before:
                    dve_norm2(p)
                dve_expert(b, 0, 0, T("y0a"))
                if before:
                    dve_out(p)
                dve_state(b, 0)
                dve_fk(b, 1)
                dve_fq(b, 2)
                dve_expert(b, 0, 1, T("y0b"))
                if more:
                    dve_qkv(n, 0, T("qkv'0"))
                    dve_qkv(n, 1, T("qkv'1"))
                    dve_res(n)
                dve_state(b, 1)
                dve_expert(b, 1, 0, T("y1a"))
                if more:
                    dve_qkv(n, 2, T("qkv'2"))
                    dve_qkv(n, 3, T("qkv'3"))
                dve_fk(b, 2)
                dve_fq(b, 3)
                dve_expert(b, 1, 1, T("y1b"))
                if more:
                    dve_ms(n)
                    dve_gate(n, T("lg'"))
                dve_expert(b, 2, 0, T("y2a"))
                dve_state(b, 2)
                if more:
                    dve_gate_sum(n)
                    dve_qn(n)
                    dve_swap(n)
                dve_expert(b, 2, 1, T("y2b"))
                if more:
                    dve_rank(n, T("rank'"))
                    dve_rope(n)
                dve_expert(b, 3, 0, T("y3a"))
                if more:
                    dve_qm(n)
                dve_expert(b, 3, 1, T("y3b"))

            dve.wait_ge(zeroed.sem, zeroed.by(Batch(0, 0), 1))
            b0 = Batch(0, 0)
            dve_stats(b0)
            dve_xn(b0)
            dve_res(b0)
            for c in range(TT):
                dve_qkv(b0, c, Turn(b0, NEXT, f"qkv'{c}"))
            dve_ms(b0)
            dve_gate(b0, Turn(b0, NEXT, "lg'"))
            dve_gate_sum(b0)
            dve_qn(b0)
            dve_swap(b0)
            dve_rank(b0, Turn(b0, NEXT, "rank'"))
            dve_rope(b0)
            dve_qm(b0)
            body(Batch(0, 0), TURNS, before=False)
            with dve.Fori(0, LASTB) as i:
                for o in (1, 2):
                    body(Batch(i, o), TURNS)
            last_b = Batch(LASTB, 1)
            body(last_b, LAST)
            dve_ln2(last_b, Turn(last_b, LAST, "bias"))
            dve_residual(last_b, Turn(last_b, LAST, "out"))
            dve_norm2(last_b)
            dve_out(last_b)


def constants():
    pos = np.arange(NS, dtype=np.float32)
    inv = np.float32(1.0) / np.float32(10000.0) ** (np.arange(0, DA, 2, dtype=np.float32) / np.float32(DA))
    ang = np.outer(pos, inv.astype(np.float32)).astype(np.float32)
    ang = np.concatenate([ang, ang], -1)
    cos, sin = np.cos(ang), np.sin(ang)
    sin[:, 0::2] *= -1
    trig = np.stack([cos, sin]).reshape(2, TT, P, DA).transpose(2, 0, 1, 3)
    row, col = np.arange(P)[:, None], np.arange(P)[None, :]
    f = np.arange(FB * P)
    weight = np.array([1, 2, 2, 2, 1], np.float32)[(f // DA) % OFF] / DA ** 2
    featw = (f[:, None] // (OFF * DA) == col // DA) * weight[:, None]
    return {
        "c_ident": np.eye(P, dtype=np.float32),
        "c_trig": np.ascontiguousarray(trig, dtype=np.float32),
        "c_featw": np.ascontiguousarray(featw.reshape(FB, P, P).transpose(1, 0, 2), dtype=np.float32),
        "c_jmask": (row // DA % GA == np.arange(GA)[None, :]).astype(np.float32),
        "c_blockmask": np.where(row // LB % 2 == np.arange(32)[None, :] // LB, 0.0, NEG).astype(np.float32),
        "c_upper": (row < col).astype(mybir.dt.np(BF16)),
        "c_first": np.broadcast_to(E - np.arange(E), (P, E)).astype(np.float32).copy(),
        "c_tmask": (np.arange(TT * E)[:, None] // E == np.arange(TT)[None, :]).astype(np.float32),
    }


_INS = ["attn_x", "attn_Wq", "attn_bq", "attn_Wk", "attn_bk", "attn_Wv", "attn_bv", "attn_Wo", "attn_norm_w",
        "ffn_in_proj_w", "ffn_in_proj_b", "ffn_out_proj_w", "ffn_out_proj_b", "ffn_ln1_g", "ffn_ln1_b",
        "ffn_ln2_g", "ffn_ln2_b", "ffn_wg", "ffn_w1", "ffn_b1", "ffn_w2", "ffn_b2"]


def laid_out(inputs):
    g = {n.split("_", 1)[1]: np.asarray(inputs["L0_" + n]) for n in _INS}
    fc = FF // P
    arrays = {
        "x": g["x"], "wg": g["wg"], "b2": g["b2"],
        "wqkvT": np.concatenate([g["Wq"].T, g["Wk"].T, g["Wv"].T], 1), "woT": g["Wo"].T,
        "ipT": g["in_proj_w"].T, "opT": g["out_proj_w"].T, "bcol": np.concatenate([g["in_proj_b"], g["out_proj_b"]]).reshape(4, P).T,
        "w1T": g["w1"].reshape(E, D, fc, P).transpose(3, 0, 2, 1), "w2": g["w2"].reshape(E, fc, P, D).transpose(2, 0, 1, 3),
        "b1T": g["b1"].reshape(E, fc, P).transpose(2, 0, 1),
    }
    for n in ("bq", "bk", "bv", "norm_w", "ln1_g", "ln1_b", "ln2_g", "ln2_b"):
        arrays[n] = g[n]
    arrays = {n: np.ascontiguousarray(a) for n, a in arrays.items()}
    arrays.update(constants())
    return arrays


SCRATCH = (("y1", (LB, NS, D)),)


def kernel(**inputs):
    import concourse.bacc as _bacc
    from concourse.bass_utils import run_bass_kernel_spmd as _run

    nc = _bacc.Bacc("TRN2", target_bir_lowering=False, num_devices=1)
    arrays = {n + "_dram": a for n, a in laid_out(inputs).items()}
    t = {n.removesuffix("_dram"): nc.dram_tensor(n, a.shape, mybir.dt.from_np(a.dtype), kind="ExternalInput").ap() for n, a in arrays.items()}
    t["out"] = nc.dram_tensor("out_dram", (LB, NS, D), F32, kind="ExternalOutput").ap()
    for n, shape in SCRATCH:
        t[n] = nc.dram_tensor(n + "_scratch", shape, F32, kind="Internal").ap()
    build(nc, t)
    r = _run(nc, [arrays], core_ids=[0])
    return r.results[0]["out_dram"]
```

```python
from contextlib import ExitStack

import numpy as np

import concourse.bass as bass
from concourse import mybir

ALU = mybir.AluOpType
ACT = mybir.ActivationFunctionType
F32 = mybir.dt.float32
BF16 = mybir.dt.bfloat16
AX = mybir.AxisListType.X

P = 128
D = 128
LB, NS = 16, 512
TT = 4
NB = LB * NS // (TT * P)
HA, DA = 16, 8
HB, DB = 4, 32
ST = 32
GA = 4
OFF = 5
FB = HA * OFF * DA // P
E, FF = 8, 512
CAP = LB * NS // E
LN_EPS = 1e-5
RMS_EPS = float(np.finfo(np.float32).eps)
NEG = -1e30


class Batch:

    def __init__(self, i, off):
        self.i, self.off = i, off

    def next(self, n=1):
        return Batch(self.i, self.off + n)

    def prev(self):
        return Batch(self.i, self.off - 1)

    @property
    def number(self):
        return self.i * 2 + self.off

    @property
    def parity(self):
        return self.off % 2


class Signal:

    def __init__(self, sem, per):
        self.sem, self.per = sem, per

    def by(self, b, n=None):
        const = b.off * self.per + (self.per if n is None else n) + 1
        if isinstance(b.i, int):
            return max(b.i * 2 * self.per + const, 1)
        assert const >= 1, "a wait below one"
        return b.i * (2 * self.per) + const


class Phase:
    pass


def start(eng, signals):
    for sig in signals:
        eng.sem_inc(sig.sem, 1)


PACKS = {
    "early": [("ident", (P,)), ("ipT", (3 * D,)), ("opT", (D,)), ("bcol", (4,)), ("blockmask", (32,))],
    "wide": [("ln", (4, D)), ("bqkv", (3 * D,)), ("norm_w", (DA,))],
    "weights": [("wqkvT", (3 * D,)), ("woT", (D,)), ("wg", (E,)), ("trig", (2, TT, DA)), ("featw", (FB, D)), ("jmask", (GA,)), ("revmask", (P,)),
                ("first", (E,)), ("b1T", (E, FF // P))],
}


def packs(sb, t):
    parts, loads = {}, []
    for pack, rows in PACKS.items():
        size = sum(int(np.prod(shape)) for _, shape in rows)
        whole = sb("pack_" + pack, [P, size])
        src = t["pack_" + pack]
        loads.append((whole[:], src.rearrange("(a n) -> a n", a=1).broadcast_to([P, size]) if pack == "wide" else src))
        at = 0
        for name, shape in rows:
            n = int(np.prod(shape))
            view = whole[:, at:at + n]
            if len(shape) == 2:
                view = view.rearrange("p (a b) -> p a b", a=shape[0])
            if len(shape) == 3:
                view = view.rearrange("p (a b c) -> p a b c", a=shape[0], b=shape[1])
            parts[name] = view
            at += n
    return parts, loads


def build(nc, t):
    ctx = ExitStack()
    with ctx:
        def sb(name, shape, dt=F32):
            return ctx.enter_context(nc.sbuf_tensor(name, shape, dt))

        def sem(name):
            return ctx.enter_context(nc.semaphore(name))

        bank = [ctx.enter_context(nc.psum_tensor(f"bank{i}", [P, 512], F32)) for i in range(8)]
        loaded, loads = packs(sb, t)
        ident = loaded["ident"]
        wqkvT = loaded["wqkvT"]
        woT = loaded["woT"]
        ipT = loaded["ipT"]
        opT = loaded["opT"]
        mexp = sb("mexp", [P, E * D])
        cpad = sb("cpad", [TT * E, TT, D])
        wg = loaded["wg"]
        bqkv = loaded["bqkv"]
        bcol = loaded["bcol"]
        pbcol = sb("pbcol", [P, 1])
        ln = loaded["ln"]
        nw = loaded["norm_w"]
        trig = loaded["trig"]
        b1T = loaded["b1T"]
        rope = sb("rope", [P, 2, TT, DA])
        featw = loaded["featw"]
        jmask = loaded["jmask"]
        revmask = loaded["revmask"]
        blockmask = loaded["blockmask"]
        upper = sb("upper", [P, P], BF16)
        ones = sb("ones", [P, P], BF16)
        first = loaded["first"]
        mhalf = sb("mhalf", [P, TT])
        lneps = sb("lneps", [P, TT])
        b2m = sb("b2m", [TT * E, D + TT])
        eps = sb("eps", [P, 1])
        carry = sb("carry", [P, E])

        everything, lasting = locals(), ctx
        ctx = early = ExitStack()
        with early:
            everything["sb"] = lambda name, shape, dt=F32: early.enter_context(nc.sbuf_tensor(name, shape, dt))
            everything["sem"] = lambda name: lasting.enter_context(nc.semaphore(name))
            soft = softmax_attention(nc, t, bank, everything)
            prep = preparation(nc, t, bank, everything)
        everything["sb"] = lambda name, shape, dt=F32: lasting.enter_context(nc.sbuf_tensor(name, shape, dt))
        squared = squared_attention_and_experts(nc, t, bank, everything)
        program(nc, lasting.enter_context(nc.Block()), prep, soft, squared)


def program(nc, block, prep, soft, squared):
    Turn, TURNS, AHEAD, LAST = squared.Turn, squared.TURNS, squared.AHEAD, squared.LAST
    two = range(2)
    b0 = Batch(0, 0)
    IN_LOOP = (NB - 4) // 2
    after_loop = [Batch(0, o) for o in range(2 * IN_LOOP + 1, NB + 1)]
    LASTB = NB // 2 - 1

    def T(name):
        return Turn(b0, AHEAD, name)

    @block.sync
    def _(sp):
        soft.load(Batch(0, 0))
        soft.load(Batch(0, 1))
        start(sp, [*soft.signals, *squared.signals])
        for o in range(2, 6):
            soft.load(Batch(0, o))
        with sp.Fori(0, NB // 2 - 3) as i:
            for o in two:
                soft.load(Batch(i, o + 6))
                soft.store(Batch(i, o))
        for o in two:
            squared.load_x(Batch(0, o))
        for o in range(NB - 6, NB - 2):
            soft.store(Batch(0, o))
        squared.turn_strips(b0)
        for o in range(NB - 2, NB):
            soft.store(Batch(0, o))
        soft.all_stored()
        for o in two:
            squared.load_y1(Batch(0, o))
        with sp.Fori(0, LASTB) as i:
            for o in two:
                squared.load_x(Batch(i, o + 2))
                squared.turn_strips(Batch(i, o + 1))
                squared.load_y1(Batch(i, o + 2))
                squared.store(Batch(i, o))
        squared.turn_strips(Batch(LASTB, 1))
        for o in two:
            squared.store(Batch(LASTB, o))
        squared.all_stored()

    @block.tensor
    def _(pe):
        prep.first_in(pe)
        soft.zeros_in(pe)
        prep.pe_column()
        soft.pe_step(Batch(0, -3))
        soft.pe_step(Batch(0, -2))
        soft.pe_step(Batch(0, -1))
        prep.rest_in(pe)
        prep.pe_experts()
        soft.pe_step(b0)
        with pe.Fori(0, IN_LOOP) as i:
            for o in (1, 2):
                soft.pe_step(Batch(i, o))
        s13, s14, s15, s16 = after_loop
        soft.pe_step(s13)
        soft.q_bank_free(pe)
        prep.pe_expert_bias(0, 2)
        soft.k_bank_free(pe)
        squared.pe_xT(b0, T("xT'"))
        soft.scores(s15)
        prep.pe_expert_bias(2, 1)
        soft.v_bank_free(pe)
        squared.pe_qkv(b0, 0, T("qkv'0"))
        soft.values(s14)
        soft.s_bank_free(pe)
        squared.pe_qkv(b0, 1, T("qkv'1"))
        squared.pe_qkv(b0, 2, T("qkv'2"))
        soft.output(s14)
        squared.pe_qkv(b0, 3, T("qkv'3"))
        prep.pe_expert_bias(3, E - 3)
        soft.pe_step(s15)
        prep.tables_in(pe)
        squared.pe_turn_qk(b0, 0, T("q'"))
        squared.pe_turn_qk(b0, 1, T("k'"))
        squared.scores_zeroed(pe)
        squared.pe_scores(b0, 0, 0)
        squared.pe_y1T(b0, T("y1T'"))
        squared.pe_scores(b0, 0, 1)
        squared.pe_logits(b0, T("lg'"))
        squared.pe_state(b0, 0)
        squared.pe_scores(b0, 1, 0)
        squared.pe_rank(b0, T("rank'"))
        soft.banks_free(pe)
        squared.pe_body(b0, TURNS, begun=True)
        with pe.Fori(0, LASTB - 1) as i:
            for o in (1, 2):
                squared.pe_body(Batch(i, o), TURNS)
        squared.pe_body(Batch(LASTB, -1), TURNS)
        squared.pe_body(Batch(LASTB, 0), TURNS)
        squared.pe_body(Batch(LASTB, 1), LAST)

    @block.scalar
    def _(act):
        prep.act_loads()
        act.preload_act_table_set("natural_log_exp_and_others")
        prep.first_in(act)
        soft.zeros_in(act)
        for o in range(-3, 1):
            soft.act_step(Batch(0, o))
        with act.Fori(0, IN_LOOP) as i:
            for o in (1, 2):
                soft.act_step(Batch(i, o))
        squared.zeros_in(act)
        s13, s14, s15, s16 = after_loop
        soft.act_step(s13)
        squared.act_xT(b0, T("xT'"))
        soft.act_step(s14)
        squared.act_square_qk(b0)
        soft.copy_o(s15)
        squared.act_rsqrt(b0)
        soft.norm1(s14)
        soft.norm1(s15)
        squared.act_double(b0)
        squared.act_qT(b0, T("q'"))
        squared.act_kg(b0, T("k'"))
        squared.act_vm(b0, 0)
        squared.act_vm(b0, 2)
        soft.front_free(act)
        squared.act_square(b0, 0, 0)
        squared.act_y1T(b0, T("y1T'"))
        squared.act_square(b0, 0, 1)
        squared.act_gate(b0)
        squared.act_square(b0, 1, 0)
        soft.memory_free(act)
        squared.act_body(b0, TURNS, begun=True)
        with act.Fori(0, LASTB - 1) as i:
            for o in (1, 2):
                squared.act_body(Batch(i, o), TURNS)
        squared.act_body(Batch(LASTB, -1), TURNS)
        squared.act_body(Batch(LASTB, 0), TURNS)
        squared.act_body(Batch(LASTB, 1), LAST)

    @block.gpsimd
    def _(pool):
        zero = pool.to_reg(0.0)
        prep.pool_fill()
        soft.pool_zero()
        soft.zeros_in(pool)
        soft.pool_step(Batch(0, -3))
        soft.pool_step(Batch(0, -2))
        squared.pool_zero()
        soft.pool_step(Batch(0, -1))
        prep.rest_in(pool)
        soft.pool_step(b0)
        with pool.Fori(0, IN_LOOP) as i:
            for o in (1, 2):
                soft.pool_step(Batch(i, o))
        s13, s14, s15, s16 = after_loop
        squared.pool_rstd(b0)
        soft.pool_step(s13)
        soft.pool_step(s14)
        soft.norm_scale1(s14)
        squared.pool_newton(b0)
        soft.norm_scale1(s15)
        prep.tables_in(pool)
        squared.pool_cos(b0)
        squared.pool_xxn(b0)
        squared.pool_res(b0)
        squared.pool_rstd(Batch(0, 1))
        soft.front_free(pool)
        squared.pool_mask(b0, 0, 0, zero)
        squared.pool_mask(b0, 0, 1, zero)
        soft.memory_free(pool)
        squared.pool_body(b0, zero, before=False, begun=True)
        with pool.Fori(0, LASTB - 1) as i:
            for o in (1, 2):
                squared.pool_body(Batch(i, o), zero)
        squared.pool_body(Batch(LASTB, -1), zero)
        squared.pool_body(Batch(LASTB, 0), zero, more=1)
        last_b = Batch(LASTB, 1)
        squared.pool_body(last_b, zero, more=0)
        squared.pool_rstd2(last_b)
        squared.pool_gain(last_b)

    @block.vector
    def _(dve):
        prep.dve_zero()
        soft.zeros_in(dve)
        prep.first_in(dve)
        soft.dve_step(Batch(0, -3))
        prep.dve_column()
        soft.dve_step(Batch(0, -2))
        soft.dve_step(Batch(0, -1))
        prep.rest_in(dve)
        prep.dve_tables()
        prep.dve_experts()
        soft.dve_step(b0)
        with dve.Fori(0, IN_LOOP) as i:
            for o in (1, 2):
                soft.dve_step(Batch(i, o))
        s13, s14, s15, s16 = after_loop
        squared.dve_stats(b0)
        soft.dve_step(s13)
        squared.dve_xn(b0)
        soft.dve_step(s14)
        for c in range(TT):
            squared.dve_qkv(b0, c, T(f"qkv'{c}"))
        soft.dve_step(s15)
        prep.dve_expert_bias()
        squared.dve_ms(b0)
        squared.dve_zero_scores()
        prep.tables_in(dve)
        soft.norm_stats1(s15)
        soft.gain(s14, dve)
        squared.dve_qn(b0)
        soft.shift(s14, dve)
        squared.dve_swap(b0)
        soft.gain(s15, dve)
        soft.shift(s15, dve)
        squared.dve_rope(b0)
        squared.dve_qm(b0)
        squared.dve_stats(Batch(0, 1))
        soft.front_free(dve)
        squared.dve_fq(b0, 1)
        squared.dve_fk(b0, 0)
        squared.dve_xn(Batch(0, 1))
        squared.dve_fk(b0, 1)
        squared.dve_gate(b0, T("lg'"))
        squared.dve_gate_sum(b0)
        squared.dve_rank(b0, T("rank'"))
        soft.memory_free(dve)
        squared.dve_body(b0, TURNS, before=False, begun=True)
        with dve.Fori(0, LASTB - 1) as i:
            for o in (1, 2):
                squared.dve_body(Batch(i, o), TURNS)
        squared.dve_body(Batch(LASTB, -1), TURNS)
        squared.dve_body(Batch(LASTB, 0), TURNS, more=1)
        last_b = Batch(LASTB, 1)
        squared.dve_body(last_b, LAST, more=0)
        squared.dve_ym(last_b, Turn(last_b, LAST, "bias"))
        squared.dve_residual(last_b, Turn(last_b, LAST, "out"))
        squared.dve_stats2(last_b)
        squared.dve_norm2(last_b)
        squared.dve_out(last_b)


def preparation(nc, t, bank, m):
    opT, mexp, cpad, rope, nw, b2m, trig, b1T = (m[k] for k in ("opT", "mexp", "cpad", "rope", "nw", "b2m", "trig", "b1T"))
    pe, act, pool, dve = nc.tensor, nc.scalar, nc.gpsimd, nc.vector
    FC = FF // P
    sb, sem = m["sb"], m["sem"]
    w1T = sb("w1T", [P, E, FC, D])
    w2 = sb("w2", [P, E, FC, D])
    b1pad = sb("b1pad", [P, E, FC, TT * E])
    c32 = sb("c32", [TT * E, D])
    B_PB, B_C, B_M = bank[5], bank[1], bank[6:8]

    first_loaded, rest_loaded, experts_loaded = sem("first_loaded"), sem("rest_loaded"), sem("experts_loaded")
    b1pad_zeroed, rope_ready, b1pad_ready, pb_full, pb_ready = (
        sem(n) for n in ("b1pad_zeroed", "rope_ready", "b1pad_ready", "pb_full", "pb_ready"))
    m_full, m_read, c_full, c_ready, cpad_ready = (
        sem(n) for n in ("m_full", "m_read", "c_full", "c_ready", "cpad_ready"))

    early, *rest = m["loads"]
    rest += [(m["upper"][:], t["c_upper"]), (b2m[:], t["b2m"])]

    def act_loads():
        act.dma_start(*early).then_inc(first_loaded, 16)
        for to, src in rest:
            act.dma_start(to, src).then_inc(rest_loaded, 16)
        for e in range(0, E, 2):
            act.dma_start(w1T[:, e:e + 2], t["w1T"][:, e:e + 2]).then_inc(experts_loaded, 16)
            act.dma_start(w2[:, e:e + 2], t["w2"][:, e:e + 2]).then_inc(experts_loaded, 16)

    def first_in(eng):
        eng.wait_ge(first_loaded, 16)

    def rest_in(eng):
        eng.wait_ge(rest_loaded, 16 * len(rest))

    def pool_fill():
        nc.gpsimd.memset(m["mhalf"][:], -0.5)
        nc.gpsimd.memset(m["lneps"][:], LN_EPS)
        nc.gpsimd.memset(m["ones"][:], 1.0)
        nc.gpsimd.memset(m["eps"][:], RMS_EPS)
        nc.gpsimd.memset(m["carry"][:], 0.0)

    def pe_column():
        nc.tensor.matmul(B_PB[:, 0:1], opT[:], m["bcol"][:, 2:3], start=True, stop=True).then_inc(pb_full, 1)

    def dve_column():
        dve.wait_ge(pb_full, 1)
        nc.vector.tensor_tensor(m["pbcol"][:], B_PB[:, 0:1], m["bcol"][:, 3:4], ALU.add).then_inc(pb_ready, 1)
        dve.wait_ge(pb_ready, 1)

    def pe_experts():
        for e in range(E):
            if e % 2 == 0:
                pe.wait_ge(experts_loaded, 16 * E)
            if e >= 2:
                pe.wait_ge(m_read, e - 1)
            for c in range(FC):
                last = nc.tensor.matmul(B_M[e % 2][:, 0:D], w1T[:, e, c, :], w2[:, e, c, :],
                                        start=(c == 0), stop=(c == FC - 1))
            last.then_inc(m_full, 1)
        pe.wait_ge(m_read, E)
        pe.wait_ge(pb_ready, 1)

    def pe_expert_bias(first, count):
        pe.wait_ge(b1pad_ready, E)
        for e in range(first, first + count):
            for c in range(FC):
                last = nc.tensor.matmul(B_C[0:TT * E, 0:D], b1pad[:, e, c, :], w2[:, e, c, :],
                                        start=(e == 0 and c == 0), stop=(e == E - 1 and c == FC - 1))
        if first + count == E:
            last.then_inc(c_full, 1)

    def dve_zero():
        nc.vector.memset(b1pad[:], 0.0).then_inc(b1pad_zeroed, 1)

    def dve_tables():
        dve.wait_ge(b1pad_zeroed, 1)
        for e in range(E):
            nc.vector.tensor_copy(b1pad[:, e, :, e::E], b1T[:, e].unsqueeze(2).broadcast_to([P, FC, TT])).then_inc(b1pad_ready, 1)
        for c in range(TT):
            nc.vector.tensor_tensor(rope[:, 0, c, :], trig[:, 0, c, :], nw[:], ALU.mult).then_inc(rope_ready, 1)
            for h in range(2):
                nc.vector.tensor_tensor(rope[:, 1, c, h::2], trig[:, 1, c, h::2], nw[:, 1 - h::2], ALU.mult).then_inc(rope_ready, 1)

    def dve_experts():
        for e in range(E):
            dve.wait_ge(m_full, e + 1)
            nc.vector.tensor_copy(mexp[:, e * D:(e + 1) * D], B_M[e % 2][:, 0:D]).then_inc(m_read, 1)

    def dve_expert_bias():
        dve.wait_ge(c_full, 1)
        nc.vector.tensor_tensor(c32[:], B_C[0:TT * E, 0:D], b2m[:, 0:D], ALU.add).then_inc(c_ready, 1)
        dve.wait_ge(c_ready, 1)
        for i in range(TT):
            nc.vector.tensor_scalar(cpad[:, i, :], c32[:], b2m[:, D + i:D + i + 1], None, ALU.mult).then_inc(cpad_ready, 1)

    def tables_in(eng):
        eng.wait_ge(rope_ready, 3 * TT)
        eng.wait_ge(m_read, E)
        eng.wait_ge(cpad_ready, TT)

    phase = Phase()
    phase.act_loads = act_loads
    phase.first_in = first_in
    phase.rest_in = rest_in
    phase.pool_fill = pool_fill
    phase.pe_column = pe_column
    phase.dve_column = dve_column
    phase.pe_experts = pe_experts
    phase.dve_zero = dve_zero
    phase.dve_tables = dve_tables
    phase.pe_expert_bias = pe_expert_bias
    phase.dve_experts = dve_experts
    phase.dve_expert_bias = dve_expert_bias
    phase.tables_in = tables_in
    return phase


def softmax_attention(nc, t, bank, m):
    ident, ipT, opT, bcol, pbcol, ln, mhalf, lneps, blockmask = (
        m[k] for k in ("ident", "ipT", "opT", "bcol", "pbcol", "ln", "mhalf", "lneps", "blockmask"))
    x, y1_dram = t["x"], t["y1"]
    sb, sem = m["sb"], m["sem"]
    sp, pe, act, pool, dve = nc.sync, nc.tensor, nc.scalar, nc.gpsimd, nc.vector

    def sig(name, per=1):
        return Signal(sem(name), per)

    two = range(2)
    xs = [sb(f"xs{i}", [P, TT, D]) for i in two]
    stats = sb("stats", [P, TT, 6])
    mv = sb("mv", [P, TT, 2])
    rstd = sb("rstd", [P, TT])
    mr = sb("mr", [P, TT])
    nb = sb("nb", [P, TT])
    xn = sb("xn", [P, TT, D])
    xT = [sb(f"xT{i}", [P, TT * P]) for i in two]
    xb = [sb(f"xb{i}", [P, TT * P]) for i in two]
    qT = sb("qT", [P, TT * P])
    kTm = sb("kTm", [P, HB, TT * P])
    v = [sb(f"v{i}", [P, TT, D]) for i in two]
    sc = sb("sc", [P, TT * HB, 32])
    mx = sb("mx", [P, TT * HB])
    ex = sb("ex", [P, TT * HB, 32])
    sm = sb("sm", [P, TT * HB])
    rs = sb("rs", [P, TT * HB])
    pr = sb("pr", [P, TT * HB, 32])
    pT = sb("pT", [P, TT * HB, P])
    oT = sb("oT", [P, TT * P])
    stats1 = sb("stats1", [P, TT, 6])
    mv1 = sb("mv1", [P, TT, 2])
    rstd1 = sb("rstd1", [P, TT])
    mr1 = sb("mr1", [P, TT])
    nb1 = sb("nb1", [P, TT])
    none = sb("none", [P, TT])
    yn = sb("yn", [P, TT, D])
    yg = sb("yg", [P, TT, D])
    y1 = [sb(f"y1_{i}", [P, TT, D]) for i in two]

    x_loaded = [Signal(sem(f"a_x_loaded{i}"), 0) for i in two]
    stored = [Signal(sem(f"a_y1_stored{i}"), 0) for i in two]
    zeroed = sig("a_zeroed")
    alone = sem("a_alone")
    s = {n: sig("a_" + n, per) for n, per in dict(
        stats=TT, mv=TT, veps=1, rstd=1, mr=1, nb=1, xn=TT, xT_full=1, xT=1, xb=1, q_full=1, q=1, k_full=1, k=HB, v_full=1, v=1,
        sc_full=1, sc=1, mx=1, sub=1, ex=1, sm=1, rs=1, pr=1, pT=TT, o_full=1, o=1, y_full=1,
        stats1=TT, mv1=TT, veps1=1, rstd1=1, mr1=1, nb1=1, yn=TT, yg=1, y1=1).items()}

    xv = x.rearrange("l (g n t) d -> g n l (t d)", t=TT, n=8)
    yv = y1_dram.rearrange("l (g n t) d -> g n l (t d)", t=TT, n=8)
    B_XT, B_Q, B_K, B_V, B_S, B_O, B_Y = *bank[0:6], bank[6:8]

    def there(b):
        return not isinstance(b.i, int) or 0 <= b.number < NB

    def load(b):
        if not (isinstance(b.i, int) and b.number < 2):
            sp.wait_ge(s["xn"].sem, s["xn"].by(b.next(-2)))
        sp.dma_start(xs[b.parity][:].rearrange("p t d -> p (t d)"), xv[b.number]).then_inc(x_loaded[b.parity].sem, 16)

    def store(b):
        sp.wait_ge(s["y1"].sem, s["y1"].by(b))
        sp.dma_start(yv[b.number], y1[b.parity][:].rearrange("p t d -> p (t d)")).then_inc(stored[b.parity].sem, 16)

    def all_stored():
        for o in two:
            sp.wait_ge(stored[o].sem, 16 * (NB // 2) + 1)

    def turn_x(b):
        pe.wait_ge(s["xn"].sem, s["xn"].by(b))
        pe.wait_ge(s["xT"].sem, s["xT"].by(b.prev()))
        for c in range(TT):
            last = nc.tensor.transpose(B_XT[:, c * P:(c + 1) * P], xn[:, c, :], ident[:])
        last.then_inc(s["xT_full"].sem, 1)

    def project_qk(b):
        pe.wait_ge(s["xT"].sem, s["xT"].by(b))
        pe.wait_ge(s["q"].sem, s["q"].by(b.prev()))
        nc.tensor.matmul(B_Q[:], ipT[:, 0:D], xT[b.parity][:], start=True, stop=True).then_inc(s["q_full"].sem, 1)
        pe.wait_ge(s["k"].sem, s["k"].by(b.prev()))
        nc.tensor.matmul(B_K[:], ipT[:, D:2 * D], xT[b.parity][:], start=True, stop=True).then_inc(s["k_full"].sem, 1)

    def project_v(b):
        pe.wait_ge(s["v"].sem, s["v"].by(b.prev()))
        for c in range(TT):
            last = nc.tensor.matmul(B_V[:, c * D:(c + 1) * D], xT[b.parity][:, c * P:(c + 1) * P],
                                    ipT[:, 2 * D:3 * D], start=True, stop=True)
        last.then_inc(s["v_full"].sem, 1)

    def scores(b):
        pe.wait_ge(s["q"].sem, s["q"].by(b))
        pe.wait_ge(s["k"].sem, s["k"].by(b))
        pe.wait_ge(s["sc"].sem, s["sc"].by(b.prev()))
        for c in range(TT):
            for k in range(4):
                a = c * P + 32 * k
                last = nc.tensor.matmul(B_S[32 * k:32 * k + 32, c * P:(c + 1) * P], qT[:, a:a + 32],
                                        kTm[:, :, a:a + 32], start=True, stop=True)
        last.then_inc(s["sc_full"].sem, 1)

    def values(b):
        pe.wait_ge(s["v"].sem, s["v"].by(b))
        pe.wait_ge(s["pT"].sem, s["pT"].by(b))
        pe.wait_ge(s["o"].sem, s["o"].by(b.prev()))
        for c in range(TT):
            for h in range(HB):
                last = nc.tensor.matmul(B_O[32 * h:32 * h + 32, c * P:(c + 1) * P], v[b.parity][:, c, 32 * h:32 * h + 32],
                                        pT[:, c * HB + h, :], start=True, stop=True)
        last.then_inc(s["o_full"].sem, 1)

    def output(b):
        pe.wait_ge(s["o"].sem, s["o"].by(b))
        pe.wait_ge(s["xb"].sem, s["xb"].by(b))
        pe.wait_ge(s["yn"].sem, s["yn"].by(b.next(-2)))
        for c in range(TT):
            nc.tensor.matmul(B_Y[b.parity][:, c * D:(c + 1) * D], oT[:, c * P:(c + 1) * P], opT[:], start=True, stop=False)
            last = nc.tensor.matmul(B_Y[b.parity][:, c * D:(c + 1) * D], xb[b.parity][:, c * P:(c + 1) * P], ident[:],
                                    start=False, stop=True)
        last.then_inc(s["y_full"].sem, 1)

    def pe_step(b):
        if there(b.next(2)):
            turn_x(b.next(2))
        if there(b.next(1)):
            scores(b.next(1))
        if there(b.next(2)):
            project_qk(b.next(2))
        if there(b):
            values(b)
        if there(b.next(2)):
            project_v(b.next(2))
        if there(b):
            output(b)

    def copy_xT(b):
        act.wait_ge(s["xT_full"].sem, s["xT_full"].by(b))
        act.wait_ge(s["v_full"].sem, s["v_full"].by(b.next(-2)))
        act.wait_ge(s["xb"].sem, s["xb"].by(b.next(-2)))
        nc.scalar.activation(xT[b.parity][:], B_XT[:], ACT.Copy).then_inc(s["xT"].sem, 1)

    def copy_qk(b):
        act.wait_ge(s["q_full"].sem, s["q_full"].by(b))
        act.wait_ge(s["sc_full"].sem, s["sc_full"].by(b.prev()))
        nc.scalar.activation(qT[:], B_Q[:], ACT.Identity, bias=bcol[:, 0:1]).then_inc(s["q"].sem, 1)
        act.wait_ge(s["k_full"].sem, s["k_full"].by(b))
        for h in range(HB):
            r = slice(32 * h, 32 * h + 32)
            nc.scalar.activation(kTm[r, h, :], B_K[r, :], ACT.Identity, bias=bcol[r, 1:2]).then_inc(s["k"].sem, 1)

    def copy_v(b):
        act.wait_ge(s["v_full"].sem, s["v_full"].by(b))
        act.wait_ge(s["o_full"].sem, s["o_full"].by(b.next(-2)))
        nc.scalar.activation(v[b.parity][:].rearrange("p t d -> p (t d)"), B_V[:], ACT.Copy).then_inc(s["v"].sem, 1)

    def exps(b):
        act.wait_ge(s["sub"].sem, s["sub"].by(b))
        act.wait_ge(s["pr"].sem, s["pr"].by(b.prev()))
        nc.scalar.activation(ex[:].rearrange("p a k -> p (a k)"), sc[:].rearrange("p a k -> p (a k)"), ACT.Exp).then_inc(s["ex"].sem, 1)

    def copy_o(b):
        act.wait_ge(s["o_full"].sem, s["o_full"].by(b))
        act.wait_ge(s["y_full"].sem, s["y_full"].by(b.prev()))
        nc.scalar.activation(oT[:], B_O[:], ACT.Copy).then_inc(s["o"].sem, 1)

    def norm(b):
        act.wait_ge(s["nb"].sem, s["nb"].by(b))
        act.wait_ge(s["xT_full"].sem, s["xT_full"].by(b.prev()))
        for c in range(TT):
            nc.scalar.activation(xn[:, c, :], xs[b.parity][:, c, :], ACT.Identity, bias=nb[:, c:c + 1],
                                 scale=rstd[:, c:c + 1]).then_inc(s["xn"].sem, 1)

    def norm1(b):
        act.wait_ge(s["nb1"].sem, s["nb1"].by(b))
        act.wait_ge(s["yg"].sem, s["yg"].by(b.prev()))
        for c in range(TT):
            nc.scalar.activation(yn[:, c, :], B_Y[b.parity][:, c * D:(c + 1) * D], ACT.Identity, bias=nb1[:, c:c + 1],
                                 scale=rstd1[:, c:c + 1]).then_inc(s["yn"].sem, 1)

    def act_step(b):
        if there(b.next(2)):
            copy_xT(b.next(2))
        if there(b.next()):
            copy_v(b.next())
        if there(b.next(2)):
            copy_qk(b.next(2))
        if there(b.next()):
            exps(b.next())
        if there(b):
            copy_o(b)
        if there(b.next(3)):
            norm(b.next(3))
        if there(b.prev()):
            norm1(b.prev())

    def norm_scale(b):
        pool.wait_ge(s["mv"].sem, s["mv"].by(b))
        pool.wait_ge(s["xn"].sem, s["xn"].by(b.prev()))
        nc.gpsimd.tensor_tensor(rstd[:], mv[:, :, 1], lneps[:], ALU.add).then_inc(s["veps"].sem, 1)
        pool.wait_ge(s["veps"].sem, s["veps"].by(b))
        nc.gpsimd.tensor_tensor(rstd[:], rstd[:], mhalf[:], ALU.pow).then_inc(s["rstd"].sem, 1)
        pool.wait_ge(s["rstd"].sem, s["rstd"].by(b))
        nc.gpsimd.tensor_tensor(mr[:], mv[:, :, 0], rstd[:], ALU.mult).then_inc(s["mr"].sem, 1)
        pool.wait_ge(s["mr"].sem, s["mr"].by(b))
        nc.gpsimd.tensor_tensor(nb[:], none[:], mr[:], ALU.subtract).then_inc(s["nb"].sem, 1)

    def norm_scale1(b):
        pool.wait_ge(s["mv1"].sem, s["mv1"].by(b))
        pool.wait_ge(s["yn"].sem, s["yn"].by(b.prev()))
        nc.gpsimd.tensor_tensor(rstd1[:], mv1[:, :, 1], lneps[:], ALU.add).then_inc(s["veps1"].sem, 1)
        pool.wait_ge(s["veps1"].sem, s["veps1"].by(b))
        nc.gpsimd.tensor_tensor(rstd1[:], rstd1[:], mhalf[:], ALU.pow).then_inc(s["rstd1"].sem, 1)
        pool.wait_ge(s["rstd1"].sem, s["rstd1"].by(b))
        nc.gpsimd.tensor_tensor(mr1[:], mv1[:, :, 0], rstd1[:], ALU.mult).then_inc(s["mr1"].sem, 1)
        pool.wait_ge(s["mr1"].sem, s["mr1"].by(b))
        nc.gpsimd.tensor_tensor(nb1[:], none[:], mr1[:], ALU.subtract).then_inc(s["nb1"].sem, 1)

    def probs(b):
        pool.wait_ge(s["rs"].sem, s["rs"].by(b))
        pool.wait_ge(s["pT"].sem, s["pT"].by(b.prev()))
        nc.gpsimd.tensor_tensor(pr[:], ex[:], rs[:].unsqueeze(2).broadcast_to([P, TT * HB, 32]), ALU.mult).then_inc(s["pr"].sem, 1)

    def gain(b, eng):
        eng.wait_ge(s["yn"].sem, s["yn"].by(b))
        eng.wait_ge(s["y1"].sem, s["y1"].by(b.prev()))
        eng.tensor_tensor(yg[:], yn[:], ln[:, 0, :].unsqueeze(1).broadcast_to([P, TT, D]), ALU.mult).then_inc(s["yg"].sem, 1)

    def shift(b, eng):
        eng.wait_ge(s["yg"].sem, s["yg"].by(b))
        done = b.i * 16 + 16 * (b.off // 2)
        if not isinstance(b.i, int) or done > 0:
            eng.wait_ge(stored[b.parity].sem, done + 1)
        eng.tensor_tensor(y1[b.parity][:], yg[:], ln[:, 1, :].unsqueeze(1).broadcast_to([P, TT, D]), ALU.add).then_inc(s["y1"].sem, 1)

    def pool_step(b):
        if there(b.next(3)):
            norm_scale(b.next(3))
        if there(b.prev()):
            norm_scale1(b.prev())
        if there(b.next()):
            probs(b.next())
        if there(b.prev()):
            gain(b.prev(), pool)
            shift(b.prev(), pool)

    def pool_zero():
        nc.gpsimd.memset(none[:], 0.0)
        nc.gpsimd.memset(kTm[:], 0.0)
        nc.gpsimd.memset(pT[:], 0.0).then_inc(zeroed.sem, 1)

    def zeros_in(eng):
        eng.wait_ge(zeroed.sem, zeroed.by(Batch(0, 0)))

    def norm_stats(b):
        dve.wait_ge(x_loaded[b.parity].sem, b.i * 16 + 16 * (b.off // 2 + 1))
        dve.wait_ge(s["mr"].sem, s["mr"].by(b.prev()))
        for c in range(TT):
            nc.vector.bn_stats(stats[:, c, :], xs[b.parity][:, c, :]).then_inc(s["stats"].sem, 1)
        dve.wait_ge(s["stats"].sem, s["stats"].by(b))
        dve.sem_inc(alone, 1)
        for c in range(TT):
            nc.vector.bn_aggr(mv[:, c, :], stats[:, c, :]).then_inc(s["mv"].sem, 1)

    def copy_xb(b):
        dve.wait_ge(s["xT"].sem, s["xT"].by(b))
        dve.wait_ge(s["y_full"].sem, s["y_full"].by(b.next(-2)))
        nc.vector.tensor_scalar(xb[b.parity][:], xT[b.parity][:], pbcol[:], None, ALU.add).then_inc(s["xb"].sem, 1)

    def norm_stats1(b):
        dve.wait_ge(s["y_full"].sem, s["y_full"].by(b))
        dve.wait_ge(s["mr1"].sem, s["mr1"].by(b.prev()))
        for c in range(TT):
            nc.vector.bn_stats(stats1[:, c, :], B_Y[b.parity][:, c * D:(c + 1) * D]).then_inc(s["stats1"].sem, 1)
        dve.wait_ge(s["stats1"].sem, s["stats1"].by(b))
        dve.sem_inc(alone, 1)
        for c in range(TT):
            nc.vector.bn_aggr(mv1[:, c, :], stats1[:, c, :]).then_inc(s["mv1"].sem, 1)

    def softmax_top(b):
        dve.wait_ge(s["sc_full"].sem, s["sc_full"].by(b))
        dve.wait_ge(s["ex"].sem, s["ex"].by(b.prev()))
        nc.vector.scalar_tensor_tensor(out=sc[:], in0=B_S[:].rearrange("p (a k) -> p a k", k=32), scalar=float(DB) ** -0.5,
                                       in1=blockmask[:].unsqueeze(1).broadcast_to([P, TT * HB, 32]),
                                       op0=ALU.mult, op1=ALU.add).then_inc(s["sc"].sem, 1)
        dve.wait_ge(s["sc"].sem, s["sc"].by(b))
        nc.vector.tensor_reduce(mx[:], sc[:], AX, ALU.max).then_inc(s["mx"].sem, 1)
        dve.wait_ge(s["mx"].sem, s["mx"].by(b))
        nc.vector.tensor_tensor(sc[:], sc[:], mx[:].unsqueeze(2).broadcast_to([P, TT * HB, 32]), ALU.subtract).then_inc(s["sub"].sem, 1)

    def softmax_sum(b):
        dve.wait_ge(s["ex"].sem, s["ex"].by(b))
        nc.vector.tensor_reduce(sm[:], ex[:], AX, ALU.add).then_inc(s["sm"].sem, 1)
        dve.wait_ge(s["sm"].sem, s["sm"].by(b))
        dve.wait_ge(s["pr"].sem, s["pr"].by(b.prev()))
        nc.vector.reciprocal(rs[:], sm[:]).then_inc(s["rs"].sem, 1)

    def turn_probs(b):
        dve.wait_ge(s["pr"].sem, s["pr"].by(b))
        dve.wait_ge(s["o_full"].sem, s["o_full"].by(b.prev()))
        for k in range(4):
            r = slice(32 * k, 32 * k + 32)
            nc.vector.transpose(pT[r, :, r], pr[r, :, :]).then_inc(s["pT"].sem, 1)

    def dve_step(b):
        if there(b.next(3)):
            norm_stats(b.next(3))
        if there(b.next()):
            copy_xb(b.next())
        if there(b):
            turn_probs(b)
        if there(b.next()):
            softmax_top(b.next())
        if there(b.prev()):
            norm_stats1(b.prev())
        if there(b.next()):
            softmax_sum(b.next())

    def k_bank_free(eng):
        eng.wait_ge(s["k"].sem, s["k"].by(Batch(0, NB - 1)))

    def q_bank_free(eng):
        eng.wait_ge(s["q"].sem, s["q"].by(Batch(0, NB - 1)))

    def v_bank_free(eng):
        eng.wait_ge(s["v"].sem, s["v"].by(Batch(0, NB - 1)))

    def s_bank_free(eng):
        eng.wait_ge(s["sc"].sem, s["sc"].by(Batch(0, NB - 1)))

    def front_free(eng):
        eng.wait_ge(s["y_full"].sem, s["y_full"].by(Batch(0, NB - 1)))

    def banks_free(eng):
        eng.wait_ge(s["yn"].sem, s["yn"].by(Batch(0, NB - 1)))

    def memory_free(eng):
        eng.wait_ge(s["y1"].sem, s["y1"].by(Batch(0, NB - 1)))
        for o in two:
            eng.wait_ge(stored[o].sem, 16 * (NB // 2) + 1)

    phase = Phase()
    phase.signals = [*s.values(), zeroed, *stored]
    phase.load = load
    phase.store = store
    phase.all_stored = all_stored
    phase.pe_step = pe_step
    phase.act_step = act_step
    phase.pool_step = pool_step
    phase.dve_step = dve_step
    phase.pool_zero = pool_zero
    phase.zeros_in = zeros_in
    phase.banks_free = banks_free
    phase.k_bank_free = k_bank_free
    phase.q_bank_free = q_bank_free
    phase.v_bank_free = v_bank_free
    phase.s_bank_free = s_bank_free
    phase.front_free = front_free
    phase.scores = scores
    phase.values = values
    phase.output = output
    phase.norm_stats1 = norm_stats1
    phase.norm_scale1 = norm_scale1
    phase.copy_o = copy_o
    phase.norm1 = norm1
    phase.gain = gain
    phase.shift = shift
    phase.memory_free = memory_free
    return phase


def squared_attention_and_experts(nc, t, bank, m):
    ident, wqkvT, woT, mexp, cpad, wg, bqkv, ln, rope, featw, jmask = (
        m[k] for k in ("ident", "wqkvT", "woT", "mexp", "cpad", "wg", "bqkv", "ln", "rope", "featw", "jmask"))
    revmask = m["revmask"]
    upper, ones, first, mhalf, lneps, eps, carry = (m[k] for k in ("upper", "ones", "first", "mhalf", "lneps", "eps", "carry"))
    x, y1_dram, out = t["x"], t["y1"], t["out"]
    H2 = 2 * HA
    W = OFF * DA
    sb, sem = m["sb"], m["sem"]
    sp, pe, act, pool, dve = nc.sync, nc.tensor, nc.scalar, nc.gpsimd, nc.vector
    two = range(2)
    pat = [sb(f"pat{i}", [P, HA, P]) for i in two]
    fk = [sb(f"fk{i}", [P, HA, OFF, DA]) for i in two]
    fq = [sb(f"fq{i}", [P, HA, OFF, DA]) for i in two]
    fqT = [sb(f"fqT{i}", [P, FB, P]) for i in two]
    state = [sb(f"state{i}", [P, FB, D]) for i in two]
    y1 = [sb(f"b_y1_{i}", [P, TT, D]) for i in two]
    y1T = [sb(f"y1T{i}", [P, TT * P]) for i in two]
    acc = [sb(f"acc{i}", [P, TT, D]) for i in two]
    z = sb("z", [P, TT, D])
    zg = sb("zg", [P, TT, D])
    zo = sb("zo", [P, TT, D])
    outs = [sb(f"outs{i}", [P, TT, D]) for i in two]
    sq = sb("sq", [P, TT, H2, DA])
    qn = sb("qn", [P, TT, H2, DA])
    t1 = sb("t1", [P, TT, H2, DA])
    t2 = sb("t2", [P, TT, H2, DA])
    qr = sb("qr", [P, TT, 2 * D])
    qT = sb("b_qT", [P, TT * P])
    qm = [sb(f"qm{i}", [P, GA, TT * P]) for i in two]
    qd = [sb(f"qd{i}", [P, TT, H2, DA + OFF - 1]) for i in two]
    vm = [sb(f"vm{i}", [P, TT, HA, 32]) for i in two]
    vrev = sb("vrev", [P, TT, D // 2])
    kg = [sb(f"kg{i}", [P, GA, TT * P]) for i in two]
    xs = [sb(f"b_xs{i}", [P, TT, D]) for i in two]
    stats, mv, rstd = sb("b_stats", [P, TT, 6]), sb("b_mv", [P, TT, 2]), sb("b_rstd", [P, TT])
    xn = sb("b_xn", [P, TT, D])
    res = [sb(f"res{i}", [P, TT, D]) for i in two]
    xT = sb("b_xT", [P, TT * P])
    qkv = [sb(f"qkv{i}", [P, TT, 3 * D]) for i in two]
    ms, lnv, r0, va, ra, rb, rc, rr = (sb(n, [P, TT, H2]) for n in ("ms", "lnv", "r0", "va", "ra", "rb", "rc", "rr"))
    zT = sb("zT", [P, TT * P])
    lg = sb("lg", [P, TT, E])
    top = sb("top", [P, TT])
    sh = sb("sh", [P, TT, E])
    ge = sb("ge", [P, TT, E])
    gs = sb("gs", [P, TT])
    gr = sb("gr", [P, TT])
    pick = sb("pick", [P, TT, E])
    best = sb("best", [P, TT])
    oh = sb("oh", [P, TT, E])
    ohb = sb("ohb", [P, TT, E], BF16)
    loc = sb("loc", [P, TT, E])
    keep = sb("keep", [P, TT, E])
    w = [sb(f"w{i}", [P, TT, E]) for i in two]
    wT = sb("wT", [TT * E, P])
    stats2, mv2, rstd2 = sb("stats2", [P, TT, 6]), sb("mv2", [P, TT, 2]), sb("rstd2", [P, TT])

    S_BANKS, G_BANKS, ST_A, ST_B, B_Z = bank[0:2], bank[2:5], bank[5], bank[6], bank[7]

    x_loaded = [sem(f"b_x_loaded{i}") for i in two]
    y_loaded = [sem(f"b_y_loaded{i}") for i in two]
    stored = [Signal(sem(f"b_stored{i}"), 0) for i in two]
    passed = sem("passed")
    zeroed = Signal(sem("b_zeroed"), 1)
    scores_zero = sem("scores_zero")
    alone = sem("b_alone")
    s = {n: Signal(sem("b_" + n), per) for n, per in dict(
        stats=TT, mv=TT, veps=1, rstd=1, xn=TT, xxn=1, res=1, xT=1, qkv=TT, vm=2 * TT, vrev=64, sq=1, ms=1, lnv=1, r0=1,
        va=1, ra=1, rb=1, rc=1, rr=1, qn=1, t1=TT, t2=2, qr=1, qd=2, qT=1, qm=GA, kg=GA,
        fk=TT - 1, fq=TT - 1, fqT=2 * (TT - 1), st_full=TT - 1, state=2 * (TT - 1),
        s_full=HA, pat=HA, masked=HA, z_full=TT, z=TT, y1T=1, lg=1, top=1, sh=1, ge=1, gs=1, gr=1,
        pick=1, best=1, oh=1, ohb=1, loc=1, keep=1, w=1, carry=1, wT=1, acc=TT * E, ym=1,
        stats2=TT, mv2=TT, veps2=1, rstd2=1, z2=TT, zg=1, zo=1, outs=1).items()}

    TURNS = ["fq1a", "fq1b", "xT'", "wT", "y0a", "qkv'0", "qkv'1", "y0b", "fq2a", "fq2b", "qkv'2", "y1a", "qkv'3", "y1T'",
             "fq3a", "fq3b", "lg'", "y1b", "y2a", "y2b", "rank'", "q'", "y3a", "k'", "y3b", "bias", "out"]
    AHEAD = ["xT'", "qkv'0", "qkv'1", "qkv'2", "qkv'3", "q'", "k'", "y1T'", "lg'", "rank'"]
    assert sorted(AHEAD) == sorted(n for n in TURNS if "'" in n)
    LAST = [n for n in TURNS if "'" not in n]

    MOVED = {"xT'": ("xT", 1, 1), "q'": ("qT", 1, 1), "k'": ("kg", GA, 1), "y1T'": ("y1T", 1, 1), "lg'": ("lg", 1, 1),
             "rank'": ("carry", 1, 1), "wT": ("wT", 1, 0), "bias": ("ym", 1, 0), "out": ("zo", 1, 0)}
    MOVED.update({f"qkv'{c}": ("qkv", c + 1, 1) for c in range(TT)})
    MOVED.update({f"fq{c}{h}": ("fqT", 2 * c - 1 + (h == "b"), 0) for c in range(1, TT) for h in "ab"})
    MOVED.update({f"y{c}{h}": ("acc", E * c + E // 2 * (1 + (h == "b")), 0) for c in range(TT) for h in "ab"})
    assert len(TURNS) % len(G_BANKS) == 0

    class Turn:

        def __init__(self, b, names, name):
            k = names.index(name)
            self.to = G_BANKS[k % len(G_BANKS)]
            if names is AHEAD:
                self.full = k + 1
            else:
                self.full = b.i * (2 * len(TURNS)) + b.off * len(TURNS) + len(AHEAD) + k + 1
            k -= len(G_BANKS)
            if k < 0 and names is not AHEAD and isinstance(b.i, int) and b.number == 0:
                k = max(j for j in range(len(AHEAD)) if j % len(G_BANKS) == k % len(G_BANKS))
                before, of = AHEAD[k], b.prev()
            elif names is AHEAD:
                before, of = (names[k], b.prev()) if k >= 0 else (TURNS[k], b.prev().prev())
            else:
                before, of = (names[k], b) if k >= 0 else (TURNS[k], b.prev())
            signal, n, ahead = MOVED[before]
            self.prior = s[signal]
            self.moved = self.prior.by(of.next() if ahead else of, n)

    xv = x.rearrange("b (c p) d -> b p c d", p=P)
    yv = y1_dram.rearrange("b (c p) d -> b p c d", p=P)
    ov = out.rearrange("b (c p) d -> b p c d", p=P)
    LASTB = NB // 2 - 1

    def turn_strips(b):
        sp.wait_ge(s["qkv"].sem, s["qkv"].by(b))
        for r in range(P // ST):
            a, z = ST * r, P - ST * (r + 1)
            sp.dma_start(vrev[z:z + ST, :, :], qkv[b.parity][a:a + ST, :, 2 * D + D // 2:3 * D]).then_inc(s["vrev"].sem, 16)

    def load_x(b):
        if not (isinstance(b.i, int) and b.number < 2):
            sp.wait_ge(s["res"].sem, s["res"].by(b.prev().prev()))
        sp.dma_start(xs[b.parity][:], xv[b.number]).then_inc(x_loaded[b.parity], 16)

    def load_y1(b):
        if not (isinstance(b.i, int) and b.number < 2):
            sp.wait_ge(s["acc"].sem, s["acc"].by(b.prev().prev(), TT * E - E + 1))
        sp.dma_start(y1[b.parity][:], yv[b.number]).then_inc(y_loaded[b.parity], 16)

    def store(b):
        sp.wait_ge(s["outs"].sem, s["outs"].by(b))
        sp.dma_start(ov[b.number], outs[b.parity][:]).then_inc(stored[b.parity].sem, 16)

    def all_stored():
        for o in two:
            sp.wait_ge(stored[o].sem, 16 * (NB // 2) + 1)

    def pe_xT(b, turn):
        pe.wait_ge(s["xn"].sem, s["xn"].by(b))
        pe.wait_ge(turn.prior.sem, turn.moved)
        to = turn.to
        for c in range(TT):
            last = nc.tensor.transpose(to[:, c * P:(c + 1) * P], xn[:, c, :], ident[:])
        last.then_inc(passed, 1)

    def pe_qkv(b, c, turn):
        pe.wait_ge(s["xT"].sem, s["xT"].by(b))
        pe.wait_ge(turn.prior.sem, turn.moved)
        to = turn.to
        nc.tensor.matmul(to[:, 0:3 * D], xT[:, c * P:(c + 1) * P], wqkvT[:], start=True, stop=True).then_inc(passed, 1)

    def pe_turn_qk(b, which, turn):
        pe.wait_ge(s["qr"].sem, s["qr"].by(b))
        pe.wait_ge(turn.prior.sem, turn.moved)
        to = turn.to
        for c in range(TT):
            last = nc.tensor.transpose(to[:, c * P:(c + 1) * P], qr[:, c, which * D:(which + 1) * D], ident[:])
        last.then_inc(passed, 1)

    def pe_scores(b, c, half):
        pe.wait_ge(s["qm"].sem, s["qm"].by(b))
        pe.wait_ge(s["kg"].sem, s["kg"].by(b))
        for rev in two:
            g = half + 2 * rev
            n = c * GA + 2 * half + rev
            if n >= 2:
                pe.wait_ge(s["pat"].sem, s["pat"].by(b, n - 1))
            else:
                pe.wait_ge(s["pat"].sem, s["pat"].by(b.prev()))
            to = S_BANKS[rev][:].rearrange("p (j q) -> p j q", j=GA)
            for r in range(P // ST):
                a = P - ST * (r + 1) if rev else ST * r
                last = nc.tensor.matmul(to[a:a + ST, :, ST * r:P], kg[b.parity][:, g, c * P + ST * r:c * P + ST * (r + 1)],
                                        qm[b.parity][:, :, c * P + ST * r:(c + 1) * P], start=True, stop=True, skip_group_check=True)
            last.then_inc(s["s_full"].sem, 1)

    def pe_fq(b, c, turns):
        pe.wait_ge(s["fq"].sem, s["fq"].by(b, c))
        for k in range(FB):
            turn = turns[k // 4]
            if k % 4 == 0:
                pe.wait_ge(turn.prior.sem, turn.moved)
                to = turn.to
            last = nc.tensor.transpose(to[:, k % 4 * P:(k % 4 + 1) * P], fq[(c + 1) % 2][:].rearrange("p h o i -> p (h o i)")[:, k * P:(k + 1) * P], ident[:])
            if k in (3, FB - 1):
                last.then_inc(passed, 1)

    def pe_state(b, c):
        pe.wait_ge(s["fk"].sem, s["fk"].by(b, c + 1))
        if c == 0:
            pe.wait_ge(s["state"].sem, s["state"].by(b.prev()))
        else:
            pe.wait_ge(s["state"].sem, s["state"].by(b, 2 * c))
        for k in range(FB):
            to = ST_A[:, k * P:(k + 1) * P] if k < 4 else ST_B[:, 0:P]
            last = nc.tensor.matmul(to, fk[c % 2][:].rearrange("p h o i -> p (h o i)")[:, k * P:(k + 1) * P],
                                    qkv[b.parity][:, c, 2 * D:3 * D], start=(c == 0 and k in (0, 4)), stop=(c == TT - 2),
                                    skip_group_check=True)
        last.then_inc(s["st_full"].sem, 1)

    def pe_values(b, c):
        if c == 0:
            pe.wait_ge(s["z"].sem, s["z"].by(b.prev()))
        else:
            pe.wait_ge(s["z"].sem, s["z"].by(b, c))
            pe.wait_ge(s["fqT"].sem, s["fqT"].by(b, 2 * c))
            pe.wait_ge(s["state"].sem, s["state"].by(b, 2 * c))
            for k in range(FB):
                nc.tensor.matmul(B_Z[:, 0:P], state[(c - 1) % 2][:, k, :], fqT[(c + 1) % 2][:, k, :], start=(k == 0), stop=False,
                                 skip_group_check=True)
        pe.wait_ge(s["vm"].sem, s["vm"].by(b))
        pe.wait_ge(s["masked"].sem, s["masked"].by(b, GA * (c + 1)))
        for j in range(GA):
            for g in range(GA):
                last = nc.tensor.matmul(B_Z[32 * g:32 * g + 32, 0:P], vm[b.parity][:, c, g * GA + j, :],
                                        pat[c % 2][:, g * GA + j, :], start=(c == 0 and j == 0), stop=(j == GA - 1),
                                        skip_group_check=True)
        last.then_inc(s["z_full"].sem, 1)

    def pe_out(b, turn):
        pe.wait_ge(s["z"].sem, s["z"].by(b))
        pe.wait_ge(turn.prior.sem, turn.moved)
        to = turn.to
        for c in range(TT):
            last = nc.tensor.matmul(to[:, c * D:(c + 1) * D], zT[:, c * P:(c + 1) * P], woT[:], start=True, stop=True)
        last.then_inc(passed, 1)

    def pe_y1T(b, turn):
        pe.wait_ge(y_loaded[b.parity], b.i * 16 + 16 * (b.off // 2 + 1))
        pe.wait_ge(turn.prior.sem, turn.moved)
        to = turn.to
        for c in range(TT):
            last = nc.tensor.transpose(to[:, c * P:(c + 1) * P], y1[b.parity][:, c, :], ident[:])
        last.then_inc(passed, 1)

    def pe_logits(b, turn):
        pe.wait_ge(s["y1T"].sem, s["y1T"].by(b))
        pe.wait_ge(turn.prior.sem, turn.moved)
        to = turn.to
        for c in range(TT):
            last = nc.tensor.matmul(to[:, c * E:(c + 1) * E], y1T[b.parity][:, c * P:(c + 1) * P], wg[:], start=True, stop=True)
        last.then_inc(passed, 1)

    def pe_rank(b, turn):
        pe.wait_ge(s["ohb"].sem, s["ohb"].by(b))
        pe.wait_ge(turn.prior.sem, turn.moved)
        to = turn.to
        o2 = ohb[:].rearrange("p c e -> p (c e)")
        nc.tensor.matmul(to[:, 0:TT * E], upper[:], o2, start=True, stop=False, skip_group_check=True)
        for d in range(1, TT):
            nc.tensor.matmul(to[:, d * E:TT * E], ones[:], o2[:, 0:(TT - d) * E], start=False, stop=False, skip_group_check=True)
        for c in range(TT):
            last = nc.tensor.matmul(to[:, TT * E:(TT + 1) * E], ones[:], o2[:, c * E:(c + 1) * E], start=False, stop=(c == TT - 1),
                                    skip_group_check=True)
        last.then_inc(passed, 1)

    def pe_wT(b, turn):
        pe.wait_ge(s["w"].sem, s["w"].by(b))
        pe.wait_ge(turn.prior.sem, turn.moved)
        to = turn.to
        nc.tensor.transpose(to[0:TT * E, 0:P], w[b.parity][:].rearrange("p c e -> p (c e)"), ident[:]).then_inc(passed, 1)

    def pe_expert(b, c, half, turn):
        pe.wait_ge(turn.prior.sem, turn.moved)
        to = turn.to
        nc.tensor.matmul(to[:], y1T[b.parity][:, c * P:(c + 1) * P], mexp[:, half * 512:(half + 1) * 512], start=True, stop=True)\
            .then_inc(passed, 1)

    def pe_bias(b, turn):
        pe.wait_ge(s["wT"].sem, s["wT"].by(b))
        pe.wait_ge(turn.prior.sem, turn.moved)
        to = turn.to
        for c in range(TT):
            last = nc.tensor.matmul(to[:, c * D:(c + 1) * D], wT[:], cpad[:, c, :], start=True, stop=True)
        last.then_inc(passed, 1)

    def pe_body(b, names, begun=False):
        def T(name):
            return Turn(b, names, name)

        n, more = b.next(), names is TURNS
        if not begun:
            pe_scores(b, 0, 0)
            pe_scores(b, 0, 1)
        pe_fq(b, 1, (T("fq1a"), T("fq1b")))
        if not begun:
            pe_state(b, 0)
        if more:
            pe_xT(n, T("xT'"))
        pe_wT(b, T("wT"))
        if not begun:
            pe_scores(b, 1, 0)
        pe_expert(b, 0, 0, T("y0a"))
        pe_values(b, 0)
        if more:
            pe_qkv(n, 0, T("qkv'0"))
            pe_qkv(n, 1, T("qkv'1"))
        pe_scores(b, 1, 1)
        pe_expert(b, 0, 1, T("y0b"))
        pe_fq(b, 2, (T("fq2a"), T("fq2b")))
        pe_state(b, 1)
        pe_scores(b, 2, 0)
        if more:
            pe_qkv(n, 2, T("qkv'2"))
        pe_expert(b, 1, 0, T("y1a"))
        pe_values(b, 1)
        if more:
            pe_qkv(n, 3, T("qkv'3"))
            pe_y1T(n, T("y1T'"))
        pe_fq(b, 3, (T("fq3a"), T("fq3b")))
        if more:
            pe_logits(n, T("lg'"))
        pe_scores(b, 2, 1)
        pe_expert(b, 1, 1, T("y1b"))
        pe_state(b, 2)
        pe_scores(b, 3, 0)
        pe_expert(b, 2, 0, T("y2a"))
        pe_values(b, 2)
        pe_expert(b, 2, 1, T("y2b"))
        pe_scores(b, 3, 1)
        if more:
            pe_rank(n, T("rank'"))
            pe_turn_qk(n, 0, T("q'"))
        pe_expert(b, 3, 0, T("y3a"))
        if more:
            pe_turn_qk(n, 1, T("k'"))
        pe_expert(b, 3, 1, T("y3b"))
        pe_values(b, 3)
        pe_bias(b, T("bias"))
        pe_out(b, T("out"))

    def act_xT(b, turn):
        act.wait_ge(passed, turn.full)
        src = turn.to
        act.wait_ge(s["qkv"].sem, s["qkv"].by(b.prev()))
        nc.scalar.activation(xT[:], src[:], ACT.Copy).then_inc(s["xT"].sem, 1)

    def act_vm(b, c):
        act.wait_ge(s["qkv"].sem, s["qkv"].by(b))
        act.wait_ge(s["vrev"].sem, s["vrev"].by(b))
        for c in (c, c + 1):
            for rev in two:
                to = bass.AP(vm[b.parity], (c * HA + rev * HA // 2) * 32, [[TT * HA * 32, P], [GA * 32, GA // 2], [32 + DA, GA], [1, DA]])
                src = vrev[:, c, :] if rev else qkv[b.parity][:, c, 2 * D:2 * D + D // 2]
                nc.scalar.activation(to, src.rearrange("p (g j d) -> p g j d", g=GA // 2, j=GA), ACT.Copy).then_inc(s["vm"].sem, 1)

    def act_square_qk(b):
        act.wait_ge(s["qkv"].sem, s["qkv"].by(b))
        act.wait_ge(s["ms"].sem, s["ms"].by(b.prev()))
        nc.scalar.activation(sq[:].rearrange("p c h d -> p c (h d)"), qkv[b.parity][:, :, 0:2 * D], ACT.Square).then_inc(s["sq"].sem, 1)

    def act_rsqrt(b):
        act.wait_ge(s["ms"].sem, s["ms"].by(b))
        act.wait_ge(s["rr"].sem, s["rr"].by(b.prev()))
        nc.scalar.activation(lnv[:], ms[:], ACT.Ln, bias=eps[:], scale=1.0 / DA).then_inc(s["lnv"].sem, 1)
        act.wait_ge(s["lnv"].sem, s["lnv"].by(b))
        nc.scalar.activation(r0[:], lnv[:], ACT.Exp, scale=-0.5).then_inc(s["r0"].sem, 1)

    def act_double(b):
        act.wait_ge(s["qr"].sem, s["qr"].by(b))
        src = qr[:].rearrange("p c (h d) -> p (c h) d", d=DA)
        to = qd[b.parity][:].rearrange("p c h d -> p (c h) d")
        nc.scalar.activation(to[:, :, 0:DA], src, ACT.Copy).then_inc(s["qd"].sem, 1)
        nc.scalar.activation(to[:, :, DA:DA + OFF - 1], src[:, :, 0:OFF - 1], ACT.Copy).then_inc(s["qd"].sem, 1)

    def act_qT(b, turn):
        act.wait_ge(passed, turn.full)
        act.wait_ge(s["qm"].sem, s["qm"].by(b.prev()))
        nc.scalar.activation(qT[:], turn.to[:], ACT.Copy).then_inc(s["qT"].sem, 1)

    def act_kg(b, turn):
        act.wait_ge(passed, turn.full)
        src = turn.to
        for g in range(GA):
            r = slice(32 * g, 32 * g + 32)
            nc.scalar.activation(kg[b.parity][r, g, :], src[r, :], ACT.Copy).then_inc(s["kg"].sem, 1)

    def act_square(b, c, half):
        for rev in two:
            g = half + 2 * rev
            n = c * GA + 2 * half + rev
            act.wait_ge(s["s_full"].sem, s["s_full"].by(b, n + 1))
            if n % GA == 0 and c >= 2:
                act.wait_ge(s["z_full"].sem, s["z_full"].by(b, c - 1))
            elif n % GA == 0:
                act.wait_ge(s["z_full"].sem, s["z_full"].by(b.prev(), TT - 1 + c))
            nc.scalar.activation(pat[c % 2][:, g * GA:(g + 1) * GA, :].rearrange("p j q -> p (j q)"), S_BANKS[rev][:],
                                 ACT.Square, scale=1.0 / DA).then_inc(s["pat"].sem, 1)

    def act_fqT(b, c, turns):
        for k, turn in enumerate(turns):
            act.wait_ge(passed, turn.full)
            src = turn.to
            if c == 3:
                act.wait_ge(s["z_full"].sem, s["z_full"].by(b, c - 1))
            else:
                act.wait_ge(s["z_full"].sem, s["z_full"].by(b.prev()))
            wide = 4 if k == 0 else FB - 4
            nc.scalar.activation(fqT[(c + 1) % 2][:, 4 * k:4 * k + wide, :].rearrange("p k q -> p (k q)"), src[:, 0:wide * P],
                                 ACT.Copy).then_inc(s["fqT"].sem, 1)

    def act_zT(b, c):
        act.wait_ge(s["z_full"].sem, s["z_full"].by(b, c + 1))
        act.wait_ge(s["zo"].sem, s["zo"].by(b.prev()))
        nc.scalar.activation(zT[:, c * P:(c + 1) * P], B_Z[:, 0:P], ACT.Copy).then_inc(s["z"].sem, 1)

    def act_y1T(b, turn):
        act.wait_ge(passed, turn.full)
        src = turn.to
        act.wait_ge(s["acc"].sem, s["acc"].by(b.prev().prev()))
        nc.scalar.activation(y1T[b.parity][:], src[:], ACT.Copy).then_inc(s["y1T"].sem, 1)

    def act_gate(b):
        act.wait_ge(s["sh"].sem, s["sh"].by(b))
        act.wait_ge(s["gs"].sem, s["gs"].by(b.prev()))
        nc.scalar.activation(ge[:], sh[:], ACT.Exp).then_inc(s["ge"].sem, 1)

    def act_wT(b, turn):
        act.wait_ge(passed, turn.full)
        src = turn.to
        act.wait_ge(s["ym"].sem, s["ym"].by(b.prev()))
        nc.scalar.activation(wT[:], src[0:TT * E, 0:P], ACT.Copy).then_inc(s["wT"].sem, 1)

    def act_body(b, names, begun=False):
        def T(name):
            return Turn(b, names, name)

        n, more = b.next(), names is TURNS
        if not begun:
            act_square(b, 0, 0)
            act_square(b, 0, 1)
        act_fqT(b, 1, (T("fq1a"), T("fq1b")))
        if more:
            act_xT(n, T("xT'"))
        act_wT(b, T("wT"))
        if not begun:
            act_square(b, 1, 0)
        act_zT(b, 0)
        act_square(b, 1, 1)
        act_fqT(b, 2, (T("fq2a"), T("fq2b")))
        act_square(b, 2, 0)
        act_zT(b, 1)
        if more:
            act_y1T(n, T("y1T'"))
            act_square_qk(n)
        act_fqT(b, 3, (T("fq3a"), T("fq3b")))
        if more:
            act_rsqrt(n)
        act_square(b, 2, 1)
        if more:
            act_gate(n)
        act_square(b, 3, 0)
        if more:
            act_vm(n, 0)
            act_vm(n, 2)
        act_zT(b, 2)
        act_square(b, 3, 1)
        if more:
            act_double(n)
            act_qT(n, T("q'"))
            act_kg(n, T("k'"))
        act_zT(b, 3)

    def pool_mask(b, c, half, zero):
        for n in (2 * half, 2 * half + 1):
            pool.wait_ge(s["pat"].sem, s["pat"].by(b, GA * c + n + 1))
            pool.sem_inc(alone, 1)
            rev = n % 2
            g = half + 2 * rev
            heads = pat[c % 2][:, g * GA:(g + 1) * GA, :]
            if rev:
                last = nc.gpsimd.tensor_tensor(heads, heads, revmask[:].unsqueeze(1).broadcast_to([P, GA, P]), ALU.mult)
            else:
                last = nc.gpsimd.affine_select(out=heads, in_=heads, compare_op=ALU.is_ge, fill=zero, base=0,
                                               pattern=[[0, GA], [1, P]], channel_multiplier=-1)
            last.then_inc(s["masked"].sem, 1)

    def pool_rstd(b):
        pool.wait_ge(s["mv"].sem, s["mv"].by(b))
        pool.wait_ge(s["xn"].sem, s["xn"].by(b.prev()))
        nc.gpsimd.tensor_tensor(rstd[:], mv[:, :, 1], lneps[:], ALU.add).then_inc(s["veps"].sem, 1)
        pool.wait_ge(s["veps"].sem, s["veps"].by(b))
        nc.gpsimd.tensor_tensor(rstd[:], rstd[:], mhalf[:], ALU.pow).then_inc(s["rstd"].sem, 1)

    def pool_newton(b):
        pool.wait_ge(s["ms"].sem, s["ms"].by(b))
        pool.sem_inc(alone, 1)
        nc.gpsimd.tensor_scalar(va[:], ms[:], 1.0 / DA, RMS_EPS, ALU.mult, ALU.add).then_inc(s["va"].sem, 1)
        pool.wait_ge(s["r0"].sem, s["r0"].by(b))
        nc.gpsimd.tensor_tensor(ra[:], r0[:], r0[:], ALU.mult).then_inc(s["ra"].sem, 1)
        pool.wait_ge(s["va"].sem, s["va"].by(b))
        pool.wait_ge(s["ra"].sem, s["ra"].by(b))
        nc.gpsimd.tensor_tensor(rb[:], ra[:], va[:], ALU.mult).then_inc(s["rb"].sem, 1)
        pool.wait_ge(s["rb"].sem, s["rb"].by(b))
        pool.sem_inc(alone, 1)
        nc.gpsimd.tensor_scalar(rc[:], rb[:], -0.5, 1.5, ALU.mult, ALU.add).then_inc(s["rc"].sem, 1)
        pool.wait_ge(s["rc"].sem, s["rc"].by(b))
        pool.wait_ge(s["qn"].sem, s["qn"].by(b.prev()))
        nc.gpsimd.tensor_tensor(rr[:], rc[:], r0[:], ALU.mult).then_inc(s["rr"].sem, 1)

    def pool_cos(b):
        pool.wait_ge(s["qn"].sem, s["qn"].by(b))
        pool.wait_ge(s["qr"].sem, s["qr"].by(b.prev()))
        for c in range(TT):
            nc.gpsimd.tensor_tensor(t1[:, c], qn[:, c], rope[:, 0, c, :].unsqueeze(1).broadcast_to([P, H2, DA]), ALU.mult).then_inc(s["t1"].sem, 1)

    def pool_xxn(b):
        pool.wait_ge(s["xn"].sem, s["xn"].by(b))
        pool.wait_ge(s["zo"].sem, s["zo"].by(b.prev().prev()))
        nc.gpsimd.tensor_tensor(res[b.parity][:], xs[b.parity][:], xn[:], ALU.add).then_inc(s["xxn"].sem, 1)

    def pool_res(b):
        pool.wait_ge(s["xxn"].sem, s["xxn"].by(b))
        nc.gpsimd.tensor_tensor(res[b.parity][:], res[b.parity][:], ln[:, 3, :].unsqueeze(1).broadcast_to([P, TT, D]),
                                ALU.add).then_inc(s["res"].sem, 1)

    def pool_rstd2(b):
        pool.wait_ge(s["mv2"].sem, s["mv2"].by(b))
        pool.wait_ge(s["z2"].sem, s["z2"].by(b.prev()))
        nc.gpsimd.tensor_tensor(rstd2[:], mv2[:, :, 1], lneps[:], ALU.add).then_inc(s["veps2"].sem, 1)
        pool.wait_ge(s["veps2"].sem, s["veps2"].by(b))
        nc.gpsimd.tensor_tensor(rstd2[:], rstd2[:], mhalf[:], ALU.pow).then_inc(s["rstd2"].sem, 1)

    def pool_gain(b):
        pool.wait_ge(s["z2"].sem, s["z2"].by(b))
        pool.wait_ge(s["outs"].sem, s["outs"].by(b.prev()))
        nc.gpsimd.tensor_tensor(zg[:], z[:], ln[:, 2, :].unsqueeze(1).broadcast_to([P, TT, D]), ALU.mult).then_inc(s["zg"].sem, 1)

    def pool_body(b, zero, more=2, before=True, begun=False):
        n, p = b.next(), b.prev()
        if not begun:
            pool_mask(b, 0, 0, zero)
            pool_mask(b, 0, 1, zero)
        if before:
            pool_rstd2(p)
            pool_gain(p)
        pool_mask(b, 1, 0, zero)
        pool_mask(b, 1, 1, zero)
        pool_mask(b, 2, 0, zero)
        if more:
            pool_xxn(n)
            pool_res(n)
            pool_newton(n)
        pool_mask(b, 2, 1, zero)
        if more:
            pool_cos(n)
        pool_mask(b, 3, 0, zero)
        pool_mask(b, 3, 1, zero)
        if more == 2:
            pool_rstd(n.next())

    def pool_zero():
        for i in two:
            nc.gpsimd.memset(vm[i][:], 0.0)
            last = nc.gpsimd.memset(kg[i][:], 0.0)
        last.then_inc(zeroed.sem, 1)

    def zeros_in(eng):
        eng.wait_ge(zeroed.sem, zeroed.by(Batch(0, 0)))

    def dve_zero_scores():
        for i in two:
            nc.vector.memset(S_BANKS[i][:], 0.0).then_inc(scores_zero, 1)

    def scores_zeroed(eng):
        eng.wait_ge(scores_zero, 2)

    def dve_stats(b):
        dve.wait_ge(x_loaded[b.parity], b.i * 16 + 16 * (b.off // 2 + 1))
        dve.wait_ge(s["veps"].sem, s["veps"].by(b.prev()))
        for c in range(TT):
            nc.vector.bn_stats(stats[:, c, :], xs[b.parity][:, c, :]).then_inc(s["stats"].sem, 1)
        dve.wait_ge(s["stats"].sem, s["stats"].by(b))
        dve.sem_inc(alone, 1)
        for c in range(TT):
            nc.vector.bn_aggr(mv[:, c, :], stats[:, c, :]).then_inc(s["mv"].sem, 1)

    def dve_xn(b):
        dve.wait_ge(s["rstd"].sem, s["rstd"].by(b))
        dve.wait_ge(s["xT"].sem, s["xT"].by(b.prev()))
        dve.wait_ge(s["xxn"].sem, s["xxn"].by(b.prev()))
        for c in range(TT):
            nc.vector.tensor_scalar(xn[:, c, :], xs[b.parity][:, c, :], mv[:, c, 0:1], rstd[:, c:c + 1],
                                    ALU.subtract, ALU.mult).then_inc(s["xn"].sem, 1)

    def dve_qkv(b, c, turn):
        dve.wait_ge(passed, turn.full)
        src = turn.to
        if c == 0:
            dve.wait_ge(s["z_full"].sem, s["z_full"].by(b.prev().prev()))
            dve.wait_ge(s["qr"].sem, s["qr"].by(b.prev().prev()))
        nc.vector.tensor_tensor(qkv[b.parity][:, c, :], src[:, 0:3 * D], bqkv[:], ALU.add).then_inc(s["qkv"].sem, 1)

    def dve_ms(b):
        dve.wait_ge(s["sq"].sem, s["sq"].by(b))
        dve.wait_ge(s["rr"].sem, s["rr"].by(b.prev()))
        nc.vector.tensor_reduce(ms[:], sq[:], AX, ALU.add).then_inc(s["ms"].sem, 1)

    def dve_qn(b):
        dve.wait_ge(s["rr"].sem, s["rr"].by(b))
        dve.wait_ge(s["qr"].sem, s["qr"].by(b.prev()))
        nc.vector.tensor_tensor(qn[:], qkv[b.parity][:, :, 0:2 * D].rearrange("p c (h d) -> p c h d", d=DA),
                                rr[:].unsqueeze(3).broadcast_to([P, TT, H2, DA]), ALU.mult).then_inc(s["qn"].sem, 1)

    def dve_swap(b):
        dve.wait_ge(s["qn"].sem, s["qn"].by(b))
        for e in two:
            nc.vector.tensor_tensor(t2[:, :, :, e::2], qn[:, :, :, 1 - e::2],
                                    rope[:, 1, :, e::2].unsqueeze(2).broadcast_to([P, TT, H2, DA // 2]), ALU.mult).then_inc(s["t2"].sem, 1)

    def dve_rope(b):
        dve.wait_ge(s["t2"].sem, s["t2"].by(b))
        dve.wait_ge(s["t1"].sem, s["t1"].by(b))
        dve.wait_ge(s["qd"].sem, s["qd"].by(b.prev()))
        dve.wait_ge(s["kg"].sem, s["kg"].by(b.prev()))
        dve.wait_ge(s["qT"].sem, s["qT"].by(b.prev()))
        nc.vector.tensor_tensor(qr[:].rearrange("p c (h d) -> p c h d", d=DA), t1[:], t2[:], ALU.add).then_inc(s["qr"].sem, 1)

    def dve_qm(b):
        dve.wait_ge(s["qT"].sem, s["qT"].by(b))
        dve.wait_ge(s["pat"].sem, s["pat"].by(b.prev().prev()))
        for j in range(GA):
            nc.vector.tensor_scalar(qm[b.parity][:, j, :], qT[:], jmask[:, j:j + 1], None, ALU.mult).then_inc(s["qm"].sem, 1)

    def features(to, b, c, which):
        wide = H2 * (DA + OFF - 1)
        base = (c * H2 + which * HA) * (DA + OFF - 1)
        dims = [[TT * wide, P], [DA + OFF - 1, HA]]
        a0 = bass.AP(qd[b.parity], base, dims + [[0, OFF], [1, DA]])
        a1 = bass.AP(qd[b.parity], base, dims + [[1, OFF], [1, DA]])
        return nc.vector.tensor_tensor(to[:], a0, a1, ALU.mult)

    def dve_fk(b, c):
        dve.wait_ge(s["qd"].sem, s["qd"].by(b))
        if c == 2:
            dve.wait_ge(s["st_full"].sem, s["st_full"].by(b, 1))
        else:
            dve.wait_ge(s["st_full"].sem, s["st_full"].by(b.prev()))
        features(fk[c % 2], b, c, 1).then_inc(s["fk"].sem, 1)

    def dve_fq(b, c):
        dve.wait_ge(s["qd"].sem, s["qd"].by(b))
        if c == 3:
            dve.wait_ge(s["fqT"].sem, s["fqT"].by(b, 2))
        else:
            dve.wait_ge(s["fqT"].sem, s["fqT"].by(b.prev()))
        features(fq[(c + 1) % 2], b, c, 0).then_inc(s["fq"].sem, 1)

    def dve_state(b, c):
        dve.wait_ge(s["st_full"].sem, s["st_full"].by(b, c + 1))
        if c == 2:
            dve.wait_ge(s["z_full"].sem, s["z_full"].by(b, 2))
        else:
            dve.wait_ge(s["z_full"].sem, s["z_full"].by(b.prev()))
        nc.vector.tensor_tensor(state[c % 2][:, 0:4, :], ST_A[:].rearrange("p (k d) -> p k d", k=4), featw[:, 0:4, :], ALU.mult)\
            .then_inc(s["state"].sem, 1)
        nc.vector.tensor_tensor(state[c % 2][:, 4, :], ST_B[:, 0:P], featw[:, 4, :], ALU.mult).then_inc(s["state"].sem, 1)

    def dve_gate(b, turn):
        dve.wait_ge(passed, turn.full)
        src = turn.to
        dve.wait_ge(s["sh"].sem, s["sh"].by(b.prev()))
        nc.vector.tensor_copy(lg[:].rearrange("p c e -> p (c e)"), src[:, 0:TT * E]).then_inc(s["lg"].sem, 1)
        dve.wait_ge(s["lg"].sem, s["lg"].by(b))
        nc.vector.tensor_reduce(top[:], lg[:], AX, ALU.max).then_inc(s["top"].sem, 1)
        dve.wait_ge(s["top"].sem, s["top"].by(b))
        dve.wait_ge(s["ge"].sem, s["ge"].by(b.prev()))
        nc.vector.tensor_tensor(sh[:], lg[:], top[:].unsqueeze(2).broadcast_to([P, TT, E]), ALU.subtract).then_inc(s["sh"].sem, 1)
        dve.wait_ge(s["sh"].sem, s["sh"].by(b))
        nc.vector.scalar_tensor_tensor(out=pick[:], in0=sh[:], scalar=0.0, in1=first[:].unsqueeze(1).broadcast_to([P, TT, E]),
                                       op0=ALU.is_equal, op1=ALU.mult).then_inc(s["pick"].sem, 1)
        dve.wait_ge(s["pick"].sem, s["pick"].by(b))
        nc.vector.tensor_reduce(best[:], pick[:], AX, ALU.max).then_inc(s["best"].sem, 1)
        dve.wait_ge(s["best"].sem, s["best"].by(b))
        nc.vector.tensor_tensor(oh[:], pick[:], best[:].unsqueeze(2).broadcast_to([P, TT, E]), ALU.is_equal).then_inc(s["oh"].sem, 1)
        dve.wait_ge(s["oh"].sem, s["oh"].by(b))
        nc.vector.tensor_copy(ohb[:], oh[:]).then_inc(s["ohb"].sem, 1)

    def dve_gate_sum(b):
        dve.wait_ge(s["ge"].sem, s["ge"].by(b))
        nc.vector.tensor_reduce(gs[:], ge[:], AX, ALU.add).then_inc(s["gs"].sem, 1)
        dve.wait_ge(s["gs"].sem, s["gs"].by(b))
        nc.vector.reciprocal(gr[:], gs[:]).then_inc(s["gr"].sem, 1)

    def dve_rank(b, turn):
        dve.wait_ge(passed, turn.full)
        src = turn.to
        nc.vector.tensor_tensor(loc[:], src[:, 0:TT * E].rearrange("p (c e) -> p c e", c=TT),
                                carry[:].unsqueeze(1).broadcast_to([P, TT, E]), ALU.add).then_inc(s["loc"].sem, 1)
        dve.wait_ge(s["loc"].sem, s["loc"].by(b))
        nc.vector.tensor_tensor(carry[:], src[:, TT * E:(TT + 1) * E], carry[:], ALU.add).then_inc(s["carry"].sem, 1)
        nc.vector.scalar_tensor_tensor(out=keep[:], in0=loc[:], scalar=float(CAP), in1=oh[:], op0=ALU.is_lt, op1=ALU.mult).then_inc(s["keep"].sem, 1)
        dve.wait_ge(s["keep"].sem, s["keep"].by(b))
        dve.wait_ge(s["gr"].sem, s["gr"].by(b))
        dve.wait_ge(s["acc"].sem, s["acc"].by(b.prev().prev()))
        nc.vector.tensor_tensor(w[b.parity][:], keep[:], gr[:].unsqueeze(2).broadcast_to([P, TT, E]), ALU.mult).then_inc(s["w"].sem, 1)

    def dve_expert(b, c, half, turn):
        dve.wait_ge(passed, turn.full)
        src = turn.to
        dve.wait_ge(s["w"].sem, s["w"].by(b))
        for k in range(E // 2):
            e = half * (E // 2) + k
            if e:
                dve.wait_ge(s["acc"].sem, s["acc"].by(b, c * E + e))
            else:
                dve.wait_ge(s["z2"].sem, s["z2"].by(b.prev()))
            prior = y1[b.parity][:, c, :] if e == 0 else acc[(e + 1) % 2][:, c, :]
            nc.vector.scalar_tensor_tensor(out=acc[e % 2][:, c, :], in0=src[:, k * D:(k + 1) * D], scalar=w[b.parity][:, c, e:e + 1], in1=prior,
                                           op0=ALU.mult, op1=ALU.add).then_inc(s["acc"].sem, 1)

    def dve_ym(b, turn):
        dve.wait_ge(passed, turn.full)
        src = turn.to
        dve.wait_ge(s["acc"].sem, s["acc"].by(b))
        nc.vector.tensor_tensor(acc[0][:], acc[1][:], src[:].rearrange("p (c d) -> p c d", c=TT), ALU.add).then_inc(s["ym"].sem, 1)

    def dve_stats2(b):
        dve.wait_ge(s["ym"].sem, s["ym"].by(b))
        for c in range(TT):
            nc.vector.bn_stats(stats2[:, c, :], acc[0][:, c, :]).then_inc(s["stats2"].sem, 1)
        dve.wait_ge(s["stats2"].sem, s["stats2"].by(b))
        dve.sem_inc(alone, 1)
        for c in range(TT):
            nc.vector.bn_aggr(mv2[:, c, :], stats2[:, c, :]).then_inc(s["mv2"].sem, 1)

    def dve_norm2(b):
        dve.wait_ge(s["rstd2"].sem, s["rstd2"].by(b))
        dve.wait_ge(s["zg"].sem, s["zg"].by(b.prev()))
        for c in range(TT):
            nc.vector.tensor_scalar(z[:, c, :], acc[0][:, c, :], mv2[:, c, 0:1], rstd2[:, c:c + 1], ALU.subtract, ALU.mult).then_inc(s["z2"].sem, 1)

    def dve_residual(b, turn):
        dve.wait_ge(passed, turn.full)
        dve.wait_ge(s["outs"].sem, s["outs"].by(b.prev()))
        nc.vector.tensor_tensor(zo[:], turn.to[:].rearrange("p (c d) -> p c d", c=TT), res[b.parity][:], ALU.add).then_inc(s["zo"].sem, 1)

    def dve_out(b):
        dve.wait_ge(s["zg"].sem, s["zg"].by(b))
        dve.wait_ge(s["zo"].sem, s["zo"].by(b))
        done = b.i * 16 + 16 * (b.off // 2)
        if not isinstance(b.i, int) or done > 0:
            dve.wait_ge(stored[b.parity].sem, done + 1)
        nc.vector.tensor_tensor(outs[b.parity][:], zg[:], zo[:], ALU.add).then_inc(s["outs"].sem, 1)

    def dve_body(b, names, before=True, more=2, begun=False):
        def T(name):
            return Turn(b, names, name)

        n, p = b.next(), b.prev()
        if before:
            dve_ym(p, Turn(p, TURNS, "bias"))
            dve_residual(p, Turn(p, TURNS, "out"))
        if not begun:
            dve_fq(b, 1)
            dve_fk(b, 0)
        if more and not begun:
            dve_xn(n)
        if before:
            dve_stats2(p)
        if not begun:
            dve_fk(b, 1)
        dve_fq(b, 2)
        dve_state(b, 0)
        if before:
            dve_norm2(p)
        dve_expert(b, 0, 0, T("y0a"))
        if before:
            dve_out(p)
        if more:
            dve_qkv(n, 0, T("qkv'0"))
            dve_qkv(n, 1, T("qkv'1"))
        dve_expert(b, 0, 1, T("y0b"))
        dve_state(b, 1)
        dve_fk(b, 2)
        if more:
            dve_qkv(n, 2, T("qkv'2"))
        dve_fq(b, 3)
        if more == 2:
            dve_stats(n.next())
        dve_expert(b, 1, 0, T("y1a"))
        if more:
            dve_qkv(n, 3, T("qkv'3"))
            dve_ms(n)
            dve_gate(n, T("lg'"))
        dve_expert(b, 1, 1, T("y1b"))
        if more:
            dve_qn(n)
            dve_swap(n)
        dve_expert(b, 2, 0, T("y2a"))
        if more:
            dve_gate_sum(n)
            dve_rope(n)
        dve_expert(b, 2, 1, T("y2b"))
        dve_state(b, 2)
        if more:
            dve_rank(n, T("rank'"))
        dve_expert(b, 3, 0, T("y3a"))
        if more:
            dve_qm(n)
        dve_expert(b, 3, 1, T("y3b"))

    phase = Phase()
    phase.signals = [*s.values(), zeroed, *stored]
    phase.load_x = load_x
    phase.turn_strips = turn_strips
    phase.dve_zero_scores = dve_zero_scores
    phase.scores_zeroed = scores_zeroed
    phase.load_y1 = load_y1
    phase.store = store
    phase.all_stored = all_stored
    phase.pe_xT = pe_xT
    phase.pe_qkv = pe_qkv
    phase.pe_turn_qk = pe_turn_qk
    phase.pe_y1T = pe_y1T
    phase.pe_logits = pe_logits
    phase.pe_rank = pe_rank
    phase.pe_body = pe_body
    phase.act_xT = act_xT
    phase.act_vm = act_vm
    phase.act_square_qk = act_square_qk
    phase.act_rsqrt = act_rsqrt
    phase.act_double = act_double
    phase.act_qT = act_qT
    phase.act_kg = act_kg
    phase.act_y1T = act_y1T
    phase.act_gate = act_gate
    phase.act_body = act_body
    phase.pool_rstd = pool_rstd
    phase.pool_newton = pool_newton
    phase.pool_cos = pool_cos
    phase.pool_rstd2 = pool_rstd2
    phase.pool_gain = pool_gain
    phase.pool_body = pool_body
    phase.pool_zero = pool_zero
    phase.zeros_in = zeros_in
    phase.dve_stats = dve_stats
    phase.dve_xn = dve_xn
    phase.pool_xxn = pool_xxn
    phase.pool_res = pool_res
    phase.dve_qkv = dve_qkv
    phase.dve_ms = dve_ms
    phase.dve_qn = dve_qn
    phase.dve_swap = dve_swap
    phase.dve_rope = dve_rope
    phase.dve_qm = dve_qm
    phase.dve_gate = dve_gate
    phase.dve_gate_sum = dve_gate_sum
    phase.dve_rank = dve_rank
    phase.dve_ym = dve_ym
    phase.dve_stats2 = dve_stats2
    phase.dve_residual = dve_residual
    phase.dve_norm2 = dve_norm2
    phase.dve_out = dve_out
    phase.dve_body = dve_body
    phase.pe_scores = pe_scores
    phase.act_square = act_square
    phase.pool_mask = pool_mask
    phase.dve_fq = dve_fq
    phase.dve_fk = dve_fk
    phase.pe_state = pe_state
    phase.Turn = Turn
    phase.TURNS = TURNS
    phase.AHEAD = AHEAD
    phase.LAST = LAST
    return phase


def constants():
    pos = np.arange(NS, dtype=np.float32)
    inv = np.float32(1.0) / np.float32(10000.0) ** (np.arange(0, DA, 2, dtype=np.float32) / np.float32(DA))
    ang = np.outer(pos, inv.astype(np.float32)).astype(np.float32)
    ang = np.concatenate([ang, ang], -1)
    cos, sin = np.cos(ang), np.sin(ang)
    sin[:, 0::2] *= -1
    trig = np.stack([cos, sin]).reshape(2, TT, P, DA).transpose(2, 0, 1, 3)
    row, col = np.arange(P)[:, None], np.arange(P)[None, :]
    f = np.arange(FB * P)
    weight = np.array([1, 2, 2, 2, 1], np.float32)[(f // DA) % OFF] / DA ** 2
    featw = (f[:, None] // (OFF * DA) == col // DA) * weight[:, None]
    return {
        "ident": np.eye(P, dtype=np.float32),
        "trig": np.ascontiguousarray(trig, dtype=np.float32),
        "featw": np.ascontiguousarray(featw.reshape(FB, P, P).transpose(1, 0, 2), dtype=np.float32),
        "jmask": (row // DA % GA == np.arange(GA)[None, :]).astype(np.float32),
        "revmask": (P - ST - row // ST * ST + row % ST <= col).astype(np.float32),
        "blockmask": np.where(row // LB % 2 == np.arange(32)[None, :] // LB, 0.0, NEG).astype(np.float32),
        "upper": (row < col).astype(mybir.dt.np(BF16)),
        "first": np.broadcast_to(E - np.arange(E), (P, E)).astype(np.float32).copy(),
    }


_INS = ["attn_x", "attn_Wq", "attn_bq", "attn_Wk", "attn_bk", "attn_Wv", "attn_bv", "attn_Wo", "attn_norm_w",
        "ffn_in_proj_w", "ffn_in_proj_b", "ffn_out_proj_w", "ffn_out_proj_b", "ffn_ln1_g", "ffn_ln1_b",
        "ffn_ln2_g", "ffn_ln2_b", "ffn_wg", "ffn_w1", "ffn_b1", "ffn_w2", "ffn_b2"]


def laid_out(inputs):
    g = {n.split("_", 1)[1]: np.asarray(inputs["L0_" + n]) for n in _INS}
    fc = FF // P
    arrays = {
        "x": g["x"], "b2m": np.concatenate([np.tile(g["b2"], (TT, 1)), np.arange(TT * E)[:, None] // E == np.arange(TT)[None, :]], 1),
        "w1T": g["w1"].reshape(E, D, fc, P).transpose(3, 0, 2, 1), "w2": g["w2"].reshape(E, fc, P, D).transpose(2, 0, 1, 3),
    }
    parts = {
        "wqkvT": np.concatenate([g["Wq"].T, g["Wk"].T, g["Wv"].T], 1), "woT": g["Wo"].T,
        "ipT": g["in_proj_w"].T, "opT": g["out_proj_w"].T, "bcol": np.concatenate([g["in_proj_b"], g["out_proj_b"]]).reshape(4, P).T,
        "wg": g["wg"], "b1T": g["b1"].reshape(E, fc, P).transpose(2, 0, 1),
        "ln": np.concatenate([g["ln1_g"], g["ln1_b"], g["ln2_g"], g["ln2_b"]]), "bqkv": np.concatenate([g["bq"], g["bk"], g["bv"]]),
        "norm_w": g["norm_w"],
    }
    fixed = constants()
    arrays["c_upper"] = fixed.pop("upper")
    parts.update(fixed)
    for pack, rows in PACKS.items():
        if pack == "wide":
            arrays["pack_" + pack] = np.concatenate([parts[n] for n, _ in rows])
        else:
            arrays["pack_" + pack] = np.concatenate([parts[n].reshape(P, -1) for n, _ in rows], 1)
    return {n: np.ascontiguousarray(a) for n, a in arrays.items()}


SCRATCH = (("y1", (LB, NS, D)),)


def kernel(**inputs):
    import concourse.bacc as _bacc
    from concourse.bass_utils import run_bass_kernel_spmd as _run

    nc = _bacc.Bacc("TRN2", target_bir_lowering=False, num_devices=1)
    arrays = {n + "_dram": a for n, a in laid_out(inputs).items()}
    t = {n.removesuffix("_dram"): nc.dram_tensor(n, a.shape, mybir.dt.from_np(a.dtype), kind="ExternalInput").ap() for n, a in arrays.items()}
    t["out"] = nc.dram_tensor("out_dram", (LB, NS, D), F32, kind="ExternalOutput").ap()
    for n, shape in SCRATCH:
        t[n] = nc.dram_tensor(n + "_scratch", shape, F32, kind="Internal").ap()
    build(nc, t)
    r = _run(nc, [arrays], core_ids=[0])
    return r.results[0]["out_dram"]
```
